# Optimizing a Trainium2 kernel written in Bass

```python
import numpy as np
import jax
import jax.numpy as jnp

def _softmax(x, axis=-1):
    return jax.nn.softmax(x, axis=axis)
def _gelu(x):
    return jax.nn.gelu(x, approximate=True)
def _silu(x):
    return jax.nn.silu(x)
def _sigmoid(x):
    return jax.nn.sigmoid(x)
def _layernorm(x, axis=-1, eps=1e-5):
    m = jnp.mean(x, axis=axis, keepdims=True)
    v = jnp.var(x, axis=axis, keepdims=True)
    return (x - m) / jnp.sqrt(v + eps)
def _scatter_add(tgt, idx, src, axis=0):
    return tgt.at[idx].add(src)
def _segment_sum(src, seg, n):
    return jax.ops.segment_sum(src, seg, n)

kernel_name = 'mk_conv_preact_d2_conv_nchw64_c0c82d'

def setup_inputs(seed: int = 0):
    np.random.seed(seed)
    _w = jnp.asarray
    def _rec_inputs():
        import jax
        import jax.numpy as jnp
        _gk = jax.random.key(seed)
        x = -7.109e-05 + 0.9999 * jax.random.normal(jax.random.fold_in(_gk, 1), (4, 64, 512, 512), jnp.float32)
        return x
    x = _rec_inputs()
    def _L0_conv_setup():
        import jax, jax.numpy as jnp
        import numpy as np
        B, C, H, W = (4, 64, 512, 512)
        K = 3

        def inv_mag(x):
            f = jnp.fft.fft2(x)
            a = jnp.arctan2(f.imag, f.real)
            ph = jax.lax.complex(jnp.cos(a), jnp.sin(a))
            return jnp.fft.ifft2(ph).real
        key = jax.random.key(seed)
        k1, k2 = jax.random.split(key)
        x = jax.random.normal(k1, (B, C, H, W), dtype=jnp.float32)
        w = jax.random.normal(k2, (1, 1, K), dtype=jnp.float32) * 0.3
        return {'x': x, 'w': w}
    _L0_conv_all = _L0_conv_setup()
    _L0_conv_in = {k: v for k, v in _L0_conv_all.items() if k in ('w', )}
    del _L0_conv_all

    def _L1_conv_setup():
        import jax, jax.numpy as jnp
        import numpy as np
        PS = 8
        LOCAL = 16

        def conv1x1(x, w, b):
            return jnp.einsum('oi,bihw->bohw', w, x) + b[None, :, None, None]

        def dynamic_local(x, w1, b1, w2, b2, k):
            B, C, H, W = x.shape
            pooled = x.mean((2, 3))
            h = jax.nn.relu(pooled @ w1.T + b1)
            kern = (h @ w2.T + b2).reshape(B, C, k, k)

            def per_batch(xb, kb):
                return jax.lax.conv_general_dilated(xb[None], kb[:, None], (1, 1), 'SAME', feature_group_count=C, dimension_numbers=('NCHW', 'OIHW', 'NCHW'))[0]
            return jax.vmap(per_batch)(x, kern)

        def channel_layernorm(x, w, b, eps=1e-06):
            u = x.mean(1, keepdims=True)
            s = ((x - u) ** 2).mean(1, keepdims=True)
            xn = (x - u) / jnp.sqrt(s + eps)
            return w[None, :, None, None] * xn + b[None, :, None, None]

        def fsas(x, hid_w, hid_b, dw_w, dw_b, ln_w, ln_b, out_w, out_b):
            hidden = conv1x1(x, hid_w, hid_b)
            mid = hidden.shape[1]
            dw = jax.lax.conv_general_dilated(hidden, dw_w[:, None], (1, 1), 'SAME', feature_group_count=mid, dimension_numbers=('NCHW', 'OIHW', 'NCHW')) + dw_b[None, :, None, None]
            q, k, v = jnp.split(dw, 3, axis=1)
            B, C, H, W = q.shape

            def patch(t):
                return t.reshape(B, C, H // PS, PS, W // PS, PS).transpose(0, 1, 2, 4, 3, 5)
            qf = jnp.fft.rfft2(patch(q))
            kf = jnp.fft.rfft2(patch(k))
            out = jnp.fft.irfft2(qf * kf, s=(PS, PS))
            out = out.transpose(0, 1, 2, 4, 3, 5).reshape(B, C, H, W)
            out = channel_layernorm(out, ln_w, ln_b)
            return conv1x1(v * out, out_w, out_b)
        key = jax.random.key(seed)
        ks = jax.random.split(key, 12)
        s = 0.02
        return {'x': jax.random.normal(ks[0], (4, 64, 256, 256), jnp.float32), 'dl1_w1': jax.random.normal(ks[1], (16, 16), jnp.float32) * s, 'dl1_b1': jnp.zeros((16,), jnp.float32), 'dl1_w2': jax.random.normal(ks[2], (144, 16), jnp.float32) * s, 'dl1_b2': jnp.zeros((144,), jnp.float32), 'dl2_w1': jax.random.normal(ks[3], (16, 16), jnp.float32) * s, 'dl2_b1': jnp.zeros((16,), jnp.float32), 'dl2_w2': jax.random.normal(ks[4], (400, 16), jnp.float32) * s, 'dl2_b2': jnp.zeros((400,), jnp.float32), 'fs_hid_w': jax.random.normal(ks[5], (144, 48), jnp.float32) * s, 'fs_hid_b': jnp.zeros((144,), jnp.float32), 'fs_dw_w': jax.random.normal(ks[6], (144, 3, 3), jnp.float32) * s, 'fs_dw_b': jnp.zeros((144,), jnp.float32), 'fs_ln_w': jnp.ones((48,), jnp.float32), 'fs_ln_b': jnp.zeros((48,), jnp.float32), 'fs_out_w': jax.random.normal(ks[7], (48, 48), jnp.float32) * s, 'fs_out_b': jnp.zeros((48,), jnp.float32), 'last_w': jax.random.normal(ks[8], (64, 64), jnp.float32) * s, 'last_b': jnp.zeros((64,), jnp.float32)}
    _L1_conv_all = _L1_conv_setup()
    _L1_conv_in = {k: v for k, v in _L1_conv_all.items() if k in ('dl1_w1', 'dl1_b1', 'dl1_w2', 'dl1_b2', 'dl2_w1', 'dl2_b1', 'dl2_w2', 'dl2_b2', 'fs_hid_w', 'fs_hid_b', 'fs_dw_w', 'fs_dw_b', 'fs_ln_w', 'fs_ln_b', 'fs_out_w', 'fs_out_b', 'last_w', 'last_b', )}
    del _L1_conv_all

    return {
        "x": x,
        "L0_conv_w": _L0_conv_in["w"],
        "L1_conv_dl1_w1": _L1_conv_in["dl1_w1"],
        "L1_conv_dl1_b1": _L1_conv_in["dl1_b1"],
        "L1_conv_dl1_w2": _L1_conv_in["dl1_w2"],
        "L1_conv_dl1_b2": _L1_conv_in["dl1_b2"],
        "L1_conv_dl2_w1": _L1_conv_in["dl2_w1"],
        "L1_conv_dl2_b1": _L1_conv_in["dl2_b1"],
        "L1_conv_dl2_w2": _L1_conv_in["dl2_w2"],
        "L1_conv_dl2_b2": _L1_conv_in["dl2_b2"],
        "L1_conv_fs_hid_w": _L1_conv_in["fs_hid_w"],
        "L1_conv_fs_hid_b": _L1_conv_in["fs_hid_b"],
        "L1_conv_fs_dw_w": _L1_conv_in["fs_dw_w"],
        "L1_conv_fs_dw_b": _L1_conv_in["fs_dw_b"],
        "L1_conv_fs_ln_w": _L1_conv_in["fs_ln_w"],
        "L1_conv_fs_ln_b": _L1_conv_in["fs_ln_b"],
        "L1_conv_fs_out_w": _L1_conv_in["fs_out_w"],
        "L1_conv_fs_out_b": _L1_conv_in["fs_out_b"],
        "L1_conv_last_w": _L1_conv_in["last_w"],
        "L1_conv_last_b": _L1_conv_in["last_b"],
    }

def reference(x, L0_conv_w, L1_conv_dl1_w1, L1_conv_dl1_b1, L1_conv_dl1_w2, L1_conv_dl1_b2, L1_conv_dl2_w1, L1_conv_dl2_b1, L1_conv_dl2_w2, L1_conv_dl2_b2, L1_conv_fs_hid_w, L1_conv_fs_hid_b, L1_conv_fs_dw_w, L1_conv_fs_dw_b, L1_conv_fs_ln_w, L1_conv_fs_ln_b, L1_conv_fs_out_w, L1_conv_fs_out_b, L1_conv_last_w, L1_conv_last_b):
    import jax
    import jax.numpy as jnp
    def _L0_conv_ref(x, w):
        import jax, jax.numpy as jnp
        import numpy as np
        B, C, H, W = (4, 64, 512, 512)
        K = 3

        def inv_mag(x):
            f = jnp.fft.fft2(x)
            a = jnp.arctan2(f.imag, f.real)
            ph = jax.lax.complex(jnp.cos(a), jnp.sin(a))
            return jnp.fft.ifft2(ph).real
        x1 = inv_mag(x)
        y = jnp.mean(x1, axis=(2, 3))
        y = y[:, None, :]
        y = jax.lax.conv_general_dilated(y, w, window_strides=(1,), padding=[((K - 1) // 2, (K - 1) // 2)], dimension_numbers=('NCH', 'OIH', 'NCH'))
        g = jax.nn.sigmoid(y)[:, 0, :]
        return x * g[:, :, None, None]

    def _L1_conv_ref(x, dl1_w1, dl1_b1, dl1_w2, dl1_b2, dl2_w1, dl2_b1, dl2_w2, dl2_b2, fs_hid_w, fs_hid_b, fs_dw_w, fs_dw_b, fs_ln_w, fs_ln_b, fs_out_w, fs_out_b, last_w, last_b):
        import jax, jax.numpy as jnp
        import numpy as np
        PS = 8
        LOCAL = 16

        def conv1x1(x, w, b):
            return jnp.einsum('oi,bihw->bohw', w, x) + b[None, :, None, None]

        def dynamic_local(x, w1, b1, w2, b2, k):
            B, C, H, W = x.shape
            pooled = x.mean((2, 3))
            h = jax.nn.relu(pooled @ w1.T + b1)
            kern = (h @ w2.T + b2).reshape(B, C, k, k)

            def per_batch(xb, kb):
                return jax.lax.conv_general_dilated(xb[None], kb[:, None], (1, 1), 'SAME', feature_group_count=C, dimension_numbers=('NCHW', 'OIHW', 'NCHW'))[0]
            return jax.vmap(per_batch)(x, kern)

        def channel_layernorm(x, w, b, eps=1e-06):
            u = x.mean(1, keepdims=True)
            s = ((x - u) ** 2).mean(1, keepdims=True)
            xn = (x - u) / jnp.sqrt(s + eps)
            return w[None, :, None, None] * xn + b[None, :, None, None]

        def fsas(x, hid_w, hid_b, dw_w, dw_b, ln_w, ln_b, out_w, out_b):
            hidden = conv1x1(x, hid_w, hid_b)
            mid = hidden.shape[1]
            dw = jax.lax.conv_general_dilated(hidden, dw_w[:, None], (1, 1), 'SAME', feature_group_count=mid, dimension_numbers=('NCHW', 'OIHW', 'NCHW')) + dw_b[None, :, None, None]
            q, k, v = jnp.split(dw, 3, axis=1)
            B, C, H, W = q.shape

            def patch(t):
                return t.reshape(B, C, H // PS, PS, W // PS, PS).transpose(0, 1, 2, 4, 3, 5)
            qf = jnp.fft.rfft2(patch(q))
            kf = jnp.fft.rfft2(patch(k))
            out = jnp.fft.irfft2(qf * kf, s=(PS, PS))
            out = out.transpose(0, 1, 2, 4, 3, 5).reshape(B, C, H, W)
            out = channel_layernorm(out, ln_w, ln_b)
            return conv1x1(v * out, out_w, out_b)
        x1, x2 = (x[:, :LOCAL], x[:, LOCAL:])
        x1 = dynamic_local(x1, dl1_w1, dl1_b1, dl1_w2, dl1_b2, 3)
        x1 = dynamic_local(x1, dl2_w1, dl2_b1, dl2_w2, dl2_b2, 5)
        x2 = fsas(x2, fs_hid_w, fs_hid_b, fs_dw_w, fs_dw_b, fs_ln_w, fs_ln_b, fs_out_w, fs_out_b)
        return conv1x1(jnp.concatenate([x1, x2], axis=1), last_w, last_b)

    def _gn(v, G=32, eps=1e-5):
        B_, C_, H_, W_ = v.shape
        g = v.reshape(B_, G, C_ // G, H_, W_)
        m = jnp.mean(g, axis=(2, 3, 4), keepdims=True)
        s = jnp.var(g, axis=(2, 3, 4), keepdims=True)
        return ((g - m) / jnp.sqrt(s + eps)).reshape(v.shape)

    def _ln_c(v, eps=1e-6):
        m = jnp.mean(v, axis=1, keepdims=True)
        s = jnp.var(v, axis=1, keepdims=True)
        return (v - m) / jnp.sqrt(s + eps)

    def _ln_t(v, eps=1e-5):
        m = jnp.mean(v, axis=-1, keepdims=True)
        s = jnp.var(v, axis=-1, keepdims=True)
        return (v - m) / jnp.sqrt(s + eps)

    def _to_tokens(v):
        B_, C_, H_, W_ = v.shape
        return v.reshape(B_, C_, H_ * W_).transpose(0, 2, 1)
    def _from_tokens(t, like):
        B_, C_, H_, W_ = like.shape
        return t.transpose(0, 2, 1).reshape(B_, C_, H_, W_)

    x = x + _L0_conv_ref(_gn(x), L0_conv_w)
    x = x + _L1_conv_ref(_gn(x), L1_conv_dl1_w1, L1_conv_dl1_b1, L1_conv_dl1_w2, L1_conv_dl1_b2, L1_conv_dl2_w1, L1_conv_dl2_b1, L1_conv_dl2_w2, L1_conv_dl2_b2, L1_conv_fs_hid_w, L1_conv_fs_hid_b, L1_conv_fs_dw_w, L1_conv_fs_dw_b, L1_conv_fs_ln_w, L1_conv_fs_ln_b, L1_conv_fs_out_w, L1_conv_fs_out_b, L1_conv_last_w, L1_conv_last_b)
    return x


_drawn_inputs = setup_inputs


def setup_inputs(seed=0):
    import zlib

    import numpy as np

    out = dict(_drawn_inputs(seed))
    spreads = {'L1_conv_dl1_b1': (0.0, 0.8),
     'L1_conv_dl1_b2': (0.0, 0.8),
     'L1_conv_dl2_b1': (0.0, 0.8),
     'L1_conv_dl2_b2': (0.0, 0.8),
     'L1_conv_fs_hid_b': (0.0, 0.8),
     'L1_conv_fs_dw_b': (0.0, 0.8),
     'L1_conv_fs_ln_w': (1.0, 0.6),
     'L1_conv_fs_ln_b': (0.0, 0.8),
     'L1_conv_fs_out_b': (0.0, 0.8),
     'L1_conv_last_b': (0.0, 0.411)}
    factors = {'L0_conv_w': 200.0,
     'L1_conv_dl1_w1': 200.0,
     'L1_conv_dl1_w2': 8.0,
     'L1_conv_dl2_w1': 200.0,
     'L1_conv_dl2_w2': 8.0,
     'L1_conv_fs_hid_w': 8.0,
     'L1_conv_fs_dw_w': 8.0,
     'L1_conv_fs_out_w': 8.0,
     'L1_conv_last_w': 4.879}
    for name, (base, spread) in spreads.items():
        noise = np.random.default_rng([zlib.crc32(name.encode()), seed]).standard_normal(out[name].shape)
        drawn = base * np.exp(spread * noise) if base else spread * noise
        out[name] = jnp.asarray(drawn.astype(out[name].dtype))
    for name, factor in factors.items():
        out[name] = (out[name] * factor).astype(out[name].dtype)
    return out
```

```python
from contextlib import ExitStack

import numpy as np

import concourse.bass as bass
from concourse import mybir

F32 = mybir.dt.float32
ALU = mybir.AluOpType
ACT = mybir.ActivationFunctionType
AX = mybir.AxisListType.X

C = 64
NL = 16
NF = C - NL
PS = 8
WIN = PS + 2
NWIN = WIN * WIN
PX = PS * PS
NSPEC = 128
NG = 2 * NSPEC + PX
SETK = 9 + 25 + 2
LB_ROWS = 122
EPS_GN = 1e-5
EPS_LN = 1e-6
QKB = 8
VB = 16


def spectral_rows():
    rows = []
    seen = set()
    for u in range(PS):
        for v in range(PS):
            other = ((-u) % PS, (-v) % PS)
            if other in seen:
                continue
            seen.add((u, v))
            own = other == (u, v)
            rows.append((u, v, 1.0 if own else 2.0, "re", "re"))
            if not own:
                rows += [(u, v, 2.0, "im", "im"), (u, v, 2.0, "re", "im"), (u, v, 2.0, "im", "re")]
    return rows


def dft_tables():
    rows = spectral_rows()
    y, x = np.meshgrid(np.arange(PS), np.arange(PS), indexing="ij")
    E = np.zeros((10, NG, NWIN + 1))
    inverse = np.zeros((NSPEC, PX))
    for n, (u, v, weight, pq, pk) in enumerate(rows):
        angle = 2 * np.pi * ((u * y + v * x) % PS) / PS
        part = {"re": np.cos(angle), "im": -np.sin(angle)}
        for base, p in ((0, pq), (NSPEC, pk)):
            for t in range(9):
                window = np.zeros((WIN, WIN))
                window[t // 3:t // 3 + PS, t % 3:t % 3 + PS] = part[p]
                E[t, base + n, :NWIN] = window.T.ravel()
            E[9, base + n, NWIN] = part[p].sum()
        if pq == pk:
            inverse[n] = (weight * (1 if pq == "re" else -1) * np.cos(angle) / PX).ravel()
        else:
            inverse[n] = (-weight * np.sin(angle) / PX).ravel()
    for p in range(PX):
        for t in range(9):
            E[t, 2 * NSPEC + p, (p % PS + t % 3) * WIN + p // PS + t // 3] = 1.0
        E[9, 2 * NSPEC + p, NWIN] = 1.0
    chunks = E.reshape(10, NG // 32, 32, NWIN + 1).transpose(1, 0, 2, 3)
    return np.ascontiguousarray(chunks, np.float32), inverse.astype(np.float32)


def shape_constants():
    p = np.arange(128)
    k = {}
    k["pair_avg"] = (p[:, None] // 2 == p // 2) / 2
    k["quad_avg"] = (p[:, None] // 4 == p // 4) / 4
    k["from_prev"] = (p[:, None] == p - 2)
    k["from_next"] = (p[:, None] == p + 2)
    for h in range(2):
        k[f"pick_half{h}"] = (p[:, None] == 2 * np.arange(NL) + h)
    k["pick_freq"] = (p[:, None] == 2 * (NL + np.arange(NF + 1))) & (np.arange(NF + 1) < NF)
    k["pick_out"] = (p[:, None] == 2 * (p % C))
    m = np.arange(2 * NF)
    same = (m[:, None] // NF == m // NF) / NF
    k["center"] = np.eye(2 * NF) - same
    k["chan_avg"] = same
    k["side0"] = (m < NF)[:, None]
    k["side1"] = (m >= NF)[:, None]
    k["identity"] = np.eye(PX)
    k["ones_row"] = (np.arange(NF + 1) == NF)[:, None]
    k["diagonals"] = (np.arange(138) == p[:, None] + 3)
    k["spread"] = np.repeat(np.eye(NL), 128, axis=1)
    return {n: np.ascontiguousarray(v, np.float32) for n, v in k.items()}


def bands(H):
    out = []
    n = -(-H // LB_ROWS)
    for i in range(n):
        r0, r1 = i * H // n, (i + 1) * H // n
        y0, y1 = max(0, r0 - 2), min(H, r1 + 2)
        z0, z1 = max(0, y0 - 1), min(H, y1 + 1)
        out.append(((r0, r1), (y0, y1), (z0, z1)))
    return out


def program(nc, t):
    x, out, scratch = t["x"], t["out"], t["local_scratch"]
    B, _, H, W = x.shape
    HW = H * W
    HH = H // 2
    NPR = H // PS
    PW = W // PS
    NPAIR = PW // 2
    SR = 8
    NST = HH // SR
    NCH = NPAIR // 8
    NS1 = PW // 4
    NQK, NV = NF // QKB, NF // VB
    HWID = W // 2
    NRG = PS * HWID // 512
    RPG = PS // NRG
    BANDS = bands(H)
    NB = len(BANDS)
    assert W == 512 and NPAIR % 8 == 0 and NST % 2 == 0 and NS1 == 16 and NRG == 4

    ctx = ExitStack()
    with ctx:
        def sb(name, shape):
            return ctx.enter_context(nc.sbuf_tensor(name, shape, F32))

        def sem(name):
            return ctx.enter_context(nc.semaphore(name))

        banks = ctx.enter_context(nc.psum_tensor("banks", [128, 8, 512], F32))

        K = {n: sb(n, list(t[n].shape)) for n in ("center", "chan_avg", "identity", "inverse")}
        gate_w = sb("gate_w", [128, 3])
        w1T = [sb(f"mlp{n}_w1T", [NL, NL]) for n in (1, 2)]
        b1 = [sb(f"mlp{n}_b1", [NL, 1]) for n in (1, 2)]
        w2T = [sb("mlp1_w2T", [NL, 9, NL]), sb("mlp2_w2T", [NL, 25, NL])]
        b2 = [sb("mlp1_b2", [NL, 9]), sb("mlp2_b2", [NL, 25])]
        hid_wb = sb("hid_wb", [NF + 1, 3 * NF])
        dw_wb = sb("dw_wb", [10, 3 * NF])
        ln_w = sb("ln_w", [2 * NF, 1])
        ln_b = sb("ln_b", [2 * NF, 1])
        out_w2 = sb("out_w2", [NF, 2, NF])
        last_wT = sb("last_wT", [NF, 2, C])
        out_b = sb("out_b", [NF, 1])
        last_b = sb("last_b", [128, 1])
        final_w = sb("final_w", [128, 2, C])
        G = sb("G", [NWIN + 1, NF, NG])
        hid_ab = sb("hid_ab", [NF + 1, B, 3 * NF])
        res_a = sb("res_a", [128, B])
        res_c = sb("res_c", [128, B])
        eps_gn = sb("eps_gn", [128, 1])
        eps_ln = sb("eps_ln", [128, 1])

        s_const = sem("constants_loaded")
        s_set = sem("constants_set")
        sp_passed = sem("sync_passed_its_waits")

        early = ctx.enter_context(ExitStack())
        K["diagonals"] = early.enter_context(nc.sbuf_tensor("diagonals", [128, 138], F32))
        local_k = early.enter_context(nc.sbuf_tensor("local_k", [128, B * NL + 1, SETK], F32))

        with ExitStack() as st:
            for n in ("pair_avg", "quad_avg", "from_prev", "from_next", "pick_half0", "pick_half1",
                      "pick_freq", "pick_out", "side0", "side1", "ones_row", "spread"):
                K[n] = st.enter_context(nc.sbuf_tensor(n, list(t[n].shape), F32))

            def sb1(name, shape):
                return st.enter_context(nc.sbuf_tensor(name, shape, F32))

            def sem1(name):
                return st.enter_context(nc.semaphore(name))

            xs = sb1("xs", [128, 2, SR * W])
            stats = sb1("stats", [128, B, NST * SR, 6])
            cols = sb1("cols", [128, B, NST, 2])
            edge = sb1("edge", [128, B, W])
            ebuf = sb1("ebuf", [10, 32 * (NWIN + 1)])
            mv = sb1("mv", [128, B, 2])
            V = {n: sb1(f"c_{n}", [128, B]) for n in (
                "mean", "var", "mc", "d", "e", "vc", "M", "d1", "e1", "v1", "i1", "r", "s", "t1", "t2",
                "g", "rg", "a", "m2", "a2", "v2", "bb", "d2", "e2", "v3", "i2", "r2", "A", "B", "bm", "Am")}
            BS = sb1("BS", [128, 10, B])
            H0 = sb1("H0", [NL, 8, B])
            H1 = sb1("H1", [NL, 8, B])
            CS = sb1("CS", [NL, 2, B])
            TOT = sb1("TOT", [NL, B])
            hid = [sb1(f"hid{n}", [NL, B]) for n in (1, 2)]
            ST = sb1("ST", [NL, B, 9])
            PR = sb1("PR", [NL, B, 9])
            KB = sb1("KB", [NL, B, SETK])
            pooled2 = sb1("pooled2", [NL, B])
            pooled2s = sb1("pooled2s", [NL, B])
            AB = sb1("AB", [NF + 1, 2, B])
            B49 = sb1("B49", [NF + 1, B])
            Bb = sb1("Bb", [NF + 1, B, NF + 1])
            ones49 = sb1("ones49", [NF + 1, NF + 1])
            bias_row = sb1("bias_row", [NF + 1, B, 3 * NF])
            bias_tot = sb1("bias_tot", [128, 1])

            x_in = [sem1("x_tile_even_in"), sem1("x_tile_odd_in")]
            edge_in = sem1("edge_rows_in")
            stat_done = sem1("stat_tiles_done")
            prep_dve = sem1("prep_dve")
            prep_pe = sem1("prep_pe")
            prep_chain = sem1("prep_chain")
            prep_act = sem1("prep_act")
            table_in = sem1("table_in")
            table_mm = sem1("table_products")
            table_out = sem1("table_copied")

            NCONST = [0]
            x_halves = x.rearrange("b c (h r) w -> b (c h) (r w)", h=2)
            with nc.Block() as block:
                @block.sync
                def _(sp):
                    def load(dst, src):
                        sp.dma_start(dst, src).then_inc(s_const, 16)
                        NCONST[0] += 16

                    for n in K:
                        load(K[n][:, :], t[n][:, :])
                    load(gate_w[:, :], t["gate_w"][:, :])
                    for n in (0, 1):
                        load(w1T[n][:, :], t[f"mlp{n + 1}_w1T"][:, :])
                        load(b1[n][:, :], t[f"mlp{n + 1}_b1"][:, :])
                        load(w2T[n][:, :, :], t[f"mlp{n + 1}_w2T"][:, :, :])
                        load(b2[n][:, :], t[f"mlp{n + 1}_b2"][:, :])
                    load(hid_wb[:, :], t["hid_wb"][:, :])
                    load(dw_wb[:, :], t["dw_wb"][:, :])
                    load(ln_w[:, :], t["ln_w"][:, :])
                    load(ln_b[:, :], t["ln_b"][:, :])
                    for s in range(2):
                        load(out_w2[:, s, :], t["out_w"][:, :])
                        load(last_wT[:, s, :], t["last_wT"][NL:C, :])
                    load(out_b[:, :], t["out_b"][:, :])
                    load(last_b[:, :], t["last_b"][:, :])
                    sp.wait_ge(s_set, 1)
                    for s in range(2):
                        load(final_w[2 * NF + NL * s:2 * NF + NL * (s + 1), s, :], t["last_wT"][0:NL, :])
                    for b in range(B):
                        for h in range(2):
                            sp.dma_start(edge[h:128:2, b, :], x[b, :, h * (H - 1), :]).then_inc(edge_in, 16)
                    for n in range(NG // 32):
                        if n:
                            sp.wait_ge(table_mm, n)
                        sp.dma_start(ebuf[:, :], t["dft"][n]).then_inc(table_in, 16)
                    with sp.Fori(0, B) as b:
                        with sp.Fori(0, NST // 2) as n2:
                            for par in range(2):
                                sp.wait_ge(stat_done, b * NST + n2 * 2 + par + 1)
                                sp.sem_inc(sp_passed, 1)
                                sp.dma_start(xs[:, par, :], x_halves[b, :, bass.ds((n2 * 2 + par) * SR * W, SR * W)]
                                             ).then_inc(x_in[par], 16)

                @block.gpsimd
                def _(pool):
                    nc.gpsimd.memset(final_w[:, :, :], 0.0).then_inc(s_set, 1)
                    nc.gpsimd.memset(eps_gn[:, :], EPS_GN).then_inc(s_set, 1)
                    nc.gpsimd.memset(eps_ln[:, :], EPS_LN).then_inc(s_set, 1)
                    nc.gpsimd.memset(ones49[:, :], 1.0).then_inc(s_set, 1)
                    nc.gpsimd.memset(local_k[:, B * NL, :], 0.0).then_inc(s_set, 1)

                @block.tensor
                def _(pe):
                    pe.wait_ge(s_const, NCONST[0])

                    for n in range(NG // 32):
                        pe.wait_ge(table_in, 16 * (n + 1))
                        if n:
                            pe.wait_ge(table_out, 4 * n)
                        kind = min(n * 32 // NSPEC, 2)
                        for j in range(32):
                            last = nc.tensor.matmul(banks[0:NWIN + 1, j // 8, (j % 8) * NF:(j % 8 + 1) * NF],
                                                    ebuf[:, j * (NWIN + 1):(j + 1) * (NWIN + 1)],
                                                    dw_wb[:, kind * NF:(kind + 1) * NF], start=True, stop=True)
                        last.then_inc(table_mm, 1)

                    last = nc.tensor.matmul(banks[0:2 * NF, 6, 0:C], out_w2[:, :, :].rearrange("m s c -> m (s c)"),
                                            last_wT[:, 0, :], start=True, stop=True)
                    last = nc.tensor.matmul(banks[:, 6, 100:101], last_wT[:, :, :].rearrange("m s c -> m (s c)"),
                                            out_b[:, :], start=True, stop=True)
                    last.then_inc(prep_pe, 1)

                    pe.wait_ge(prep_dve, 2)
                    nc.tensor.matmul(banks[:, 4, 0:B], K["pair_avg"][:, :], V["mean"][:, :],
                                     start=True, stop=True).then_inc(prep_pe, 1)
                    pe.wait_ge(prep_dve, 3)
                    nc.tensor.matmul(banks[:, 4, 8:8 + B], K["pair_avg"][:, :], V["e"][:, :], start=True, stop=True)
                    nc.tensor.matmul(banks[:, 4, 16:16 + B], K["quad_avg"][:, :], V["mc"][:, :],
                                     start=True, stop=True).then_inc(prep_pe, 1)
                    pe.wait_ge(prep_dve, 4)
                    nc.tensor.matmul(banks[:, 4, 24:24 + B], K["quad_avg"][:, :], V["e1"][:, :],
                                     start=True, stop=True)
                    nc.tensor.matmul(banks[:, 4, 32:32 + B], K["from_prev"][:, :], V["s"][:, :], start=True, stop=True)
                    nc.tensor.matmul(banks[:, 4, 40:40 + B], K["from_next"][:, :], V["s"][:, :],
                                     start=True, stop=True).then_inc(prep_pe, 1)
                    pe.wait_ge(prep_dve, 6)
                    nc.tensor.matmul(banks[:, 4, 48:48 + B], K["quad_avg"][:, :], V["m2"][:, :],
                                     start=True, stop=True).then_inc(prep_pe, 1)
                    pe.wait_ge(prep_dve, 7)
                    nc.tensor.matmul(banks[:, 4, 56:56 + B], K["quad_avg"][:, :], V["e2"][:, :],
                                     start=True, stop=True).then_inc(prep_pe, 1)
                    pe.wait_ge(prep_dve, 9)
                    bs = BS[:, :, :].rearrange("p q b -> p (q b)")
                    nc.tensor.matmul(banks[0:NL, 5, 0:8 * B], K["pick_half0"][:, :], bs[:, 0:8 * B], start=True, stop=True)
                    nc.tensor.matmul(banks[0:NL, 5, 64:64 + 8 * B], K["pick_half1"][:, :], bs[:, 0:8 * B],
                                     start=True, stop=True)
                    nc.tensor.matmul(banks[0:NF + 1, 5, 128:128 + 2 * B], K["pick_freq"][:, :], bs[:, 6 * B:8 * B],
                                     start=True, stop=True)
                    nc.tensor.matmul(banks[:, 5, 192:192 + 2 * B], K["pick_out"][:, :], bs[:, 8 * B:10 * B],
                                     start=True, stop=True).then_inc(prep_pe, 1)
                    pe.wait_ge(prep_dve, 10)
                    for b in range(B):
                        nc.tensor.matmul(banks[0:NF + 1, b % 4, 0:3 * NF], Bb[:, b, :], hid_wb[:, :], start=True, stop=True)
                    nc.tensor.matmul(banks[0:NL, 6, 0:B], w1T[0][:, :], H0[:, 5, :],
                                     start=True, stop=True).then_inc(prep_pe, 1)
                    pe.wait_ge(prep_act, 4)
                    for q in range(9):
                        last = nc.tensor.matmul(banks[0:NL, 6, 16 + q * B:16 + (q + 1) * B], w2T[0][:, q, :],
                                                hid[0][:, :], start=True, stop=True)
                    last.then_inc(prep_pe, 1)
                    pe.wait_ge(prep_dve, 11)
                    nc.tensor.matmul(banks[0:NL, 7, 0:B], w1T[1][:, :], pooled2s[:, :],
                                     start=True, stop=True).then_inc(prep_pe, 1)
                    pe.wait_ge(prep_act, 5)
                    for q in range(25):
                        last = nc.tensor.matmul(banks[0:NL, 7, 16 + q * B:16 + (q + 1) * B], w2T[1][:, q, :],
                                                hid[1][:, :], start=True, stop=True)
                    last.then_inc(prep_pe, 1)
                    pe.wait_ge(prep_dve, 12)
                    for c in range(NL):
                        last = nc.tensor.matmul(banks[:, c // 3 % 6, c % 3 * B * SETK:(c % 3 + 1) * B * SETK],
                                                K["spread"][:, c * 128:(c + 1) * 128],
                                                KB[:, :, :].rearrange("p b q -> p (b q)"), start=True, stop=True)
                    last.then_inc(prep_pe, 1)

                @block.scalar
                def _(act):
                    act.wait_ge(s_const, NCONST[0])
                    for n in range(NG // 32):
                        act.wait_ge(table_mm, n + 1)
                        for j in (0, 1):
                            nc.scalar.copy(G[:, :, 32 * n + 8 * j:32 * n + 8 * (j + 1)].rearrange("p c f -> p f c"),
                                           banks[0:NWIN + 1, j, 0:8 * NF].rearrange("p (f c) -> p f c", c=NF)
                                           ).then_inc(table_out, 1)
                    act.wait_ge(s_set, 4)
                    act.wait_ge(prep_dve, 5)
                    nc.scalar.activation(V["r"][:, :], V["i1"][:, :], ACT.Sqrt).then_inc(prep_act, 1)
                    nc.scalar.activation(V["g"][:, :], V["t2"][:, :], ACT.Sigmoid).then_inc(prep_act, 1)
                    act.wait_ge(prep_dve, 8)
                    nc.scalar.activation(V["r2"][:, :], V["i2"][:, :], ACT.Sqrt).then_inc(prep_act, 1)
                    act.wait_ge(prep_pe, 8)
                    nc.scalar.activation(hid[0][:, :], banks[0:NL, 6, 0:B], ACT.Relu, bias=b1[0][:, :]
                                         ).then_inc(prep_act, 1)
                    act.wait_ge(prep_pe, 10)
                    nc.scalar.activation(hid[1][:, :], banks[0:NL, 7, 0:B], ACT.Relu, bias=b1[1][:, :]
                                         ).then_inc(prep_act, 1)

                @block.vector
                def _(dve):
                    v = nc.vector
                    dve.sem_inc(stat_done, 2)
                    steps = [0]

                    def link(ins):
                        steps[0] += 1
                        ins.then_inc(prep_chain, 1)
                        dve.wait_ge(prep_chain, steps[0])

                    def done(ins, n):
                        ins.then_inc(prep_dve, 1)
                        dve.wait_ge(prep_dve, n)

                    dve.wait_ge(s_const, NCONST[0])
                    for n in range(NG // 32):
                        dve.wait_ge(table_mm, n + 1)
                        for j in (2, 3):
                            v.tensor_copy(G[:, :, 32 * n + 8 * j:32 * n + 8 * (j + 1)].rearrange("p c f -> p f c"),
                                          banks[0:NWIN + 1, j, 0:8 * NF].rearrange("p (f c) -> p f c", c=NF)
                                          ).then_inc(table_out, 1)
                    dve.wait_ge(prep_pe, 1)
                    v.tensor_scalar(final_w[0:2 * NF, 0, :], banks[0:2 * NF, 6, 0:C], K["side0"][:, :], None, ALU.mult)
                    v.tensor_scalar(final_w[0:2 * NF, 1, :], banks[0:2 * NF, 6, 0:C], K["side1"][:, :], None, ALU.mult)
                    done(v.tensor_tensor(bias_tot[:, :], banks[:, 6, 100:101], last_b[:, :], ALU.add), 1)

                    with dve.Fori(0, B) as b:
                        with dve.Fori(0, NST // 2) as n2:
                            for par in range(2):
                                n = n2 * 2 + par
                                dve.wait_ge(x_in[par], 16 * (b * (NST // 2) + n2) + 16)
                                for r in range(SR):
                                    v.bn_stats(stats[:, b, n * SR + r, :], xs[:, par, r * W:(r + 1) * W])
                                v.tensor_reduce(cols[:, b, n, :], xs[:, par, :].rearrange("p (r w) -> p w r", w=W)
                                                [:, 0:W:W - 1, :], AX, ALU.add).then_inc(stat_done, 1)
                    dve.wait_ge(stat_done, B * NST + 2)
                    for b in range(B):
                        last = v.bn_aggr(mv[:, b, :], stats[:, b, :, :].rearrange("p n s -> p (n s)"))
                    link(last)
                    v.tensor_copy(V["mean"][:, :], mv[:, :, 0])
                    done(v.tensor_copy(V["var"][:, :], mv[:, :, 1]), 2)

                    def tt(o, a, c, op):
                        return v.tensor_tensor(V[o][:, :], V[a][:, :], V[c][:, :], op)

                    dve.wait_ge(prep_pe, 2)
                    v.tensor_copy(V["mc"][:, :], banks[:, 4, 0:B])
                    link(v.tensor_tensor(V["d"][:, :], V["mean"][:, :], banks[:, 4, 0:B], ALU.subtract))
                    link(tt("d", "d", "d", ALU.mult))
                    done(tt("e", "d", "var", ALU.add), 3)
                    dve.wait_ge(prep_pe, 3)
                    v.tensor_copy(V["M"][:, :], banks[:, 4, 16:16 + B])
                    v.tensor_copy(V["vc"][:, :], banks[:, 4, 8:8 + B])
                    link(v.tensor_tensor(V["d1"][:, :], V["mc"][:, :], banks[:, 4, 16:16 + B], ALU.subtract))
                    link(v.tensor_scalar(V["s"][:, :], V["d1"][:, :], 0.0, None, ALU.is_ge))
                    link(v.tensor_scalar(V["s"][:, :], V["s"][:, :], 2.0, -1.0, ALU.mult, ALU.add))
                    link(tt("e1", "d1", "d1", ALU.mult))
                    done(tt("e1", "e1", "vc", ALU.add), 4)
                    dve.wait_ge(prep_pe, 4)
                    link(v.tensor_scalar(V["v1"][:, :], banks[:, 4, 24:24 + B], EPS_GN, None, ALU.add))
                    link(v.reciprocal(V["i1"][:, :], V["v1"][:, :]))
                    link(v.tensor_scalar(V["t1"][:, :], banks[:, 4, 32:32 + B], gate_w[:, 0:1], None, ALU.mult))
                    link(v.scalar_tensor_tensor(V["t1"][:, :], V["s"][:, :], gate_w[:, 1:2], V["t1"][:, :],
                                                ALU.mult, ALU.add))
                    link(v.scalar_tensor_tensor(V["t1"][:, :], banks[:, 4, 40:40 + B], gate_w[:, 2:3], V["t1"][:, :],
                                                ALU.mult, ALU.add))
                    done(v.tensor_scalar(V["t2"][:, :], V["t1"][:, :], 1.0 / HW, None, ALU.mult), 5)
                    dve.wait_ge(prep_act, 2)
                    link(tt("rg", "r", "g", ALU.mult))
                    link(v.tensor_scalar(V["a"][:, :], V["rg"][:, :], 1.0, None, ALU.add))
                    link(tt("m2", "d1", "rg", ALU.mult))
                    link(tt("m2", "m2", "mc", ALU.add))
                    link(tt("a2", "a", "a", ALU.mult))
                    link(tt("v2", "a2", "vc", ALU.mult))
                    link(tt("bb", "M", "rg", ALU.mult))
                    done(v.tensor_scalar(V["bb"][:, :], V["bb"][:, :], -1.0, None, ALU.mult), 6)
                    dve.wait_ge(prep_pe, 5)
                    link(v.tensor_tensor(V["d2"][:, :], V["m2"][:, :], banks[:, 4, 48:48 + B], ALU.subtract))
                    link(v.tensor_tensor(V["bm"][:, :], V["bb"][:, :], banks[:, 4, 48:48 + B], ALU.subtract))
                    link(tt("e2", "d2", "d2", ALU.mult))
                    done(tt("e2", "e2", "v2", ALU.add), 7)
                    dve.wait_ge(prep_pe, 6)
                    link(v.tensor_scalar(V["v3"][:, :], banks[:, 4, 56:56 + B], EPS_GN, None, ALU.add))
                    done(v.reciprocal(V["i2"][:, :], V["v3"][:, :]), 8)
                    dve.wait_ge(prep_act, 3)
                    link(tt("A", "a", "r2", ALU.mult))
                    link(tt("B", "bm", "r2", ALU.mult))
                    dve.wait_ge(edge_in, 32 * B)
                    v.tensor_reduce(BS[:, 0, :], edge[:, :, :], AX, ALU.add)
                    v.tensor_copy(BS[:, 1, :], edge[:, :, 0])
                    v.tensor_copy(BS[:, 2, :], edge[:, :, W - 1])
                    v.tensor_reduce(BS[:, 3, :], cols[:, :, :, 0], AX, ALU.add)
                    v.tensor_reduce(BS[:, 4, :], cols[:, :, :, 1], AX, ALU.add)
                    link(v.tensor_copy(BS[:, 5, :], V["mc"][:, :]))
                    for q, count in enumerate((W, 1, 1, HH, HH, 1)):
                        link(v.tensor_tensor(BS[:, q, :], BS[:, q, :], V["A"][:, :], ALU.mult))
                        link(v.scalar_tensor_tensor(BS[:, q, :], V["B"][:, :], float(count), BS[:, q, :],
                                                    ALU.mult, ALU.add))
                    v.tensor_copy(BS[:, 6, :], V["A"][:, :])
                    v.tensor_copy(BS[:, 7, :], V["B"][:, :])
                    v.tensor_copy(BS[:, 8, :], V["a"][:, :])
                    done(v.tensor_copy(BS[:, 9, :], V["bb"][:, :]), 9)

                    dve.wait_ge(prep_pe, 7)
                    v.tensor_copy(H0[:, :, :], banks[0:NL, 5, 0:8 * B].rearrange("p (q b) -> p q b", b=B))
                    v.tensor_copy(H1[:, :, :], banks[0:NL, 5, 64:64 + 8 * B].rearrange("p (q b) -> p q b", b=B))
                    v.tensor_copy(AB[:, :, :], banks[0:NF + 1, 5, 128:128 + 2 * B].rearrange("p (q b) -> p q b", b=B))
                    v.tensor_copy(res_a[:, :], banks[:, 5, 192:192 + B])
                    link(v.tensor_scalar(res_c[:, :], banks[:, 5, 192 + B:192 + 2 * B], bias_tot[:, :], None, ALU.add))
                    link(v.tensor_scalar(B49[:, :], AB[:, 1, :], K["ones_row"][:, :], None, ALU.add))
                    for b in range(B):
                        last = v.tensor_scalar(Bb[:, b, :], ones49[:, :], B49[:, b:b + 1], None, ALU.mult)
                    done(last, 10)

                    link(v.tensor_tensor(CS[:, :, :], H0[:, 3:5, :], H1[:, 3:5, :], ALU.add))
                    link(v.tensor_scalar(TOT[:, :], H0[:, 5, :], float(HW), None, ALU.mult))
                    for q in range(9):
                        dy, dx = q // 3 - 1, q % 3 - 1
                        dst = ST[:, :, q]
                        link(v.tensor_copy(dst, TOT[:, :]))
                        side = H0 if dy > 0 else H1
                        if dy:
                            link(v.tensor_tensor(dst, dst, side[:, 0, :], ALU.subtract))
                        if dx:
                            link(v.tensor_tensor(dst, dst, CS[:, 0 if dx > 0 else 1, :], ALU.subtract))
                        if dx and dy:
                            link(v.tensor_tensor(dst, dst, side[:, 1 if dx > 0 else 2, :], ALU.add))
                    dve.wait_ge(prep_pe, 8)
                    for b in range(B):
                        link(v.tensor_scalar(bias_row[:, b, :], banks[0:NF + 1, b % 4, 0:3 * NF],
                                             K["ones_row"][:, :], None, ALU.mult))
                        link(v.scalar_tensor_tensor(hid_ab[:, b, :], hid_wb[:, :], AB[:, 0, b:b + 1],
                                                    bias_row[:, b, :], ALU.mult, ALU.add))
                    dve.wait_ge(prep_pe, 9)
                    for b in range(B):
                        link(v.tensor_tensor(KB[:, b, 0:9], banks[0:NL, 6, 16 + b:16 + 9 * B:B], b2[0][:, :], ALU.add))
                    link(v.tensor_tensor(PR[:, :, :], KB[:, :, 0:9], ST[:, :, :], ALU.mult))
                    link(v.tensor_reduce(pooled2[:, :], PR[:, :, :], AX, ALU.add))
                    done(v.tensor_scalar(pooled2s[:, :], pooled2[:, :], 1.0 / HW, None, ALU.mult), 11)
                    dve.wait_ge(prep_pe, 11)
                    for b in range(B):
                        v.tensor_tensor(KB[:, b, 9:34], banks[0:NL, 7, 16 + b:16 + 25 * B:B], b2[1][:, :], ALU.add)
                        v.tensor_copy(KB[:, b, 34:35], H0[:, 6, b:b + 1])
                        last = v.tensor_copy(KB[:, b, 35:36], H0[:, 7, b:b + 1])
                    done(last, 12)
                    dve.wait_ge(prep_pe, 12)
                    for c in range(NL):
                        v.tensor_copy(local_k[:, c:B * NL:NL, :], banks[:, c // 3 % 6, c % 3 * B * SETK:(c % 3 + 1) * B * SETK]
                                      .rearrange("p (b q) -> p b q", q=SETK))

        with ExitStack() as st:
            def sb3(name, shape):
                return st.enter_context(nc.sbuf_tensor(name, shape, F32))

            def sem3(name):
                return st.enter_context(nc.semaphore(name))

            xl = sb3("xl", [128, 2, W])
            zl = sb3("zl", [128, 2, W + 2])
            y1 = sb3("y1", [128, 2, W + 4])
            y2 = sb3("y2", [128, 2, W])
            taps = sb3("taps", [128, 2, SETK])
            T3 = sb3("T3", [128, 2, 3, 132])
            T5 = sb3("T5", [128, 2, 5, 132])
            l_set = sem3("local_pads_zero")
            l_in = [sem3(f"local_x{n}_in") for n in (0, 1)]
            l_z = sem3("local_z")
            l_p1 = sem3("local_3x3_products")
            l_y1 = sem3("local_y1")
            l_p2 = sem3("local_5x5_products")
            l_y2 = sem3("local_y2")
            l_st = [sem3(f"local_y2_{n}_stored") for n in (0, 1)]
            l_T = sem3("local_matrices")
            l_chain = sem3("local_matrix_steps")
            NSTEP = 2 * NB
            LAG = min(4, NSTEP)

            with nc.Block() as block:
                def cells():
                    return [(n, n // NB, n % NB) for n in range(NSTEP)]

                def store_local(sp, k, n, b, c2):
                    ch, bd = n // NB, n % NB
                    r0, r1 = BANDS[bd][0]
                    sp.wait_ge(l_y2, k * NSTEP + n + 3)
                    sp.sem_inc(sp_passed, 1)
                    sp.dma_start(scratch[b, c2 * 2 + ch, r0:r1, :], y2[0:r1 - r0, n % 2, :]
                                 ).then_inc(l_st[n % 2], 16)

                @block.sync
                def _(sp):
                    sp.sem_inc(l_st[0], 1)
                    sp.sem_inc(l_st[1], 1)
                    with sp.Fori(0, B) as b:
                        with sp.Fori(0, NL // 2) as c2:
                            k = b * (NL // 2) + c2
                            for n, ch, bd in cells():
                                z0, z1 = BANDS[bd][2]
                                sp.wait_ge(l_z, k * NSTEP + n + 1)
                                sp.sem_inc(sp_passed, 1)
                                sp.dma_start(xl[0:z1 - z0, n % 2, :], x[b, c2 * 2 + ch, z0:z1, :]
                                             ).then_inc(l_in[n % 2], 16)
                                if n >= LAG:
                                    store_local(sp, k, n - LAG, b, c2)
                            for n in range(NSTEP - LAG, NSTEP):
                                store_local(sp, k, n, b, c2)
                    for n in (0, 1):
                        sp.wait_ge(l_st[n], 1 + 16 * (B * NL // 2) * NB)

                def y1_out(act, k, n):
                    a0, a1 = BANDS[n % NB][1]
                    act.wait_ge(l_p1, k * NSTEP + n + 3)
                    act.wait_ge(l_p2, k * NSTEP + n + 1)
                    nc.scalar.copy(y1[0:a1 - a0, n % 2, 2:W + 2], banks[0:a1 - a0, n % 2, :]).then_inc(l_y1, 1)

                @block.scalar
                def _(act):
                    act.sem_inc(l_z, 2)
                    act.sem_inc(l_y1, 2)
                    act.wait_ge(l_set, 2)
                    with act.Fori(0, B) as b:
                        with act.Fori(0, NL // 2) as c2:
                            k = b * (NL // 2) + c2
                            for n, ch, bd in cells():
                                z0, z1 = BANDS[bd][2]
                                act.wait_ge(l_in[n % 2], 16 * (k * NB + n // 2 + 1))
                                act.wait_ge(l_p1, k * NSTEP + n + 1)
                                act.wait_ge(l_T, 2 * k + ch + 1)
                                nc.scalar.activation(zl[0:z1 - z0, n % 2, 1:W + 1], xl[0:z1 - z0, n % 2, :],
                                                     ACT.Identity, bias=taps[0:z1 - z0, ch, 35:36],
                                                     scale=taps[0:z1 - z0, ch, 34:35]).then_inc(l_z, 1)
                                if n >= 1:
                                    y1_out(act, k, n - 1)
                            y1_out(act, k, NSTEP - 1)

                @block.tensor
                def _(pe):
                    pe.sem_inc(l_p1, 2)
                    pe.sem_inc(l_p2, 2)
                    pe.wait_ge(l_set, 2)

                    def three(k, n):
                        ch, bd = n // NB, n % NB
                        (r0, r1), (a0, a1), (z0, z1) = BANDS[bd]
                        pe.wait_ge(l_z, k * NSTEP + n + 3)
                        pe.wait_ge(l_y1, k * NSTEP + n + 1)
                        off = a0 - z0
                        for dx in range(3):
                            last = nc.tensor.matmul(banks[0:a1 - a0, n % 2, :],
                                                    T3[0:z1 - z0, ch, dx, off:off + a1 - a0],
                                                    zl[0:z1 - z0, n % 2, dx:dx + W], start=dx == 0, stop=dx == 2)
                        last.then_inc(l_p1, 1)

                    def five(k, n):
                        ch, bd = n // NB, n % NB
                        (r0, r1), (a0, a1), (z0, z1) = BANDS[bd]
                        pe.wait_ge(l_y1, k * NSTEP + n + 3)
                        pe.wait_ge(l_y2, k * NSTEP + n + 1)
                        off = r0 - a0
                        for dx in range(5):
                            last = nc.tensor.matmul(banks[0:r1 - r0, 2 + n % 2, :],
                                                    T5[0:a1 - a0, ch, dx, off:off + r1 - r0],
                                                    y1[0:a1 - a0, n % 2, dx:dx + W], start=dx == 0, stop=dx == 4)
                        last.then_inc(l_p2, 1)

                    with pe.Fori(0, B) as b:
                        with pe.Fori(0, NL // 2) as c2:
                            k = b * (NL // 2) + c2
                            for n in range(NSTEP):
                                if n % NB == 0:
                                    pe.wait_ge(l_T, 2 * k + n // NB + 1)
                                three(k, n)
                                if n:
                                    five(k, n - 1)
                            five(k, NSTEP - 1)

                @block.vector
                def _(dve):
                    v = nc.vector
                    for n in (0, 1):
                        v.memset(zl[:, n, :], 0.0)
                        last = v.memset(y1[:, n, :], 0.0)
                    last.then_inc(l_set, 2)
                    dve.sem_inc(l_y2, 2)
                    dve.sem_inc(l_chain, 1)

                    def matrices(cell, ch):
                        base = cell * 34 + 1
                        v.tensor_copy(taps[:, ch, :], local_k[:, bass.ds(cell, 1), :]
                                      .rearrange("p a q -> p (a q)")).then_inc(l_chain, 1)
                        dve.wait_ge(l_chain, base + 1)
                        n = 1
                        for T, side, first in ((T3, 3, 0), (T5, 5, 9)):
                            for ky in range(side):
                                if ky:
                                    dve.wait_ge(l_chain, base + n)
                                for dx in range(side):
                                    s = 3 + ky - side // 2
                                    tap = taps[:, ch, first + ky * side + dx:first + ky * side + dx + 1]
                                    diagonal = K["diagonals"][:, s:s + 132]
                                    if ky == 0:
                                        i = v.tensor_scalar(T[:, ch, dx, :], diagonal, tap, None, ALU.mult)
                                    else:
                                        i = v.scalar_tensor_tensor(T[:, ch, dx, :], diagonal, tap, T[:, ch, dx, :],
                                                                   ALU.mult, ALU.add)
                                    n += 1
                                    i.then_inc(l_T if n == 35 else l_chain, 1)
                                if n in (10, 20, 30):
                                    yield

                    def y2_out(k, n):
                        r0, r1 = BANDS[n % NB][0]
                        dve.wait_ge(l_p2, k * NSTEP + n + 3)
                        dve.wait_ge(l_st[n % 2], 16 * (k * NB + n // 2) + 1)
                        v.tensor_copy(y2[0:r1 - r0, n % 2, :], banks[0:r1 - r0, 2 + n % 2, :]).then_inc(l_y2, 1)

                    for _part in matrices(0, 0):
                        pass
                    with dve.Fori(0, B * NL // 2) as k:
                        for ch in range(2):
                            parts = matrices(2 * k + ch + 1, 1 - ch)
                            for n in range(ch * NB, (ch + 1) * NB):
                                next(parts, None)
                                if n == (ch + 1) * NB - 1:
                                    for _part in parts:
                                        pass
                                y2_out(k, n)

        early.close()

        band = sb("band", [NF + 1, WIN, W + 2])
        wins = sb("wins", [NF + 1, W + 2, WIN])
        hidden = sb("hidden", [NWIN + 1, 3 * NF, PW])
        prod = sb("prod", [NSPEC, NPAIR, 2, NF])
        vpix = sb("vpix", [PX, NPAIR, 2, NF])
        kspec = sb("kspec", [NSPEC, 2, QKB * PW])
        osb = sb("osb", [2 * NF, 512])
        sq = sb("sq", [2 * NF, 512])
        rstd = sb("rstd", [2 * NF, 512])
        normed = sb("normed", [2 * NF, 512])
        mixed = sb("mixed", [128, PS, HWID])
        xa = sb("xa", [128, PS, HWID])
        ot = sb("ot", [128, PS, HWID])
        hid_cur = sb("hid_cur", [NF + 1, 3 * NF])
        a_cur = sb("a_cur", [128, 1])
        c_cur = sb("c_cur", [128, 1])

        m_set = sem("main_tiles_set")
        band_in = sem("band_in")
        edge_rows_in = sem("edge_rows_of_band_in")
        cur_set = sem("batch_coefficients_set")
        s1_mm = sem("s1_products")
        S1_LEAD = NS1
        pool_passed = sem("pool_passed_its_waits")
        wins_done = sem("windows_ready")
        s1_act = sem("s1_copied_by_act")
        s1_dve = sem("s1_copied_by_dve")
        qk_mm = sem("qk_products")
        qk_act = sem("k_spectra_copied")
        qk_dve = sem("spectral_products")
        v_mm = sem("v_products")
        v_act = sem("v_copied")
        o_mm = sem("inverse_dft")
        o_act = sem("inverse_dft_copied")
        oc_mm = sem("centered")
        sq_act = sem("squared")
        var_mm = sem("variance")
        ln_act = sem("variance_log")
        r_act = sem("rstd_ready")
        vt_mm = sem("v_transposed")
        t_dve = sem("normed_ready")
        y_dve = sem("mixed_ready")
        fin_mm = sem("final_products")
        fin_dve = sem("final_sums")
        xr_in = sem("residual_x_in")
        y2_in = sem("local_branch_in")
        xa_done = sem("residual_scaled")
        stored = sem("output_stored")

        BO, BOC, BVAR, BVT = 4, 5, 6, 7

        def after(eng, s, count):
            eng.wait_ge(s, count + 1)

        def rows_of_batch(eng, b, row):
            k0 = b * NPR
            row(k0, None)
            with eng.Fori(1, NPR) as j:
                row(k0 + j, k0 + j - 1)
            row(None, k0 + (NPR - 1))

        with nc.Block() as block:
            @block.gpsimd
            def _(pool):
                nc.gpsimd.memset(band[:, :, :], 1.0).then_inc(m_set, 1)
                nc.gpsimd.memset(hidden[:, :, :], 1.0).then_inc(m_set, 1)
                pool.wait_ge(m_set, 2)
                nc.gpsimd.memset(band[:, :, 0:1], 0.0).then_inc(m_set, 1)
                nc.gpsimd.memset(band[:, :, W + 1:W + 2], 0.0).then_inc(m_set, 1)
                pool.sem_inc(xa_done, 1)
                pool.sem_inc(wins_done, 1)
                with pool.Fori(0, B) as b:
                    pool.wait_ge(cur_set, b + 1)

                    def windows(k):
                        after(pool, band_in, 16 * (k + 1))
                        for i in range(4):
                            after(pool, s1_mm, 16 * k - (16 - min(16, 4 * (i + 1) + 1)) + S1_LEAD)
                            pool.sem_inc(pool_passed, 1)
                            lo, hi = i * (W // 4), (i + 1) * (W // 4) + (2 if i == 3 else 0)
                            nc.gpsimd.tensor_copy(wins[:, lo:hi, :].rearrange("p x y -> p y x"),
                                                  band[:, :, lo:hi]).then_inc(wins_done, 1)

                    def residual(k):
                        after(pool, xr_in, 32 * (k + 1))
                        pool.sem_inc(pool_passed, 1)
                        nc.gpsimd.tensor_scalar(xa[:, :, :], xa[:, :, :], a_cur[:, :], c_cur[:, :],
                                                ALU.mult, ALU.add).then_inc(xa_done, 1)

                    windows(b * NPR)
                    with pool.Fori(1, NPR) as j:
                        windows(b * NPR + j)
                        residual(b * NPR + j - 1)
                    residual(b * NPR + (NPR - 1))

            @block.sync
            def _(sp):
                for s in (xr_in, y2_in, stored):
                    sp.sem_inc(s, 1)
                sp.sem_inc(band_in, 1)
                sp.wait_ge(m_set, 4)

                def load_band(b, k, j, y0, n, at):
                    sp.dma_start(band[0:NF, at:at + n, 1:W + 1], x[b, NL:C, bass.ds(y0, n), :]
                                 ).then_inc(band_in, 16)

                def set_row(r, source):
                    if source == "zeros":
                        sp.dma_start(band[:, r, 1:W + 1], t["zeros"][:, :]).then_inc(edge_rows_in, 16)
                    else:
                        sp.dma_start(band[NF:NF + 1, r, 1:W + 1], t["ones"][:, :]).then_inc(edge_rows_in, 16)

                def load_rest(b, k, j):
                    after(sp, fin_dve, 4 * k)
                    sp.sem_inc(sp_passed, 1)
                    after(sp, fin_mm, 4 * k)
                    sp.sem_inc(sp_passed, 1)
                    for s in range(2):
                        sp.dma_start(xa[C * s:C * (s + 1), :, :],
                                     x[b, :, bass.ds(j * PS, PS), HWID * s:HWID * (s + 1)]).then_inc(xr_in, 16)
                        p = 2 * NF + NL * s
                        sp.dma_start(mixed[p:p + NL, :, :],
                                     scratch[b, :, bass.ds(j * PS, PS), HWID * s:HWID * (s + 1)]).then_inc(y2_in, 16)

                def store(b, k, j):
                    after(sp, fin_dve, 4 * (k + 1))
                    sp.sem_inc(sp_passed, 1)
                    for s in range(2):
                        sp.dma_start(out[b, :, bass.ds(j * PS, PS), HWID * s:HWID * (s + 1)],
                                     ot[C * s:C * (s + 1), :, :]).then_inc(stored, 16)

                with sp.Fori(0, B) as b:
                    k0 = b * NPR
                    after(sp, wins_done, 4 * k0)
                    sp.sem_inc(sp_passed, 1)
                    set_row(0, "zeros")
                    set_row(WIN - 1, "ones")
                    sp.wait_ge(edge_rows_in, 64 * b + 32)
                    load_band(b, k0, 0, 0, PS + 1, 1)
                    after(sp, wins_done, 4 * (k0 + 1))
                    sp.sem_inc(sp_passed, 1)
                    set_row(0, "ones")
                    sp.wait_ge(edge_rows_in, 64 * b + 48)
                    load_band(b, k0 + 1, 1, PS - 1, WIN, 0)
                    load_rest(b, k0, 0)
                    with sp.Fori(2, NPR - 1) as j:
                        after(sp, wins_done, 4 * (k0 + j))
                        sp.sem_inc(sp_passed, 1)
                        load_band(b, k0 + j, j, j * PS - 1, WIN, 0)
                        store(b, k0 + j - 2, j - 2)
                        load_rest(b, k0 + j - 1, j - 1)
                    j = NPR - 1
                    after(sp, wins_done, 4 * (k0 + j))
                    sp.sem_inc(sp_passed, 1)
                    set_row(WIN - 1, "zeros")
                    sp.wait_ge(edge_rows_in, 64 * b + 64)
                    load_band(b, k0 + j, j, j * PS - 1, WIN - 1, 0)
                    store(b, k0 + j - 2, j - 2)
                    load_rest(b, k0 + j - 1, j - 1)
                    store(b, k0 + j - 1, j - 1)
                    load_rest(b, k0 + j, j)
                    store(b, k0 + j, j)
                sp.wait_ge(stored, 32 * B * NPR + 1)

            @block.tensor
            def _(pe):
                for s in (s1_mm, qk_mm, v_mm, o_mm, oc_mm, var_mm, vt_mm, fin_mm):
                    pe.sem_inc(s, 1)
                pe.sem_inc(s1_mm, S1_LEAD)
                pe.wait_ge(m_set, 4)

                def s1(k, m):
                    if m == 0:
                        after(pe, v_act, 3 * k)
                        after(pe, qk_dve, 6 * k)
                    elif m >= 2 and m % 2 == 0:
                        after(pe, s1_act, 8 * k + m // 2)
                    elif m >= 2:
                        after(pe, s1_dve, 8 * k + m // 2)
                    after(pe, wins_done, 4 * k + min(m // 4 + 1 + (m % 4 == 3), 4))
                    for i in range(4):
                        x0 = (4 * m + i) * PS
                        last = nc.tensor.matmul(banks[0:NWIN, m % 2 * 2 + i // 2, i % 2 * 3 * NF:(i % 2 + 1) * 3 * NF],
                                                wins[:, x0:x0 + WIN, :].rearrange("p x y -> p (x y)"), hid_cur[:, :], start=True, stop=True)
                    last.then_inc(s1_mm, 1)

                def s2_qk(k, q):
                    if q == 0:
                        after(pe, s1_act, 8 * k + 8)
                        after(pe, s1_dve, 8 * k + 8)
                    elif q >= 2:
                        after(pe, qk_dve, 6 * k + q - 1)
                    for part in range(2):
                        for c in range(QKB):
                            ch = q * QKB + c
                            last = nc.tensor.matmul(banks[:, q % 2 * 2 + part, c * PW:(c + 1) * PW],
                                                    G[:, ch, part * NSPEC:(part + 1) * NSPEC],
                                                    hidden[:, part * NF + ch, :], start=True, stop=True)
                    last.then_inc(qk_mm, 1)

                def s2_v(k, r):
                    if r < 2:
                        after(pe, qk_dve, 6 * k + 5 + r)
                    else:
                        after(pe, v_act, 3 * k + 1)
                    for c in range(VB):
                        ch = r * VB + c
                        last = nc.tensor.matmul(banks[0:PX, r % 2 * 2 + c // 8, c % 8 * PW:(c % 8 + 1) * PW],
                                                G[:, ch, 2 * NSPEC:NG], hidden[:, 2 * NF + ch, :],
                                                start=True, stop=True)
                    last.then_inc(v_mm, 1)

                def chunk_out(bank, i):
                    return banks[0:2 * NF, bank, :].rearrange("p (y i x) -> p y i x", y=PS, i=8)[:, :, i, :]

                def norm_step(k, m):
                    c, step = m // 4, m % 4
                    if step == 0:
                        if c == 0:
                            after(pe, fin_dve, 4 * k)
                        after(pe, o_act, 4 * k + c)
                        for i in range(8):
                            last = nc.tensor.matmul(chunk_out(BO, i),
                                                    prod[:, 8 * c + i, :, :].rearrange("p s c -> p (s c)"),
                                                    K["inverse"][:, :].rearrange("p (y x) -> p y x", y=PS),
                                                    start=True, stop=True)
                        last.then_inc(o_mm, 1)
                    elif step == 1:
                        after(pe, o_act, 4 * k + c + 1)
                        after(pe, t_dve, 4 * k + c)
                        nc.tensor.matmul(banks[0:2 * NF, BOC, :], K["center"][:, :], osb[:, :],
                                         start=True, stop=True).then_inc(oc_mm, 1)
                    elif step == 2:
                        after(pe, sq_act, 4 * k + c + 1)
                        after(pe, ln_act, 4 * k + c)
                        after(pe, y_dve, 4 * k + c)
                        nc.tensor.matmul(banks[0:2 * NF, BVAR, :], K["chan_avg"][:, :], sq[:, :],
                                         start=True, stop=True).then_inc(var_mm, 1)
                        for i in range(8):
                            last = nc.tensor.transpose(chunk_out(BVT, i),
                                                       vpix[:, 8 * c + i, :, :].rearrange("p s c -> p (s c)"),
                                                       K["identity"][:, :].rearrange("p (y x) -> p y x", y=PS))
                        last.then_inc(vt_mm, 1)

                def final(k, f):
                    if f == 0:
                        after(pe, y_dve, 4 * k + 4)
                        after(pe, y2_in, 32 * (k + 1))
                        after(pe, ln_act, 4 * k + 4)
                    elif f >= 2:
                        after(pe, fin_dve, 4 * k + f - 1)
                    nc.tensor.matmul(banks[:, BO if f % 2 == 0 else BVAR, :],
                                     final_w[:, :, :].rearrange("p s c -> p (s c)"),
                                     mixed[:, f * RPG:(f + 1) * RPG, :].rearrange("p r x -> p (r x)"),
                                     start=True, stop=True).then_inc(fin_mm, 1)

                def row(k, kl):
                    for m in range(NS1):
                        if k is not None:
                            s1(k, m)
                        if kl is not None:
                            norm_step(kl, m)
                    for q in range(NQK):
                        if k is not None:
                            s2_qk(k, q)
                        if kl is not None and 1 <= q <= NRG:
                            final(kl, q - 1)
                    for r in range(NV):
                        if k is not None:
                            s2_v(k, r)

                with pe.Fori(0, B) as b:
                    pe.wait_ge(cur_set, b + 1)
                    rows_of_batch(pe, b, row)

            def copy_hidden(copy, m):
                return copy(hidden[0:NWIN, :, 4 * m:4 * m + 4].rearrange("p o (b t) -> p b t o", b=2),
                            banks[0:NWIN, m % 2 * 2:m % 2 * 2 + 2, 0:6 * NF].rearrange("p b (t o) -> p b t o", t=2))

            @block.scalar
            def _(act):
                nc.scalar.preload_act_table_set("natural_log_exp_and_others")
                for s in (s1_act, qk_act, v_act, o_act, sq_act, ln_act, r_act):
                    act.sem_inc(s, 1)

                def norm_step(k, m):
                    c, step = m // 4, m % 4
                    if step == 0:
                        after(act, o_mm, 4 * k + c + 1)
                        nc.scalar.copy(osb[:, :], banks[0:2 * NF, BO, :]).then_inc(o_act, 1)
                    elif step == 1:
                        after(act, oc_mm, 4 * k + c + 1)
                        nc.scalar.activation(sq[:, :], banks[0:2 * NF, BOC, :], ACT.Square).then_inc(sq_act, 1)
                    elif step == 2:
                        after(act, var_mm, 4 * k + c + 1)
                        after(act, t_dve, 4 * k + c)
                        nc.scalar.activation(rstd[:, :], banks[0:2 * NF, BVAR, :], ACT.Ln, bias=eps_ln[0:2 * NF, :]
                                             ).then_inc(ln_act, 1)
                        after(act, ln_act, 4 * k + c + 1)
                        nc.scalar.activation(rstd[:, :], rstd[:, :], ACT.Exp, scale=-0.5).then_inc(r_act, 1)

                def row(k, kl):
                    for m in range(NS1):
                        if k is not None and m % 2 == 0:
                            after(act, s1_mm, 16 * k + m + 1 + S1_LEAD)
                            copy_hidden(nc.scalar.copy, m).then_inc(s1_act, 1)
                        if kl is not None:
                            norm_step(kl, m)
                    if k is None:
                        return
                    for q in range(NQK):
                        after(act, qk_mm, 6 * k + q + 1)
                        after(act, qk_dve, 6 * k + max(q - 1, 0))
                        nc.scalar.copy(kspec[:, q % 2, :], banks[:, q % 2 * 2 + 1, :]).then_inc(qk_act, 1)
                    for r in range(NV):
                        after(act, v_mm, 3 * k + r + 1)
                        nc.scalar.copy(vpix[:, :, :, r * VB:(r + 1) * VB].rearrange("p i s c -> p c s i"),
                                       banks[0:PX, r % 2 * 2:r % 2 * 2 + 2, :]
                                       .rearrange("p b (c s i) -> p (b c) s i", s=2, i=NPAIR)).then_inc(v_act, 1)

                with act.Fori(0, B) as b:
                    rows_of_batch(act, b, row)

            @block.vector
            def _(dve):
                v = nc.vector
                for s in (s1_dve, qk_dve, t_dve, y_dve, fin_dve):
                    dve.sem_inc(s, 1)

                def norm(k, c):
                    after(dve, r_act, 4 * k + c + 1)
                    v.scalar_tensor_tensor(normed[:, :], banks[0:2 * NF, BOC, :], ln_w[:, :], rstd[:, :],
                                           ALU.mult, ALU.mult).then_inc(t_dve, 1)
                    after(dve, t_dve, 4 * k + c + 1)
                    after(dve, vt_mm, 4 * k + c + 1)
                    v.scalar_tensor_tensor(mixed[0:2 * NF, :, 64 * c:64 * (c + 1)],
                                           normed[:, :].rearrange("p (y x) -> p y x", y=PS), ln_b[:, :],
                                           banks[0:2 * NF, BVT, :].rearrange("p (y x) -> p y x", y=PS),
                                           ALU.add, ALU.mult).then_inc(y_dve, 1)

                def final(k, f):
                    if f == 0:
                        after(dve, xa_done, k + 1)
                        after(dve, stored, 32 * k)
                    after(dve, fin_mm, 4 * k + f + 1)
                    rows = slice(f * RPG, (f + 1) * RPG)
                    v.tensor_tensor(ot[:, rows, :], banks[:, BO if f % 2 == 0 else BVAR, :]
                                    .rearrange("p (r x) -> p r x", r=RPG), xa[:, rows, :], ALU.add).then_inc(fin_dve, 1)

                def row(k, kl):
                    for m in range(NS1):
                        if k is not None and m % 2 == 1:
                            after(dve, s1_mm, 16 * k + m + 1 + S1_LEAD)
                            copy_hidden(v.tensor_copy, m).then_inc(s1_dve, 1)
                        if kl is not None and m % 4 == 3:
                            norm(kl, m // 4)
                    for q in range(NQK):
                        if k is not None:
                            after(dve, qk_mm, 6 * k + q + 1)
                            after(dve, qk_act, 6 * k + q + 1)
                            v.tensor_tensor(prod[:, :, :, q * QKB:(q + 1) * QKB].rearrange("p i s c -> p c s i"),
                                            banks[:, q % 2 * 2, :].rearrange("p (c s i) -> p c s i", s=2, i=NPAIR),
                                            kspec[:, q % 2, :].rearrange("p (c s i) -> p c s i", s=2, i=NPAIR),
                                            ALU.mult).then_inc(qk_dve, 1)
                        if kl is not None and 1 <= q <= NRG:
                            final(kl, q - 1)

                with dve.Fori(0, B) as b:
                    v.tensor_copy(hid_cur[:, :], hid_ab[:, bass.ds(b, 1), :].rearrange("p b o -> p (b o)"))
                    v.tensor_copy(a_cur[:, :], res_a[:, bass.ds(b, 1)])
                    v.tensor_copy(c_cur[:, :], res_c[:, bass.ds(b, 1)]).then_inc(cur_set, 1)
                    rows_of_batch(dve, b, row)


def kernel(**inputs):
    import numpy as _np
    import concourse.bacc as _bacc
    from concourse import mybir as _mybir
    from concourse.bass_utils import run_bass_kernel_spmd as _run

    def a(name):
        return _np.asarray(inputs[name])

    def twice(v):
        return _np.concatenate([v, v]).reshape(-1, 1)

    table, inverse = dft_tables()
    arrays = dict(shape_constants())
    arrays["inverse"] = inverse
    arrays["dft"] = table.reshape(NG // 32, 10, 32 * (NWIN + 1))
    B, _, H, W = a("x").shape
    arrays["zeros"] = _np.zeros((NF + 1, W), _np.float32)
    arrays["ones"] = _np.ones((1, W), _np.float32)
    arrays["x"] = a("x")
    arrays["gate_w"] = _np.broadcast_to(a("L0_conv_w").reshape(1, 3), (128, 3))
    for n, side in ((1, 3), (2, 5)):
        pre = f"L1_conv_dl{n}_"
        arrays[f"mlp{n}_w1T"] = a(pre + "w1").T
        arrays[f"mlp{n}_b1"] = a(pre + "b1").reshape(NL, 1)
        arrays[f"mlp{n}_w2T"] = a(pre + "w2").reshape(NL, side * side, NL).transpose(2, 1, 0)
        arrays[f"mlp{n}_b2"] = a(pre + "b2").reshape(NL, side * side)
    arrays["hid_wb"] = _np.concatenate([a("L1_conv_fs_hid_w").T, a("L1_conv_fs_hid_b")[None]])
    arrays["dw_wb"] = _np.concatenate([a("L1_conv_fs_dw_w").reshape(3 * NF, 9).T, a("L1_conv_fs_dw_b")[None]])
    arrays["ln_w"] = twice(a("L1_conv_fs_ln_w"))
    arrays["ln_b"] = twice(a("L1_conv_fs_ln_b"))
    arrays["out_w"] = a("L1_conv_fs_out_w")
    arrays["out_b"] = a("L1_conv_fs_out_b").reshape(NF, 1)
    arrays["last_wT"] = a("L1_conv_last_w").T
    arrays["last_b"] = twice(a("L1_conv_last_b"))
    arrays = {n: _np.ascontiguousarray(v) for n, v in arrays.items()}

    nc = _bacc.Bacc("TRN2", target_bir_lowering=False, num_devices=1)
    f32 = _mybir.dt.float32
    t = {n: nc.dram_tensor(f"in_{n}_dram", v.shape, f32, kind="ExternalInput").ap() for n, v in arrays.items()}
    t["out"] = nc.dram_tensor("out_0_dram", (B, C, H, W), f32, kind="ExternalOutput").ap()
    t["local_scratch"] = nc.dram_tensor("local_scratch", (B, NL, H, W), f32, kind="Internal").ap()
    program(nc, t)
    r = _run(nc, [{f"in_{n}_dram": v for n, v in arrays.items()}], core_ids=[0])
    return r.results[0]["out_0_dram"]
```

```python
from contextlib import ExitStack

import numpy as np

import concourse.bass as bass
from concourse import mybir

F32 = mybir.dt.float32
F16 = mybir.dt.float16
ALU = mybir.AluOpType
ACT = mybir.ActivationFunctionType
AX = mybir.AxisListType.X

C = 64
NL = 16
NF = C - NL
PS = 8
WIN = PS + 2
NWIN = WIN * WIN
PX = PS * PS
NSPEC = 128
NG = 2 * NSPEC + PX
HID_SCALE = 64.0
SPEC_SCALE = 8.0
LO = 64
SETK = 9 + 25 + 2
LB_ROWS = 122
EPS_GN = 1e-5
EPS_LN = 1e-6
QKB = 8
VB = 16


def spectral_rows():
    rows = []
    seen = set()
    for u in range(PS):
        for v in range(PS):
            other = ((-u) % PS, (-v) % PS)
            if other in seen:
                continue
            seen.add((u, v))
            own = other == (u, v)
            rows.append((u, v, 1.0 if own else 2.0, "re", "re"))
            if not own:
                rows += [(u, v, 2.0, "im", "im"), (u, v, 2.0, "re", "im"), (u, v, 2.0, "im", "re")]
    return rows


def dft_tables():
    rows = spectral_rows()
    y, x = np.meshgrid(np.arange(PS), np.arange(PS), indexing="ij")
    E = np.zeros((10, NG, NWIN + 1))
    inverse = np.zeros((NSPEC, PX))
    for n, (u, v, weight, pq, pk) in enumerate(rows):
        angle = 2 * np.pi * ((u * y + v * x) % PS) / PS
        part = {"re": np.cos(angle), "im": -np.sin(angle)}
        for base, p in ((0, pq), (NSPEC, pk)):
            for t in range(9):
                window = np.zeros((WIN, WIN))
                window[t // 3:t // 3 + PS, t % 3:t % 3 + PS] = part[p]
                E[t, base + n, :NWIN] = window.T.ravel()
            E[9, base + n, NWIN] = part[p].sum()
        if pq == pk:
            inverse[n] = (weight * (1 if pq == "re" else -1) * np.cos(angle) / PX).ravel()
        else:
            inverse[n] = (-weight * np.sin(angle) / PX).ravel()
    for p in range(PX):
        for t in range(9):
            E[t, 2 * NSPEC + p, (p % PS + t % 3) * WIN + p // PS + t // 3] = 1.0
        E[9, 2 * NSPEC + p, NWIN] = 1.0
    E *= SPEC_SCALE
    inverse /= SPEC_SCALE * SPEC_SCALE
    chunks = E.reshape(10, NG // 32, 32, NWIN + 1).transpose(1, 0, 2, 3)
    return np.ascontiguousarray(chunks, np.float32), inverse.astype(np.float32)


def shape_constants():
    p = np.arange(128)
    k = {}
    k["pair_avg"] = (p[:, None] // 2 == p // 2) / 2
    k["quad_avg"] = (p[:, None] // 4 == p // 4) / 4
    k["from_prev"] = (p[:, None] == p - 2)
    k["from_next"] = (p[:, None] == p + 2)
    for h in range(2):
        k[f"pick_half{h}"] = (p[:, None] == 2 * np.arange(NL) + h)
    k["pick_freq"] = (p[:, None] == 2 * (NL + np.arange(NF + 1))) & (np.arange(NF + 1) < NF)
    k["pick_out"] = (p[:, None] == 2 * (p % C))
    m = np.arange(2 * NF)
    same = (m[:, None] // NF == m // NF) / NF
    k["center"] = np.pad(np.eye(2 * NF) - same, (0, 128 - 2 * NF))
    k["chan_avg"] = np.pad(same, (0, 128 - 2 * NF))
    k["w_scale"] = HID_SCALE * (np.arange(NF + 1) < NF)[:, None]
    k["bias_scale"] = HID_SCALE * (np.arange(NF + 1) == NF)[:, None]
    k["side0"] = (m < NF)[:, None]
    k["side1"] = (m >= NF)[:, None]
    k["identity"] = np.eye(PX)
    k["ones_row"] = (np.arange(NF + 1) == NF)[:, None]
    k["diagonals"] = (np.arange(138) == p[:, None] + 3)
    k["spread"] = np.repeat(np.eye(NL), 128, axis=1)
    return {n: np.ascontiguousarray(v, np.float32) for n, v in k.items()}


def bands(H):
    out = []
    n = -(-H // LB_ROWS)
    for i in range(n):
        r0, r1 = i * H // n, (i + 1) * H // n
        y0, y1 = max(0, r0 - 2), min(H, r1 + 2)
        z0, z1 = max(0, y0 - 1), min(H, y1 + 1)
        out.append(((r0, r1), (y0, y1), (z0, z1)))
    return out


def program(nc, t):
    x, out, scratch = t["x"], t["out"], t["local_scratch"]
    B, _, H, W = x.shape
    HW = H * W
    HH = H // 2
    NPR = H // PS
    PW = W // PS
    NPAIR = PW // 2
    SR = 8
    NST = HH // SR
    NCH = NPAIR // 8
    NS1 = PW // 4
    NQK, NV = NF // QKB, NF // VB
    HWID = W // 2
    NRG = PS * HWID // 512
    RPG = PS // NRG
    BANDS = bands(H)
    NB = len(BANDS)
    assert W == 512 and NPAIR % 8 == 0 and NST % 2 == 0 and NS1 == 16 and NRG == 4

    ctx = ExitStack()
    with ctx:
        def sb(name, shape, dt=F32):
            return ctx.enter_context(nc.sbuf_tensor(name, shape, dt))

        def sem(name):
            return ctx.enter_context(nc.semaphore(name))

        banks = ctx.enter_context(nc.psum_tensor("banks", [128, 8, 512], F32))

        K = {n: sb(n, list(t[n].shape)) for n in ("center", "chan_avg", "identity", "inverse")}
        gate_w = sb("gate_w", [128, 3])
        w1T = [sb(f"mlp{n}_w1T", [NL, NL]) for n in (1, 2)]
        b1 = [sb(f"mlp{n}_b1", [NL, 1]) for n in (1, 2)]
        w2T = [sb("mlp1_w2T", [NL, 9, NL]), sb("mlp2_w2T", [NL, 25, NL])]
        b2 = [sb("mlp1_b2", [NL, 9]), sb("mlp2_b2", [NL, 25])]
        hid_wb = sb("hid_wb", [NF + 1, 3 * NF])
        dw_wb = sb("dw_wb", [10, 3 * NF])
        ln_w = sb("ln_w", [2 * NF, 1])
        ln_b = sb("ln_b", [2 * NF, 1])
        out_w2 = sb("out_w2", [NF, 2, NF])
        last_wT = sb("last_wT", [NF, 2, C])
        out_b = sb("out_b", [NF, 1])
        last_b = sb("last_b", [128, 1])
        final_w = sb("final_w", [128, 2, C])
        G = [sb(f"G_{part}", [NWIN + 1, NF, NG], F16) for part in ("hi", "lo")]
        hid_m = [sb(f"hid_m_{part}", [128, B, 3 * NF], F16) for part in ("hi", "lo")]
        in_a = sb("in_a", [NF + 1, B])
        res_a = sb("res_a", [128, B])
        res_c = sb("res_c", [128, B])
        eps_gn = sb("eps_gn", [128, 1])
        eps_ln = sb("eps_ln", [128, 1])

        s_const = sem("constants_loaded")
        s_set = sem("constants_set")
        sp_passed = sem("sync_passed_its_waits")

        early = ctx.enter_context(ExitStack())
        K["diagonals"] = early.enter_context(nc.sbuf_tensor("diagonals", [128, 138], F32))
        local_k = early.enter_context(nc.sbuf_tensor("local_k", [128, B * NL + 1, SETK], F32))

        with ExitStack() as st:
            for n in ("pair_avg", "quad_avg", "from_prev", "from_next", "pick_half0", "pick_half1",
                      "pick_freq", "pick_out", "side0", "side1", "ones_row", "w_scale", "bias_scale", "spread"):
                K[n] = st.enter_context(nc.sbuf_tensor(n, list(t[n].shape), F32))

            def sb1(name, shape):
                return st.enter_context(nc.sbuf_tensor(name, shape, F32))

            def sem1(name):
                return st.enter_context(nc.semaphore(name))

            xs = sb1("xs", [128, 2, SR * W])
            stats = sb1("stats", [128, B, NST * SR, 6])
            cols = sb1("cols", [128, B, NST, 2])
            edge = sb1("edge", [128, B, W])
            ebuf = sb1("ebuf", [10, 32 * (NWIN + 1)])
            mv = sb1("mv", [128, B, 2])
            V = {n: sb1(f"c_{n}", [128, B]) for n in (
                "mean", "var", "mc", "d", "e", "vc", "M", "d1", "e1", "v1", "i1", "r", "s", "t1", "t2",
                "g", "rg", "a", "m2", "a2", "v2", "bb", "d2", "e2", "v3", "i2", "r2", "A", "B", "bm", "Am")}
            BS = sb1("BS", [128, 10, B])
            H0 = sb1("H0", [NL, 8, B])
            H1 = sb1("H1", [NL, 8, B])
            CS = sb1("CS", [NL, 2, B])
            TOT = sb1("TOT", [NL, B])
            hid = [sb1(f"hid{n}", [NL, B]) for n in (1, 2)]
            ST = sb1("ST", [NL, B, 9])
            PR = sb1("PR", [NL, B, 9])
            KB = sb1("KB", [NL, B, SETK])
            pooled2 = sb1("pooled2", [NL, B])
            pooled2s = sb1("pooled2s", [NL, B])
            AB = sb1("AB", [NF + 1, 2, B])
            B49 = sb1("B49", [NF + 1, B])
            Bb = sb1("Bb", [NF + 1, B, NF + 1])
            ones49 = sb1("ones49", [NF + 1, NF + 1])
            bias_row = sb1("bias_row", [NF + 1, B, 3 * NF])
            bias_tot = sb1("bias_tot", [128, 1])

            x_in = [sem1("x_tile_even_in"), sem1("x_tile_odd_in")]
            edge_in = sem1("edge_rows_in")
            stat_done = sem1("stat_tiles_done")
            prep_dve = sem1("prep_dve")
            prep_pe = sem1("prep_pe")
            prep_chain = sem1("prep_chain")
            prep_act = sem1("prep_act")
            table_in = sem1("table_in")
            table_mm = sem1("table_products")
            table_hi = sem1("table_high_parts")
            table_out = sem1("table_split")

            NCONST = [0]
            x_halves = x.rearrange("b c (h r) w -> b (c h) (r w)", h=2)
            with nc.Block() as block:
                @block.sync
                def _(sp):
                    def load(dst, src):
                        sp.dma_start(dst, src).then_inc(s_const, 16)
                        NCONST[0] += 16

                    for n in K:
                        load(K[n][:, :], t[n][:, :])
                    load(gate_w[:, :], t["gate_w"][:, :])
                    for n in (0, 1):
                        load(w1T[n][:, :], t[f"mlp{n + 1}_w1T"][:, :])
                        load(b1[n][:, :], t[f"mlp{n + 1}_b1"][:, :])
                        load(w2T[n][:, :, :], t[f"mlp{n + 1}_w2T"][:, :, :])
                        load(b2[n][:, :], t[f"mlp{n + 1}_b2"][:, :])
                    load(hid_wb[:, :], t["hid_wb"][:, :])
                    load(dw_wb[:, :], t["dw_wb"][:, :])
                    load(ln_w[:, :], t["ln_w"][:, :])
                    load(ln_b[:, :], t["ln_b"][:, :])
                    for s in range(2):
                        load(out_w2[:, s, :], t["out_w"][:, :])
                        load(last_wT[:, s, :], t["last_wT"][NL:C, :])
                    load(out_b[:, :], t["out_b"][:, :])
                    load(last_b[:, :], t["last_b"][:, :])
                    sp.wait_ge(s_set, 1)
                    for s in range(2):
                        load(final_w[2 * NF + NL * s:2 * NF + NL * (s + 1), s, :], t["last_wT"][0:NL, :])
                    for b in range(B):
                        for h in range(2):
                            sp.dma_start(edge[h:128:2, b, :], x[b, :, h * (H - 1), :]).then_inc(edge_in, 16)
                    for n in range(NG // 32):
                        if n:
                            sp.wait_ge(table_mm, n)
                        sp.dma_start(ebuf[:, :], t["dft"][n]).then_inc(table_in, 16)
                    with sp.Fori(0, B) as b:
                        with sp.Fori(0, NST // 2) as n2:
                            for par in range(2):
                                sp.wait_ge(stat_done, b * NST + n2 * 2 + par + 1)
                                sp.sem_inc(sp_passed, 1)
                                sp.dma_start(xs[:, par, :], x_halves[b, :, bass.ds((n2 * 2 + par) * SR * W, SR * W)]
                                             ).then_inc(x_in[par], 16)

                @block.gpsimd
                def _(pool):
                    nc.gpsimd.memset(final_w[:, :, :], 0.0).then_inc(s_set, 1)
                    nc.gpsimd.memset(eps_gn[:, :], EPS_GN).then_inc(s_set, 1)
                    nc.gpsimd.memset(eps_ln[:, :], EPS_LN).then_inc(s_set, 1)
                    nc.gpsimd.memset(ones49[:, :], 1.0).then_inc(s_set, 1)
                    nc.gpsimd.memset(local_k[:, B * NL, :], 0.0).then_inc(s_set, 1)
                    for part in hid_m:
                        nc.gpsimd.memset(part[:, :, :], 0.0).then_inc(s_set, 1)

                @block.tensor
                def _(pe):
                    pe.wait_ge(s_const, NCONST[0])

                    for n in range(NG // 32):
                        pe.wait_ge(table_in, 16 * (n + 1))
                        if n:
                            pe.wait_ge(table_out, 4 * n)
                        kind = min(n * 32 // NSPEC, 2)
                        for j in range(32):
                            last = nc.tensor.matmul(banks[0:NWIN + 1, j // 8, (j % 8) * NF:(j % 8 + 1) * NF],
                                                    ebuf[:, j * (NWIN + 1):(j + 1) * (NWIN + 1)],
                                                    dw_wb[:, kind * NF:(kind + 1) * NF], start=True, stop=True)
                        last.then_inc(table_mm, 1)

                    last = nc.tensor.matmul(banks[0:2 * NF, 6, 0:C], out_w2[:, :, :].rearrange("m s c -> m (s c)"),
                                            last_wT[:, 0, :], start=True, stop=True)
                    last = nc.tensor.matmul(banks[:, 6, 100:101], last_wT[:, :, :].rearrange("m s c -> m (s c)"),
                                            out_b[:, :], start=True, stop=True)
                    last.then_inc(prep_pe, 1)

                    pe.wait_ge(prep_dve, 2)
                    nc.tensor.matmul(banks[:, 4, 0:B], K["pair_avg"][:, :], V["mean"][:, :],
                                     start=True, stop=True).then_inc(prep_pe, 1)
                    pe.wait_ge(prep_dve, 3)
                    nc.tensor.matmul(banks[:, 4, 8:8 + B], K["pair_avg"][:, :], V["e"][:, :], start=True, stop=True)
                    nc.tensor.matmul(banks[:, 4, 16:16 + B], K["quad_avg"][:, :], V["mc"][:, :],
                                     start=True, stop=True).then_inc(prep_pe, 1)
                    pe.wait_ge(prep_dve, 4)
                    nc.tensor.matmul(banks[:, 4, 24:24 + B], K["quad_avg"][:, :], V["e1"][:, :],
                                     start=True, stop=True)
                    nc.tensor.matmul(banks[:, 4, 32:32 + B], K["from_prev"][:, :], V["s"][:, :], start=True, stop=True)
                    nc.tensor.matmul(banks[:, 4, 40:40 + B], K["from_next"][:, :], V["s"][:, :],
                                     start=True, stop=True).then_inc(prep_pe, 1)
                    pe.wait_ge(prep_dve, 6)
                    nc.tensor.matmul(banks[:, 4, 48:48 + B], K["quad_avg"][:, :], V["m2"][:, :],
                                     start=True, stop=True).then_inc(prep_pe, 1)
                    pe.wait_ge(prep_dve, 7)
                    nc.tensor.matmul(banks[:, 4, 56:56 + B], K["quad_avg"][:, :], V["e2"][:, :],
                                     start=True, stop=True).then_inc(prep_pe, 1)
                    pe.wait_ge(prep_dve, 9)
                    bs = BS[:, :, :].rearrange("p q b -> p (q b)")
                    nc.tensor.matmul(banks[0:NL, 5, 0:8 * B], K["pick_half0"][:, :], bs[:, 0:8 * B], start=True, stop=True)
                    nc.tensor.matmul(banks[0:NL, 5, 64:64 + 8 * B], K["pick_half1"][:, :], bs[:, 0:8 * B],
                                     start=True, stop=True)
                    nc.tensor.matmul(banks[0:NF + 1, 5, 128:128 + 2 * B], K["pick_freq"][:, :], bs[:, 6 * B:8 * B],
                                     start=True, stop=True)
                    nc.tensor.matmul(banks[:, 5, 192:192 + 2 * B], K["pick_out"][:, :], bs[:, 8 * B:10 * B],
                                     start=True, stop=True).then_inc(prep_pe, 1)
                    pe.wait_ge(prep_dve, 10)
                    for b in range(B):
                        nc.tensor.matmul(banks[0:NF + 1, b % 4, 0:3 * NF], Bb[:, b, :], hid_wb[:, :], start=True, stop=True)
                    nc.tensor.matmul(banks[0:NL, 6, 0:B], w1T[0][:, :], H0[:, 5, :],
                                     start=True, stop=True).then_inc(prep_pe, 1)
                    pe.wait_ge(prep_act, 4)
                    for q in range(9):
                        last = nc.tensor.matmul(banks[0:NL, 6, 16 + q * B:16 + (q + 1) * B], w2T[0][:, q, :],
                                                hid[0][:, :], start=True, stop=True)
                    last.then_inc(prep_pe, 1)
                    pe.wait_ge(prep_dve, 11)
                    nc.tensor.matmul(banks[0:NL, 7, 0:B], w1T[1][:, :], pooled2s[:, :],
                                     start=True, stop=True).then_inc(prep_pe, 1)
                    pe.wait_ge(prep_act, 5)
                    for q in range(25):
                        last = nc.tensor.matmul(banks[0:NL, 7, 16 + q * B:16 + (q + 1) * B], w2T[1][:, q, :],
                                                hid[1][:, :], start=True, stop=True)
                    last.then_inc(prep_pe, 1)
                    pe.wait_ge(prep_dve, 12)
                    for c in range(NL):
                        last = nc.tensor.matmul(banks[:, c // 3 % 6, c % 3 * B * SETK:(c % 3 + 1) * B * SETK],
                                                K["spread"][:, c * 128:(c + 1) * 128],
                                                KB[:, :, :].rearrange("p b q -> p (b q)"), start=True, stop=True)
                    last.then_inc(prep_pe, 1)

                @block.scalar
                def _(act):
                    act.wait_ge(s_const, NCONST[0])
                    for n in range(NG // 32):
                        act.wait_ge(table_mm, n + 1)
                        for j in range(4):
                            nc.scalar.copy(G[0][:, :, 32 * n + 8 * j:32 * n + 8 * (j + 1)].rearrange("p c f -> p f c"),
                                           banks[0:NWIN + 1, j, 0:8 * NF].rearrange("p (f c) -> p f c", c=NF)
                                           ).then_inc(table_hi, 1)
                    act.wait_ge(s_set, 4)
                    act.wait_ge(prep_dve, 5)
                    nc.scalar.activation(V["r"][:, :], V["i1"][:, :], ACT.Sqrt).then_inc(prep_act, 1)
                    nc.scalar.activation(V["g"][:, :], V["t2"][:, :], ACT.Sigmoid).then_inc(prep_act, 1)
                    act.wait_ge(prep_dve, 8)
                    nc.scalar.activation(V["r2"][:, :], V["i2"][:, :], ACT.Sqrt).then_inc(prep_act, 1)
                    act.wait_ge(prep_pe, 8)
                    nc.scalar.activation(hid[0][:, :], banks[0:NL, 6, 0:B], ACT.Relu, bias=b1[0][:, :]
                                         ).then_inc(prep_act, 1)
                    act.wait_ge(prep_pe, 10)
                    nc.scalar.activation(hid[1][:, :], banks[0:NL, 7, 0:B], ACT.Relu, bias=b1[1][:, :]
                                         ).then_inc(prep_act, 1)

                @block.vector
                def _(dve):
                    v = nc.vector
                    dve.sem_inc(stat_done, 2)
                    steps = [0]

                    def link(ins):
                        steps[0] += 1
                        ins.then_inc(prep_chain, 1)
                        dve.wait_ge(prep_chain, steps[0])

                    def done(ins, n):
                        ins.then_inc(prep_dve, 1)
                        dve.wait_ge(prep_dve, n)

                    dve.wait_ge(s_const, NCONST[0])
                    for n in range(NG // 32):
                        for j in range(4):
                            dve.wait_ge(table_hi, 4 * n + j + 1)
                            at = slice(32 * n + 8 * j, 32 * n + 8 * (j + 1))
                            v.tensor_tensor(G[1][:, :, at].rearrange("p c f -> p f c"),
                                            banks[0:NWIN + 1, j, 0:8 * NF].rearrange("p (f c) -> p f c", c=NF),
                                            G[0][:, :, at].rearrange("p c f -> p f c"), ALU.subtract
                                            ).then_inc(table_out, 1)
                    dve.wait_ge(prep_pe, 1)
                    v.tensor_scalar(final_w[0:2 * NF, 0, :], banks[0:2 * NF, 6, 0:C], K["side0"][:, :], None, ALU.mult)
                    v.tensor_scalar(final_w[0:2 * NF, 1, :], banks[0:2 * NF, 6, 0:C], K["side1"][:, :], None, ALU.mult)
                    done(v.tensor_tensor(bias_tot[:, :], banks[:, 6, 100:101], last_b[:, :], ALU.add), 1)

                    with dve.Fori(0, B) as b:
                        with dve.Fori(0, NST // 2) as n2:
                            for par in range(2):
                                n = n2 * 2 + par
                                dve.wait_ge(x_in[par], 16 * (b * (NST // 2) + n2) + 16)
                                for r in range(SR):
                                    v.bn_stats(stats[:, b, n * SR + r, :], xs[:, par, r * W:(r + 1) * W])
                                v.tensor_reduce(cols[:, b, n, :], xs[:, par, :].rearrange("p (r w) -> p w r", w=W)
                                                [:, 0:W:W - 1, :], AX, ALU.add).then_inc(stat_done, 1)
                    dve.wait_ge(stat_done, B * NST + 2)
                    for b in range(B):
                        last = v.bn_aggr(mv[:, b, :], stats[:, b, :, :].rearrange("p n s -> p (n s)"))
                    link(last)
                    v.tensor_copy(V["mean"][:, :], mv[:, :, 0])
                    done(v.tensor_copy(V["var"][:, :], mv[:, :, 1]), 2)

                    def tt(o, a, c, op):
                        return v.tensor_tensor(V[o][:, :], V[a][:, :], V[c][:, :], op)

                    dve.wait_ge(prep_pe, 2)
                    v.tensor_copy(V["mc"][:, :], banks[:, 4, 0:B])
                    link(v.tensor_tensor(V["d"][:, :], V["mean"][:, :], banks[:, 4, 0:B], ALU.subtract))
                    link(tt("d", "d", "d", ALU.mult))
                    done(tt("e", "d", "var", ALU.add), 3)
                    dve.wait_ge(prep_pe, 3)
                    v.tensor_copy(V["M"][:, :], banks[:, 4, 16:16 + B])
                    v.tensor_copy(V["vc"][:, :], banks[:, 4, 8:8 + B])
                    link(v.tensor_tensor(V["d1"][:, :], V["mc"][:, :], banks[:, 4, 16:16 + B], ALU.subtract))
                    link(v.tensor_scalar(V["s"][:, :], V["d1"][:, :], 0.0, None, ALU.is_ge))
                    link(v.tensor_scalar(V["s"][:, :], V["s"][:, :], 2.0, -1.0, ALU.mult, ALU.add))
                    link(tt("e1", "d1", "d1", ALU.mult))
                    done(tt("e1", "e1", "vc", ALU.add), 4)
                    dve.wait_ge(prep_pe, 4)
                    link(v.tensor_scalar(V["v1"][:, :], banks[:, 4, 24:24 + B], EPS_GN, None, ALU.add))
                    link(v.reciprocal(V["i1"][:, :], V["v1"][:, :]))
                    link(v.tensor_scalar(V["t1"][:, :], banks[:, 4, 32:32 + B], gate_w[:, 0:1], None, ALU.mult))
                    link(v.scalar_tensor_tensor(V["t1"][:, :], V["s"][:, :], gate_w[:, 1:2], V["t1"][:, :],
                                                ALU.mult, ALU.add))
                    link(v.scalar_tensor_tensor(V["t1"][:, :], banks[:, 4, 40:40 + B], gate_w[:, 2:3], V["t1"][:, :],
                                                ALU.mult, ALU.add))
                    done(v.tensor_scalar(V["t2"][:, :], V["t1"][:, :], 1.0 / HW, None, ALU.mult), 5)
                    dve.wait_ge(prep_act, 2)
                    link(tt("rg", "r", "g", ALU.mult))
                    link(v.tensor_scalar(V["a"][:, :], V["rg"][:, :], 1.0, None, ALU.add))
                    link(tt("m2", "d1", "rg", ALU.mult))
                    link(tt("m2", "m2", "mc", ALU.add))
                    link(tt("a2", "a", "a", ALU.mult))
                    link(tt("v2", "a2", "vc", ALU.mult))
                    link(tt("bb", "M", "rg", ALU.mult))
                    done(v.tensor_scalar(V["bb"][:, :], V["bb"][:, :], -1.0, None, ALU.mult), 6)
                    dve.wait_ge(prep_pe, 5)
                    link(v.tensor_tensor(V["d2"][:, :], V["m2"][:, :], banks[:, 4, 48:48 + B], ALU.subtract))
                    link(v.tensor_tensor(V["bm"][:, :], V["bb"][:, :], banks[:, 4, 48:48 + B], ALU.subtract))
                    link(tt("e2", "d2", "d2", ALU.mult))
                    done(tt("e2", "e2", "v2", ALU.add), 7)
                    dve.wait_ge(prep_pe, 6)
                    link(v.tensor_scalar(V["v3"][:, :], banks[:, 4, 56:56 + B], EPS_GN, None, ALU.add))
                    done(v.reciprocal(V["i2"][:, :], V["v3"][:, :]), 8)
                    dve.wait_ge(prep_act, 3)
                    link(tt("A", "a", "r2", ALU.mult))
                    link(tt("B", "bm", "r2", ALU.mult))
                    dve.wait_ge(edge_in, 32 * B)
                    v.tensor_reduce(BS[:, 0, :], edge[:, :, :], AX, ALU.add)
                    v.tensor_copy(BS[:, 1, :], edge[:, :, 0])
                    v.tensor_copy(BS[:, 2, :], edge[:, :, W - 1])
                    v.tensor_reduce(BS[:, 3, :], cols[:, :, :, 0], AX, ALU.add)
                    v.tensor_reduce(BS[:, 4, :], cols[:, :, :, 1], AX, ALU.add)
                    link(v.tensor_copy(BS[:, 5, :], V["mc"][:, :]))
                    for q, count in enumerate((W, 1, 1, HH, HH, 1)):
                        link(v.tensor_tensor(BS[:, q, :], BS[:, q, :], V["A"][:, :], ALU.mult))
                        link(v.scalar_tensor_tensor(BS[:, q, :], V["B"][:, :], float(count), BS[:, q, :],
                                                    ALU.mult, ALU.add))
                    v.tensor_copy(BS[:, 6, :], V["A"][:, :])
                    v.tensor_copy(BS[:, 7, :], V["B"][:, :])
                    v.tensor_copy(BS[:, 8, :], V["a"][:, :])
                    done(v.tensor_copy(BS[:, 9, :], V["bb"][:, :]), 9)

                    dve.wait_ge(prep_pe, 7)
                    v.tensor_copy(H0[:, :, :], banks[0:NL, 5, 0:8 * B].rearrange("p (q b) -> p q b", b=B))
                    v.tensor_copy(H1[:, :, :], banks[0:NL, 5, 64:64 + 8 * B].rearrange("p (q b) -> p q b", b=B))
                    v.tensor_copy(AB[:, :, :], banks[0:NF + 1, 5, 128:128 + 2 * B].rearrange("p (q b) -> p q b", b=B))
                    v.tensor_copy(res_a[:, :], banks[:, 5, 192:192 + B])
                    link(v.tensor_scalar(res_c[:, :], banks[:, 5, 192 + B:192 + 2 * B], bias_tot[:, :], None, ALU.add))
                    link(v.tensor_scalar(B49[:, :], AB[:, 1, :], K["ones_row"][:, :], None, ALU.add))
                    for b in range(B):
                        last = v.tensor_scalar(Bb[:, b, :], ones49[:, :], B49[:, b:b + 1], None, ALU.mult)
                    done(last, 10)

                    link(v.tensor_tensor(CS[:, :, :], H0[:, 3:5, :], H1[:, 3:5, :], ALU.add))
                    link(v.tensor_scalar(TOT[:, :], H0[:, 5, :], float(HW), None, ALU.mult))
                    for q in range(9):
                        dy, dx = q // 3 - 1, q % 3 - 1
                        dst = ST[:, :, q]
                        link(v.tensor_copy(dst, TOT[:, :]))
                        side = H0 if dy > 0 else H1
                        if dy:
                            link(v.tensor_tensor(dst, dst, side[:, 0, :], ALU.subtract))
                        if dx:
                            link(v.tensor_tensor(dst, dst, CS[:, 0 if dx > 0 else 1, :], ALU.subtract))
                        if dx and dy:
                            link(v.tensor_tensor(dst, dst, side[:, 1 if dx > 0 else 2, :], ALU.add))
                    dve.wait_ge(s_set, 7)
                    v.tensor_scalar(in_a[:, :], AB[:, 0, :], K["ones_row"][:, :], None, ALU.add)
                    dve.wait_ge(prep_pe, 8)
                    for b in range(B):
                        link(v.tensor_scalar(bias_row[:, b, :], banks[0:NF + 1, b % 4, 0:3 * NF],
                                             K["bias_scale"][:, :], None, ALU.mult))
                        link(v.scalar_tensor_tensor(bias_row[:, b, :], hid_wb[:, :], K["w_scale"][:, :],
                                                    bias_row[:, b, :], ALU.mult, ALU.add))
                        v.tensor_copy(hid_m[0][LO:LO + NF + 1, b, :], bias_row[:, b, :])
                        link(v.tensor_copy(hid_m[0][0:NF + 1, b, :], bias_row[:, b, :]))
                        link(v.tensor_tensor(hid_m[1][0:NF + 1, b, :], bias_row[:, b, :], hid_m[0][0:NF + 1, b, :],
                                             ALU.subtract))
                    dve.wait_ge(prep_pe, 9)
                    for b in range(B):
                        link(v.tensor_tensor(KB[:, b, 0:9], banks[0:NL, 6, 16 + b:16 + 9 * B:B], b2[0][:, :], ALU.add))
                    link(v.tensor_tensor(PR[:, :, :], KB[:, :, 0:9], ST[:, :, :], ALU.mult))
                    link(v.tensor_reduce(pooled2[:, :], PR[:, :, :], AX, ALU.add))
                    done(v.tensor_scalar(pooled2s[:, :], pooled2[:, :], 1.0 / HW, None, ALU.mult), 11)
                    dve.wait_ge(prep_pe, 11)
                    for b in range(B):
                        v.tensor_tensor(KB[:, b, 9:34], banks[0:NL, 7, 16 + b:16 + 25 * B:B], b2[1][:, :], ALU.add)
                        v.tensor_copy(KB[:, b, 34:35], H0[:, 6, b:b + 1])
                        last = v.tensor_copy(KB[:, b, 35:36], H0[:, 7, b:b + 1])
                    done(last, 12)
                    dve.wait_ge(prep_pe, 12)
                    for c in range(NL):
                        v.tensor_copy(local_k[:, c:B * NL:NL, :], banks[:, c // 3 % 6, c % 3 * B * SETK:(c % 3 + 1) * B * SETK]
                                      .rearrange("p (b q) -> p b q", q=SETK))

        with ExitStack() as st:
            def sb3(name, shape):
                return st.enter_context(nc.sbuf_tensor(name, shape, F32))

            def sem3(name):
                return st.enter_context(nc.semaphore(name))

            xl = sb3("xl", [128, 2, W])
            zl = sb3("zl", [128, 2, W + 2])
            y1 = sb3("y1", [128, 2, W + 4])
            y2 = sb3("y2", [128, 2, W])
            taps = sb3("taps", [128, 2, SETK])
            T3 = sb3("T3", [128, 2, 3, 132])
            T5 = sb3("T5", [128, 2, 5, 132])
            l_set = sem3("local_pads_zero")
            l_in = [sem3(f"local_x{n}_in") for n in (0, 1)]
            l_z = sem3("local_z")
            l_p1 = sem3("local_3x3_products")
            l_y1 = sem3("local_y1")
            l_p2 = sem3("local_5x5_products")
            l_y2 = sem3("local_y2")
            l_st = [sem3(f"local_y2_{n}_stored") for n in (0, 1)]
            l_T = sem3("local_matrices")
            l_chain = sem3("local_matrix_steps")
            NSTEP = 2 * NB
            LAG = min(4, NSTEP)

            with nc.Block() as block:
                def cells():
                    return [(n, n // NB, n % NB) for n in range(NSTEP)]

                def store_local(sp, k, n, b, c2):
                    ch, bd = n // NB, n % NB
                    r0, r1 = BANDS[bd][0]
                    sp.wait_ge(l_y2, k * NSTEP + n + 3)
                    sp.sem_inc(sp_passed, 1)
                    sp.dma_start(scratch[b, c2 * 2 + ch, r0:r1, :], y2[0:r1 - r0, n % 2, :]
                                 ).then_inc(l_st[n % 2], 16)

                @block.sync
                def _(sp):
                    sp.sem_inc(l_st[0], 1)
                    sp.sem_inc(l_st[1], 1)
                    with sp.Fori(0, B) as b:
                        with sp.Fori(0, NL // 2) as c2:
                            k = b * (NL // 2) + c2
                            for n, ch, bd in cells():
                                z0, z1 = BANDS[bd][2]
                                sp.wait_ge(l_z, k * NSTEP + n + 1)
                                sp.sem_inc(sp_passed, 1)
                                sp.dma_start(xl[0:z1 - z0, n % 2, :], x[b, c2 * 2 + ch, z0:z1, :]
                                             ).then_inc(l_in[n % 2], 16)
                                if n >= LAG:
                                    store_local(sp, k, n - LAG, b, c2)
                            for n in range(NSTEP - LAG, NSTEP):
                                store_local(sp, k, n, b, c2)
                    for n in (0, 1):
                        sp.wait_ge(l_st[n], 1 + 16 * (B * NL // 2) * NB)

                def y1_out(act, k, n):
                    a0, a1 = BANDS[n % NB][1]
                    act.wait_ge(l_p1, k * NSTEP + n + 3)
                    act.wait_ge(l_p2, k * NSTEP + n + 1)
                    nc.scalar.copy(y1[0:a1 - a0, n % 2, 2:W + 2], banks[0:a1 - a0, n % 2, :]).then_inc(l_y1, 1)

                @block.scalar
                def _(act):
                    act.sem_inc(l_z, 2)
                    act.sem_inc(l_y1, 2)
                    act.wait_ge(l_set, 2)
                    with act.Fori(0, B) as b:
                        with act.Fori(0, NL // 2) as c2:
                            k = b * (NL // 2) + c2
                            for n, ch, bd in cells():
                                z0, z1 = BANDS[bd][2]
                                act.wait_ge(l_in[n % 2], 16 * (k * NB + n // 2 + 1))
                                act.wait_ge(l_p1, k * NSTEP + n + 1)
                                act.wait_ge(l_T, 2 * k + ch + 1)
                                nc.scalar.activation(zl[0:z1 - z0, n % 2, 1:W + 1], xl[0:z1 - z0, n % 2, :],
                                                     ACT.Identity, bias=taps[0:z1 - z0, ch, 35:36],
                                                     scale=taps[0:z1 - z0, ch, 34:35]).then_inc(l_z, 1)
                                if n >= 1:
                                    y1_out(act, k, n - 1)
                            y1_out(act, k, NSTEP - 1)

                @block.tensor
                def _(pe):
                    pe.sem_inc(l_p1, 2)
                    pe.sem_inc(l_p2, 2)
                    pe.wait_ge(l_set, 2)

                    def three(k, n):
                        ch, bd = n // NB, n % NB
                        (r0, r1), (a0, a1), (z0, z1) = BANDS[bd]
                        pe.wait_ge(l_z, k * NSTEP + n + 3)
                        pe.wait_ge(l_y1, k * NSTEP + n + 1)
                        off = a0 - z0
                        for dx in range(3):
                            last = nc.tensor.matmul(banks[0:a1 - a0, n % 2, :],
                                                    T3[0:z1 - z0, ch, dx, off:off + a1 - a0],
                                                    zl[0:z1 - z0, n % 2, dx:dx + W], start=dx == 0, stop=dx == 2)
                        last.then_inc(l_p1, 1)

                    def five(k, n):
                        ch, bd = n // NB, n % NB
                        (r0, r1), (a0, a1), (z0, z1) = BANDS[bd]
                        pe.wait_ge(l_y1, k * NSTEP + n + 3)
                        pe.wait_ge(l_y2, k * NSTEP + n + 1)
                        off = r0 - a0
                        for dx in range(5):
                            last = nc.tensor.matmul(banks[0:r1 - r0, 2 + n % 2, :],
                                                    T5[0:a1 - a0, ch, dx, off:off + r1 - r0],
                                                    y1[0:a1 - a0, n % 2, dx:dx + W], start=dx == 0, stop=dx == 4)
                        last.then_inc(l_p2, 1)

                    with pe.Fori(0, B) as b:
                        with pe.Fori(0, NL // 2) as c2:
                            k = b * (NL // 2) + c2
                            for n in range(NSTEP):
                                if n % NB == 0:
                                    pe.wait_ge(l_T, 2 * k + n // NB + 1)
                                three(k, n)
                                if n:
                                    five(k, n - 1)
                            five(k, NSTEP - 1)

                @block.vector
                def _(dve):
                    v = nc.vector
                    for n in (0, 1):
                        v.memset(zl[:, n, :], 0.0)
                        last = v.memset(y1[:, n, :], 0.0)
                    last.then_inc(l_set, 2)
                    dve.sem_inc(l_y2, 2)
                    dve.sem_inc(l_chain, 1)

                    def matrices(cell, ch):
                        base = cell * 34 + 1
                        v.tensor_copy(taps[:, ch, :], local_k[:, bass.ds(cell, 1), :]
                                      .rearrange("p a q -> p (a q)")).then_inc(l_chain, 1)
                        dve.wait_ge(l_chain, base + 1)
                        n = 1
                        for T, side, first in ((T3, 3, 0), (T5, 5, 9)):
                            for ky in range(side):
                                if ky:
                                    dve.wait_ge(l_chain, base + n)
                                for dx in range(side):
                                    s = 3 + ky - side // 2
                                    tap = taps[:, ch, first + ky * side + dx:first + ky * side + dx + 1]
                                    diagonal = K["diagonals"][:, s:s + 132]
                                    if ky == 0:
                                        i = v.tensor_scalar(T[:, ch, dx, :], diagonal, tap, None, ALU.mult)
                                    else:
                                        i = v.scalar_tensor_tensor(T[:, ch, dx, :], diagonal, tap, T[:, ch, dx, :],
                                                                   ALU.mult, ALU.add)
                                    n += 1
                                    i.then_inc(l_T if n == 35 else l_chain, 1)
                                if n in (10, 20, 30):
                                    yield

                    def y2_out(k, n):
                        r0, r1 = BANDS[n % NB][0]
                        dve.wait_ge(l_p2, k * NSTEP + n + 3)
                        dve.wait_ge(l_st[n % 2], 16 * (k * NB + n // 2) + 1)
                        v.tensor_copy(y2[0:r1 - r0, n % 2, :], banks[0:r1 - r0, 2 + n % 2, :]).then_inc(l_y2, 1)

                    for _part in matrices(0, 0):
                        pass
                    with dve.Fori(0, B * NL // 2) as k:
                        for ch in range(2):
                            parts = matrices(2 * k + ch + 1, 1 - ch)
                            for n in range(ch * NB, (ch + 1) * NB):
                                next(parts, None)
                                if n == (ch + 1) * NB - 1:
                                    for _part in parts:
                                        pass
                                y2_out(k, n)

        early.close()

        band = sb("band", [NF + 1, WIN, W + 2])
        wins = sb("wins", [128, (W + 2) * WIN + 128 - NWIN], F16)
        hidden = [sb(f"hidden_{part}", [NWIN + 1, 3 * NF, PW], F16) for part in ("hi", "lo")]
        prod = sb("prod", [NSPEC, NPAIR, 2, NF])
        vpix = sb("vpix", [PX, NPAIR, 2, NF])
        kspec = sb("kspec", [NSPEC, 2, QKB * PW])
        osb = sb("osb", [128, 512])
        sq = sb("sq", [128, 512])
        rstd = sb("rstd", [2 * NF, 512])
        normed = sb("normed", [2 * NF, 512])
        mixed = sb("mixed", [128, PS, HWID])
        xa = sb("xa", [128, PS, HWID])
        ot = sb("ot", [128, PS, HWID])
        hid_cur = [sb(f"hid_cur_{part}", [128, 3 * NF], F16) for part in ("hi", "lo")]
        in_a_cur = sb("in_a_cur", [NF + 1, 1])
        a_cur = sb("a_cur", [128, 1])
        c_cur = sb("c_cur", [128, 1])

        m_set = sem("main_tiles_set")
        band_in = sem("band_in")
        pool_passed = sem("pool_passed_its_waits")
        edge_rows_in = sem("edge_rows_of_band_in")
        cur_set = sem("batch_coefficients_set")
        wins_hi = sem("windows_high_parts")
        wins_lo = sem("windows_low_parts")
        s1_mm = sem("s1_products")
        s1_act = sem("hidden_high_parts")
        s1_dve = sem("hidden_low_parts")
        qk_mm = sem("qk_products")
        qk_act = sem("k_spectra_copied")
        qk_dve = sem("spectral_products")
        v_mm = sem("v_products")
        v_act = sem("v_copied")
        o_mm = sem("inverse_dft")
        o_act = sem("inverse_dft_copied")
        oc_mm = sem("centered")
        sq_act = sem("squared")
        var_mm = sem("variance")
        ln_act = sem("variance_log")
        r_act = sem("rstd_ready")
        vt_mm = sem("v_transposed")
        t_dve = sem("normed_ready")
        y_dve = sem("mixed_ready")
        fin_mm = sem("final_products")
        fin_dve = sem("final_sums")
        xr_in = sem("residual_x_in")
        y2_in = sem("local_branch_in")
        xa_done = sem("residual_scaled")
        stored = sem("output_stored")

        BO, BOC, BVAR, BVT = 4, 5, 6, 7

        def after(eng, s, count):
            eng.wait_ge(s, count + 1)

        def rows_of_batch(eng, b, row):
            k0 = b * NPR
            row(k0, None, True)
            with eng.Fori(1, NPR - 1) as j:
                row(k0 + j, k0 + j - 1, True)
            row(k0 + (NPR - 1), k0 + (NPR - 2), False)
            row(None, k0 + (NPR - 1), False)

        def window_part(i):
            return i * (W // 4), (i + 1) * (W // 4) + (2 if i == 3 else 0)

        PART_BEHIND = {4: 0, 8: 1, 12: 2, 15: 3}

        with nc.Block() as block:
            @block.gpsimd
            def _(pool):
                nc.gpsimd.memset(band[:, :, :], 1.0).then_inc(m_set, 1)
                nc.gpsimd.memset(hidden[0][:, :, :], 1.0).then_inc(m_set, 1)
                nc.gpsimd.memset(hidden[1][:, :, :], 0.0).then_inc(m_set, 1)
                nc.gpsimd.memset(wins[:, :], 0.0).then_inc(m_set, 1)
                nc.gpsimd.memset(osb[:, :], 0.0).then_inc(m_set, 1)
                nc.gpsimd.memset(sq[:, :], 0.0).then_inc(m_set, 1)
                pool.wait_ge(m_set, 6)
                nc.gpsimd.memset(band[:, :, 0:1], 0.0).then_inc(m_set, 1)
                nc.gpsimd.memset(band[:, :, W + 1:W + 2], 0.0).then_inc(m_set, 1)
                pool.sem_inc(xa_done, 1)
                with pool.Fori(0, B) as b:
                    pool.wait_ge(cur_set, b + 1)
                    pool.sem_inc(pool_passed, 1)
                    with pool.Fori(0, NPR) as j:
                        k = b * NPR + j
                        after(pool, xr_in, 32 * (k + 1))
                        pool.sem_inc(pool_passed, 1)
                        nc.gpsimd.tensor_scalar(xa[:, :, :], xa[:, :, :], a_cur[:, :], c_cur[:, :],
                                                ALU.mult, ALU.add).then_inc(xa_done, 1)

            @block.sync
            def _(sp):
                for s in (xr_in, y2_in, stored):
                    sp.sem_inc(s, 1)
                sp.sem_inc(band_in, 1)
                sp.wait_ge(m_set, 8)

                def load_band(b, k, j, y0, n, at):
                    sp.dma_start(band[0:NF, at:at + n, 1:W + 1], x[b, NL:C, bass.ds(y0, n), :]
                                 ).then_inc(band_in, 16)

                def set_row(r, source):
                    if source == "zeros":
                        sp.dma_start(band[:, r, 1:W + 1], t["zeros"][:, :]).then_inc(edge_rows_in, 16)
                    else:
                        sp.dma_start(band[NF:NF + 1, r, 1:W + 1], t["ones"][:, :]).then_inc(edge_rows_in, 16)

                def load_rest(b, k, j):
                    after(sp, fin_dve, 4 * k)
                    sp.sem_inc(sp_passed, 1)
                    after(sp, fin_mm, 4 * k)
                    sp.sem_inc(sp_passed, 1)
                    for s in range(2):
                        sp.dma_start(xa[C * s:C * (s + 1), :, :],
                                     x[b, :, bass.ds(j * PS, PS), HWID * s:HWID * (s + 1)]).then_inc(xr_in, 16)
                        p = 2 * NF + NL * s
                        sp.dma_start(mixed[p:p + NL, :, :],
                                     scratch[b, :, bass.ds(j * PS, PS), HWID * s:HWID * (s + 1)]).then_inc(y2_in, 16)

                def store(b, k, j):
                    after(sp, fin_dve, 4 * (k + 1))
                    sp.sem_inc(sp_passed, 1)
                    for s in range(2):
                        sp.dma_start(out[b, :, bass.ds(j * PS, PS), HWID * s:HWID * (s + 1)],
                                     ot[C * s:C * (s + 1), :, :]).then_inc(stored, 16)

                def band_free(k):
                    after(sp, wins_lo, 4 * k)
                    sp.sem_inc(sp_passed, 1)

                with sp.Fori(0, B) as b:
                    k0 = b * NPR
                    band_free(k0)
                    set_row(0, "zeros")
                    set_row(WIN - 1, "ones")
                    sp.wait_ge(edge_rows_in, 64 * b + 32)
                    load_band(b, k0, 0, 0, PS + 1, 1)
                    band_free(k0 + 1)
                    set_row(0, "ones")
                    sp.wait_ge(edge_rows_in, 64 * b + 48)
                    load_band(b, k0 + 1, 1, PS - 1, WIN, 0)
                    band_free(k0 + 2)
                    load_band(b, k0 + 2, 2, 2 * PS - 1, WIN, 0)
                    load_rest(b, k0, 0)
                    with sp.Fori(3, NPR - 1) as j:
                        band_free(k0 + j)
                        load_band(b, k0 + j, j, j * PS - 1, WIN, 0)
                        store(b, k0 + j - 3, j - 3)
                        load_rest(b, k0 + j - 2, j - 2)
                    j = NPR - 1
                    band_free(k0 + j)
                    set_row(WIN - 1, "zeros")
                    sp.wait_ge(edge_rows_in, 64 * b + 64)
                    load_band(b, k0 + j, j, j * PS - 1, WIN - 1, 0)
                    for j in range(NPR - 3, NPR):
                        store(b, k0 + j - 1, j - 1)
                        load_rest(b, k0 + j, j)
                    store(b, k0 + NPR - 1, NPR - 1)
                sp.wait_ge(stored, 32 * B * NPR + 1)

            @block.tensor
            def _(pe):
                for s in (s1_mm, qk_mm, v_mm, o_mm, oc_mm, var_mm, vt_mm, fin_mm):
                    pe.sem_inc(s, 1)
                pe.wait_ge(m_set, 8)

                def s1(k, m):
                    if m == 0:
                        after(pe, v_act, 3 * k)
                    elif m >= 2:
                        after(pe, s1_dve, 16 * k + m - 1)
                    after(pe, wins_lo, 4 * k + min(m // 4 + 1 + (m % 4 == 3), 4))
                    for i in range(4):
                        x0 = (4 * m + i) * PS
                        for part in range(2):
                            last = nc.tensor.matmul(banks[:, m % 2 * 2 + i // 2, i % 2 * 3 * NF:(i % 2 + 1) * 3 * NF],
                                                    wins[:, x0 * WIN:x0 * WIN + 128], hid_cur[part][:, :],
                                                    start=part == 0, stop=part == 1)
                    last.then_inc(s1_mm, 1)

                def split_product(to, ch, columns, o):
                    for n, (g, h) in enumerate(((0, 1), (0, 0), (1, 0))):
                        last = nc.tensor.matmul(to, G[g][:, ch, columns], hidden[h][:, o, :], start=n == 0, stop=n == 2)
                    return last

                def s2_qk(k, q):
                    if q == 0:
                        after(pe, s1_dve, 16 * k + 16)
                    elif q >= 2:
                        after(pe, qk_dve, 6 * k + q - 1)
                    for part in range(2):
                        for c in range(QKB):
                            ch = q * QKB + c
                            last = split_product(banks[:, q % 2 * 2 + part, c * PW:(c + 1) * PW], ch,
                                                 slice(part * NSPEC, (part + 1) * NSPEC), part * NF + ch)
                    last.then_inc(qk_mm, 1)

                def s2_v(k, r):
                    if r < 2:
                        after(pe, qk_dve, 6 * k + 5 + r)
                    else:
                        after(pe, v_act, 3 * k + 1)
                    for c in range(VB):
                        ch = r * VB + c
                        last = split_product(banks[0:PX, r % 2 * 2 + c // 8, c % 8 * PW:(c % 8 + 1) * PW], ch,
                                             slice(2 * NSPEC, NG), 2 * NF + ch)
                    last.then_inc(v_mm, 1)

                def chunk_out(bank, i):
                    return banks[0:2 * NF, bank, :].rearrange("p (y i x) -> p y i x", y=PS, i=8)[:, :, i, :]

                def norm_step(k, m):
                    c, step = m // 4, m % 4
                    if step == 0:
                        if c == 0:
                            after(pe, fin_dve, 4 * k)
                        after(pe, o_act, 4 * k + c)
                        for i in range(8):
                            last = nc.tensor.matmul(chunk_out(BO, i),
                                                    prod[:, 8 * c + i, :, :].rearrange("p s c -> p (s c)"),
                                                    K["inverse"][:, :].rearrange("p (y x) -> p y x", y=PS),
                                                    start=True, stop=True)
                        last.then_inc(o_mm, 1)
                    elif step == 1:
                        after(pe, o_act, 4 * k + c + 1)
                        after(pe, t_dve, 4 * k + c)
                        nc.tensor.matmul(banks[:, BOC, :], K["center"][:, :], osb[:, :],
                                         start=True, stop=True).then_inc(oc_mm, 1)
                    elif step == 2:
                        after(pe, sq_act, 4 * k + c + 1)
                        after(pe, ln_act, 4 * k + c)
                        after(pe, y_dve, 4 * k + c)
                        nc.tensor.matmul(banks[:, BVAR, :], K["chan_avg"][:, :], sq[:, :],
                                         start=True, stop=True).then_inc(var_mm, 1)
                        for i in range(8):
                            last = nc.tensor.transpose(chunk_out(BVT, i),
                                                       vpix[:, 8 * c + i, :, :].rearrange("p s c -> p (s c)"),
                                                       K["identity"][:, :].rearrange("p (y x) -> p y x", y=PS))
                        last.then_inc(vt_mm, 1)

                def final(k, f):
                    if f == 0:
                        after(pe, y_dve, 4 * k + 4)
                        after(pe, y2_in, 32 * (k + 1))
                        after(pe, ln_act, 4 * k + 4)
                    elif f >= 2:
                        after(pe, fin_dve, 4 * k + f - 1)
                    nc.tensor.matmul(banks[:, BO if f % 2 == 0 else BVAR, :],
                                     final_w[:, :, :].rearrange("p s c -> p (s c)"),
                                     mixed[:, f * RPG:(f + 1) * RPG, :].rearrange("p r x -> p (r x)"),
                                     start=True, stop=True).then_inc(fin_mm, 1)

                def row(k, kl, following):
                    for m in range(NS1):
                        if k is not None:
                            s1(k, m)
                        if kl is not None:
                            norm_step(kl, m)
                    for q in range(NQK):
                        if k is not None:
                            s2_qk(k, q)
                        if kl is not None and 1 <= q <= NRG:
                            final(kl, q - 1)
                    for r in range(NV):
                        if k is not None:
                            s2_v(k, r)

                with pe.Fori(0, B) as b:
                    pe.wait_ge(cur_set, b + 1)
                    rows_of_batch(pe, b, row)

            def hidden_at(part, m):
                return hidden[part][0:NWIN, :, 4 * m:4 * m + 4].rearrange("p o (b t) -> p b t o", b=2)

            def hidden_from(m):
                return banks[0:NWIN, m % 2 * 2:m % 2 * 2 + 2, 0:6 * NF].rearrange("p b (t o) -> p b t o", t=2)

            def window_at(p, lo, hi):
                return wins[p:p + NF + 1, lo * WIN:hi * WIN].rearrange("p (x y) -> p x y", y=WIN)

            @block.scalar
            def _(act):
                nc.scalar.preload_act_table_set("natural_log_exp_and_others")
                for s in (wins_hi, s1_act, qk_act, v_act, o_act, sq_act, ln_act, r_act):
                    act.sem_inc(s, 1)

                def window_hi(k, i):
                    if i == 0:
                        after(act, band_in, 16 * (k + 1))
                    lo, hi = window_part(i)
                    nc.scalar.activation(window_at(0, lo, hi), band[:, :, lo:hi].rearrange("p y x -> p x y"),
                                         ACT.Copy, scale=in_a_cur[:, :]).then_inc(wins_hi, 1)

                def norm_step(k, m):
                    c, step = m // 4, m % 4
                    if step == 0:
                        after(act, o_mm, 4 * k + c + 1)
                        nc.scalar.copy(osb[0:2 * NF, :], banks[0:2 * NF, BO, :]).then_inc(o_act, 1)
                    elif step == 1:
                        after(act, oc_mm, 4 * k + c + 1)
                        nc.scalar.activation(sq[0:2 * NF, :], banks[0:2 * NF, BOC, :], ACT.Square).then_inc(sq_act, 1)
                    elif step == 2:
                        after(act, var_mm, 4 * k + c + 1)
                        after(act, t_dve, 4 * k + c)
                        nc.scalar.activation(rstd[:, :], banks[0:2 * NF, BVAR, :], ACT.Ln, bias=eps_ln[0:2 * NF, :]
                                             ).then_inc(ln_act, 1)
                        after(act, ln_act, 4 * k + c + 1)
                        nc.scalar.activation(rstd[:, :], rstd[:, :], ACT.Exp, scale=-0.5).then_inc(r_act, 1)

                def row(k, kl, following):
                    for m in range(NS1):
                        if k is not None:
                            after(act, s1_mm, 16 * k + m + 1)
                            nc.scalar.activation(hidden_at(0, m), hidden_from(m), ACT.Copy, scale=1 / HID_SCALE
                                                 ).then_inc(s1_act, 1)
                        if following and m in PART_BEHIND:
                            window_hi(k + 1, PART_BEHIND[m])
                        if kl is not None:
                            norm_step(kl, m)
                    if k is None:
                        return
                    for q in range(NQK):
                        after(act, qk_mm, 6 * k + q + 1)
                        after(act, qk_dve, 6 * k + max(q - 1, 0))
                        nc.scalar.copy(kspec[:, q % 2, :], banks[:, q % 2 * 2 + 1, :]).then_inc(qk_act, 1)
                    for r in range(NV):
                        after(act, v_mm, 3 * k + r + 1)
                        nc.scalar.activation(vpix[:, :, :, r * VB:(r + 1) * VB].rearrange("p i s c -> p c s i"),
                                             banks[0:PX, r % 2 * 2:r % 2 * 2 + 2, :]
                                             .rearrange("p b (c s i) -> p (b c) s i", s=2, i=NPAIR),
                                             ACT.Copy, scale=1 / SPEC_SCALE).then_inc(v_act, 1)

                act.wait_ge(m_set, 8)
                with act.Fori(0, B) as b:
                    act.wait_ge(cur_set, b + 1)
                    for i in range(4):
                        window_hi(b * NPR, i)
                    rows_of_batch(act, b, row)

            @block.vector
            def _(dve):
                v = nc.vector
                for s in (wins_lo, s1_dve, qk_dve, t_dve, y_dve, fin_dve):
                    dve.sem_inc(s, 1)

                def window_lo(k, i):
                    after(dve, wins_hi, 4 * k + i + 1)
                    lo, hi = window_part(i)
                    v.scalar_tensor_tensor(window_at(LO, lo, hi), band[:, :, lo:hi].rearrange("p y x -> p x y"),
                                           in_a_cur[:, :], window_at(0, lo, hi), ALU.mult, ALU.subtract
                                           ).then_inc(wins_lo, 1)

                def norm(k, c):
                    after(dve, r_act, 4 * k + c + 1)
                    v.scalar_tensor_tensor(normed[:, :], banks[0:2 * NF, BOC, :], ln_w[:, :], rstd[:, :],
                                           ALU.mult, ALU.mult).then_inc(t_dve, 1)
                    after(dve, t_dve, 4 * k + c + 1)
                    after(dve, vt_mm, 4 * k + c + 1)
                    v.scalar_tensor_tensor(mixed[0:2 * NF, :, 64 * c:64 * (c + 1)],
                                           normed[:, :].rearrange("p (y x) -> p y x", y=PS), ln_b[:, :],
                                           banks[0:2 * NF, BVT, :].rearrange("p (y x) -> p y x", y=PS),
                                           ALU.add, ALU.mult).then_inc(y_dve, 1)

                def final(k, f):
                    if f == 0:
                        after(dve, xa_done, k + 1)
                        after(dve, stored, 32 * k)
                    after(dve, fin_mm, 4 * k + f + 1)
                    rows = slice(f * RPG, (f + 1) * RPG)
                    v.tensor_tensor(ot[:, rows, :], banks[:, BO if f % 2 == 0 else BVAR, :]
                                    .rearrange("p (r x) -> p r x", r=RPG), xa[:, rows, :], ALU.add).then_inc(fin_dve, 1)

                def row(k, kl, following):
                    for m in range(NS1):
                        if k is not None:
                            after(dve, s1_act, 16 * k + m + 1)
                            v.scalar_tensor_tensor(hidden_at(1, m), hidden_from(m), 1 / HID_SCALE, hidden_at(0, m),
                                                   ALU.mult, ALU.subtract).then_inc(s1_dve, 1)
                        if following and m in PART_BEHIND:
                            window_lo(k + 1, PART_BEHIND[m])
                        if kl is not None and m % 4 == 3:
                            norm(kl, m // 4)
                    for q in range(NQK):
                        if k is not None:
                            after(dve, qk_mm, 6 * k + q + 1)
                            after(dve, qk_act, 6 * k + q + 1)
                            v.tensor_tensor(prod[:, :, :, q * QKB:(q + 1) * QKB].rearrange("p i s c -> p c s i"),
                                            banks[:, q % 2 * 2, :].rearrange("p (c s i) -> p c s i", s=2, i=NPAIR),
                                            kspec[:, q % 2, :].rearrange("p (c s i) -> p c s i", s=2, i=NPAIR),
                                            ALU.mult).then_inc(qk_dve, 1)
                        if kl is not None and 1 <= q <= NRG:
                            final(kl, q - 1)

                dve.wait_ge(m_set, 8)
                with dve.Fori(0, B) as b:
                    for part in range(2):
                        v.tensor_copy(hid_cur[part][:, :], hid_m[part][:, bass.ds(b, 1), :].rearrange("p b o -> p (b o)"))
                    v.tensor_copy(in_a_cur[:, :], in_a[:, bass.ds(b, 1)])
                    v.tensor_copy(a_cur[:, :], res_a[:, bass.ds(b, 1)])
                    v.tensor_copy(c_cur[:, :], res_c[:, bass.ds(b, 1)]).then_inc(cur_set, 1)
                    for i in range(4):
                        window_lo(b * NPR, i)
                    rows_of_batch(dve, b, row)


def kernel(**inputs):
    import numpy as _np
    import concourse.bacc as _bacc
    from concourse import mybir as _mybir
    from concourse.bass_utils import run_bass_kernel_spmd as _run

    def a(name):
        return _np.asarray(inputs[name])

    def twice(v):
        return _np.concatenate([v, v]).reshape(-1, 1)

    table, inverse = dft_tables()
    arrays = dict(shape_constants())
    arrays["inverse"] = inverse
    arrays["dft"] = table.reshape(NG // 32, 10, 32 * (NWIN + 1))
    B, _, H, W = a("x").shape
    arrays["zeros"] = _np.zeros((NF + 1, W), _np.float32)
    arrays["ones"] = _np.ones((1, W), _np.float32)
    arrays["x"] = a("x")
    arrays["gate_w"] = _np.broadcast_to(a("L0_conv_w").reshape(1, 3), (128, 3))
    for n, side in ((1, 3), (2, 5)):
        pre = f"L1_conv_dl{n}_"
        arrays[f"mlp{n}_w1T"] = a(pre + "w1").T
        arrays[f"mlp{n}_b1"] = a(pre + "b1").reshape(NL, 1)
        arrays[f"mlp{n}_w2T"] = a(pre + "w2").reshape(NL, side * side, NL).transpose(2, 1, 0)
        arrays[f"mlp{n}_b2"] = a(pre + "b2").reshape(NL, side * side)
    arrays["hid_wb"] = _np.concatenate([a("L1_conv_fs_hid_w").T, a("L1_conv_fs_hid_b")[None]])
    arrays["dw_wb"] = _np.concatenate([a("L1_conv_fs_dw_w").reshape(3 * NF, 9).T, a("L1_conv_fs_dw_b")[None]])
    arrays["ln_w"] = twice(a("L1_conv_fs_ln_w"))
    arrays["ln_b"] = twice(a("L1_conv_fs_ln_b"))
    arrays["out_w"] = a("L1_conv_fs_out_w")
    arrays["out_b"] = a("L1_conv_fs_out_b").reshape(NF, 1)
    arrays["last_wT"] = a("L1_conv_last_w").T
    arrays["last_b"] = twice(a("L1_conv_last_b"))
    arrays = {n: _np.ascontiguousarray(v) for n, v in arrays.items()}

    nc = _bacc.Bacc("TRN2", target_bir_lowering=False, num_devices=1)
    f32 = _mybir.dt.float32
    t = {n: nc.dram_tensor(f"in_{n}_dram", v.shape, f32, kind="ExternalInput").ap() for n, v in arrays.items()}
    t["out"] = nc.dram_tensor("out_0_dram", (B, C, H, W), f32, kind="ExternalOutput").ap()
    t["local_scratch"] = nc.dram_tensor("local_scratch", (B, NL, H, W), f32, kind="Internal").ap()
    program(nc, t)
    r = _run(nc, [{f"in_{n}_dram": v for n, v in arrays.items()}], core_ids=[0])
    return r.results[0]["out_0_dram"]
```

```python
from contextlib import ExitStack

import numpy as np

import concourse.bass as bass
from concourse import mybir

F32 = mybir.dt.float32
F16 = mybir.dt.float16
ALU = mybir.AluOpType
ACT = mybir.ActivationFunctionType
AX = mybir.AxisListType.X

C = 64
NL = 16
NF = C - NL
PS = 8
WIN = PS + 2
NWIN = WIN * WIN
PX = PS * PS
NSPEC = 128
NG = 2 * NSPEC + PX
HID_SCALE = 64.0
SPEC_SCALE = 8.0
TAP_SCALE = 64.0
LO = 64
SETK = 9 + 25 + 2
LB_ROWS = 122
EPS_GN = 1e-5
EPS_LN = 1e-6
QKB = 8
VB = 16


def spectral_rows():
    rows = []
    seen = set()
    for u in range(PS):
        for v in range(PS):
            other = ((-u) % PS, (-v) % PS)
            if other in seen:
                continue
            seen.add((u, v))
            own = other == (u, v)
            rows.append((u, v, 1.0 if own else 2.0, "re", "re"))
            if not own:
                rows += [(u, v, 2.0, "im", "im"), (u, v, 2.0, "re", "im"), (u, v, 2.0, "im", "re")]
    return rows


def dft_tables():
    rows = spectral_rows()
    y, x = np.meshgrid(np.arange(PS), np.arange(PS), indexing="ij")
    E = np.zeros((10, NG, NWIN + 1))
    inverse = np.zeros((NSPEC, PX))
    for n, (u, v, weight, pq, pk) in enumerate(rows):
        angle = 2 * np.pi * ((u * y + v * x) % PS) / PS
        part = {"re": np.cos(angle), "im": -np.sin(angle)}
        for base, p in ((0, pq), (NSPEC, pk)):
            for t in range(9):
                window = np.zeros((WIN, WIN))
                window[t // 3:t // 3 + PS, t % 3:t % 3 + PS] = part[p]
                E[t, base + n, :NWIN] = window.T.ravel()
            E[9, base + n, NWIN] = part[p].sum()
        if pq == pk:
            inverse[n] = (weight * (1 if pq == "re" else -1) * np.cos(angle) / PX).ravel()
        else:
            inverse[n] = (-weight * np.sin(angle) / PX).ravel()
    for p in range(PX):
        for t in range(9):
            E[t, 2 * NSPEC + p, (p % PS + t % 3) * WIN + p // PS + t // 3] = 1.0
        E[9, 2 * NSPEC + p, NWIN] = 1.0
    E *= SPEC_SCALE
    inverse /= SPEC_SCALE * SPEC_SCALE
    chunks = E.reshape(10, NG // 32, 32, NWIN + 1).transpose(1, 0, 2, 3)
    return np.ascontiguousarray(chunks, np.float32), inverse.astype(np.float32)


def shape_constants():
    p = np.arange(128)
    k = {}
    k["pair_avg"] = (p[:, None] // 2 == p // 2) / 2
    k["quad_avg"] = (p[:, None] // 4 == p // 4) / 4
    k["from_prev"] = (p[:, None] == p - 2)
    k["from_next"] = (p[:, None] == p + 2)
    for h in range(2):
        k[f"pick_half{h}"] = (p[:, None] == 2 * np.arange(NL) + h)
    k["pick_freq"] = (p[:, None] == 2 * (NL + np.arange(NF + 1))) & (np.arange(NF + 1) < NF)
    k["pick_out"] = (p[:, None] == 2 * (p % C))
    m = np.arange(2 * NF)
    same = (m[:, None] // NF == m // NF) / NF
    k["chan_avg"] = np.pad(same, (0, 128 - 2 * NF))
    k["w_scale"] = HID_SCALE * (np.arange(NF + 1) < NF)[:, None]
    k["bias_scale"] = HID_SCALE * (np.arange(NF + 1) == NF)[:, None]
    k["side0"] = (m < NF)[:, None]
    k["side1"] = (m >= NF)[:, None]
    k["identity"] = np.eye(PX)
    k["ones_row"] = (np.arange(NF + 1) == NF)[:, None]
    k["diagonals"] = TAP_SCALE * (np.arange(138) == p[:, None] + 3)
    k["spread"] = np.repeat(np.eye(NL), 128, axis=1)
    return {n: np.ascontiguousarray(v, np.float32) for n, v in k.items()}


def bands(H):
    out = []
    n = -(-H // LB_ROWS)
    for i in range(n):
        r0, r1 = i * H // n, (i + 1) * H // n
        y0, y1 = max(0, r0 - 2), min(H, r1 + 2)
        z0, z1 = max(0, y0 - 1), min(H, y1 + 1)
        out.append(((r0, r1), (y0, y1), (z0, z1)))
    return out


def program(nc, t):
    x, out, scratch = t["x"], t["out"], t["local_scratch"]
    B, _, H, W = x.shape
    HW = H * W
    HH = H // 2
    NPR = H // PS
    PW = W // PS
    NPAIR = PW // 2
    SR = 8
    NST = HH // SR
    NTAB = NG // 32
    PER = B * NST // 2 // (4 * NTAB)
    NCH = NPAIR // 8
    NS1 = PW // 4
    NWP = 8
    GPW = NS1 // NWP
    NQK, NV = NF // QKB, NF // VB
    HWID = W // 2
    NRG = PS * HWID // 512
    RPG = PS // NRG
    BANDS = bands(H)
    NB = len(BANDS)
    assert W == 512 and NPAIR % 8 == 0 and NST % 2 == 0 and NS1 == 16 and NRG == 4

    ctx = ExitStack()
    with ctx:
        def sb(name, shape, dt=F32):
            return ctx.enter_context(nc.sbuf_tensor(name, shape, dt))

        def sem(name):
            return ctx.enter_context(nc.semaphore(name))

        banks = ctx.enter_context(nc.psum_tensor("banks", [128, 8, 512], F32))

        K = {n: sb(n, list(t[n].shape)) for n in ("chan_avg", "identity", "inverse")}
        gate_w = sb("gate_w", [128, 3])
        w1T = [sb(f"mlp{n}_w1T", [NL, NL]) for n in (1, 2)]
        b1 = [sb(f"mlp{n}_b1", [NL, 1]) for n in (1, 2)]
        w2T = [sb("mlp1_w2T", [NL, 9, NL]), sb("mlp2_w2T", [NL, 25, NL])]
        b2 = [sb("mlp1_b2", [NL, 9]), sb("mlp2_b2", [NL, 25])]
        hid_wb = sb("hid_wb", [NF + 1, 3 * NF])
        dw_wb = sb("dw_wb", [10, 3 * NF])
        ln_w = sb("ln_w", [2 * NF, 1])
        ln_b = sb("ln_b", [2 * NF, 1])
        out_w2 = sb("out_w2", [NF, 2, NF])
        last_wT = sb("last_wT", [NF, 2, C])
        out_b = sb("out_b", [NF, 1])
        last_b = sb("last_b", [128, 1])
        final_w = sb("final_w", [128, 2, C])
        G = [sb(f"G_{part}", [NWIN + 1, NF, NG], F16) for part in ("hi", "lo")]
        hid_m = [sb(f"hid_m_{part}", [128, B, 3 * NF], F16) for part in ("hi", "lo")]
        in_a = sb("in_a", [NF + 1, B])
        res_a = sb("res_a", [128, B])
        res_c = sb("res_c", [128, B])
        eps_gn = sb("eps_gn", [128, 1])
        eps_ln = sb("eps_ln", [128, 1])

        s_const = sem("constants_loaded")
        s_set = sem("constants_set")
        sp_passed = sem("sync_passed_its_waits")

        early = ctx.enter_context(ExitStack())
        K["diagonals"] = early.enter_context(nc.sbuf_tensor("diagonals", [128, 138], F32))
        local_k = early.enter_context(nc.sbuf_tensor("local_k", [128, B * NL + 1, SETK], F32))

        with ExitStack() as st:
            for n in ("pair_avg", "quad_avg", "from_prev", "from_next", "pick_half0", "pick_half1",
                      "pick_freq", "pick_out", "side0", "side1", "ones_row", "w_scale", "bias_scale", "spread"):
                K[n] = st.enter_context(nc.sbuf_tensor(n, list(t[n].shape), F32))

            def sb1(name, shape):
                return st.enter_context(nc.sbuf_tensor(name, shape, F32))

            def sem1(name):
                return st.enter_context(nc.semaphore(name))

            xs = sb1("xs", [128, 2, SR * W])
            stats = sb1("stats", [128, B, NST * SR, 6])
            cols = sb1("cols", [128, B, NST, 2])
            edge = sb1("edge", [128, B, W])
            ebuf = sb1("ebuf", [10, 32 * (NWIN + 1)])
            mv = sb1("mv", [128, B, 2])
            V = {n: sb1(f"c_{n}", [128, B]) for n in (
                "mean", "var", "mc", "d", "e", "vc", "M", "d1", "e1", "v1", "i1", "r", "s", "t1", "t2",
                "g", "rg", "a", "m2", "a2", "v2", "bb", "d2", "e2", "v3", "i2", "r2", "A", "B", "bm", "Am")}
            BS = sb1("BS", [128, 10, B])
            H0 = sb1("H0", [NL, 8, B])
            H1 = sb1("H1", [NL, 8, B])
            CS = sb1("CS", [NL, 2, B])
            TOT = sb1("TOT", [NL, B])
            hid = [sb1(f"hid{n}", [NL, B]) for n in (1, 2)]
            ST = sb1("ST", [NL, B, 9])
            PR = sb1("PR", [NL, B, 9])
            KB = sb1("KB", [NL, B, SETK])
            pooled2 = sb1("pooled2", [NL, B])
            pooled2s = sb1("pooled2s", [NL, B])
            AB = sb1("AB", [NF + 1, 2, B])
            B49 = sb1("B49", [NF + 1, B])
            Bb = sb1("Bb", [NF + 1, B, NF + 1])
            ones49 = sb1("ones49", [NF + 1, NF + 1])
            bias_row = sb1("bias_row", [NF + 1, B, 3 * NF])
            bias_tot = sb1("bias_tot", [128, 1])

            x_in = [sem1("x_tile_even_in"), sem1("x_tile_odd_in")]
            edge_in = sem1("edge_rows_in")
            stat_done = sem1("stat_tiles_done")
            prep_dve = sem1("prep_dve")
            prep_pe = sem1("prep_pe")
            prep_chain = sem1("prep_chain")
            prep_act = sem1("prep_act")
            table_in = sem1("table_in")
            table_mm = sem1("table_products")
            table_hi = sem1("table_high_parts")
            table_out = sem1("table_split")

            NCONST = [0]
            x_halves = x.rearrange("b c (h r) w -> b (c h) (r w)", h=2)
            with nc.Block() as block:
                @block.sync
                def _(sp):
                    def load(dst, src):
                        sp.dma_start(dst, src).then_inc(s_const, 16)
                        NCONST[0] += 16

                    for n in K:
                        load(K[n][:, :], t[n][:, :])
                    load(gate_w[:, :], t["gate_w"][:, :])
                    for n in (0, 1):
                        load(w1T[n][:, :], t[f"mlp{n + 1}_w1T"][:, :])
                        load(b1[n][:, :], t[f"mlp{n + 1}_b1"][:, :])
                        load(w2T[n][:, :, :], t[f"mlp{n + 1}_w2T"][:, :, :])
                        load(b2[n][:, :], t[f"mlp{n + 1}_b2"][:, :])
                    load(hid_wb[:, :], t["hid_wb"][:, :])
                    load(dw_wb[:, :], t["dw_wb"][:, :])
                    load(ln_w[:, :], t["ln_w"][:, :])
                    load(ln_b[:, :], t["ln_b"][:, :])
                    for s in range(2):
                        load(out_w2[:, s, :], t["out_w"][:, :])
                        load(last_wT[:, s, :], t["last_wT"][NL:C, :])
                    load(out_b[:, :], t["out_b"][:, :])
                    load(last_b[:, :], t["last_b"][:, :])
                    sp.wait_ge(s_set, 1)
                    for s in range(2):
                        load(final_w[2 * NF + NL * s:2 * NF + NL * (s + 1), s, :], t["last_wT"][0:NL, :])
                    for b in range(B):
                        for h in range(2):
                            sp.dma_start(edge[h:128:2, b, :], x[b, :, h * (H - 1), :]).then_inc(edge_in, 16)
                    with sp.Fori(0, B) as b:
                        with sp.Fori(0, NST // 2) as n2:
                            for par in range(2):
                                sp.wait_ge(stat_done, b * NST + n2 * 2 + par + 1)
                                sp.sem_inc(sp_passed, 1)
                                sp.dma_start(xs[:, par, :], x_halves[b, :, bass.ds((n2 * 2 + par) * SR * W, SR * W)]
                                             ).then_inc(x_in[par], 16)

                @block.gpsimd
                def _(pool):
                    nc.gpsimd.memset(final_w[:, :, :], 0.0).then_inc(s_set, 1)
                    nc.gpsimd.memset(eps_gn[:, :], EPS_GN).then_inc(s_set, 1)
                    nc.gpsimd.memset(eps_ln[:, :], EPS_LN).then_inc(s_set, 1)
                    nc.gpsimd.memset(ones49[:, :], 1.0).then_inc(s_set, 1)
                    nc.gpsimd.memset(local_k[:, B * NL, :], 0.0).then_inc(s_set, 1)
                    for part in hid_m:
                        nc.gpsimd.memset(part[:, :, :], 0.0).then_inc(s_set, 1)

                @block.tensor
                def _(pe):
                    pe.wait_ge(s_const, NCONST[0])

                    for n in range(NTAB):
                        pe.wait_ge(table_in, 16 * (n + 1))
                        if n:
                            pe.wait_ge(table_out, 4 * n)
                        kind = min(n * 32 // NSPEC, 2)
                        for j in range(32):
                            last = nc.tensor.matmul(banks[0:NWIN + 1, j // 8, (j % 8) * NF:(j % 8 + 1) * NF],
                                                    ebuf[:, j * (NWIN + 1):(j + 1) * (NWIN + 1)],
                                                    dw_wb[:, kind * NF:(kind + 1) * NF], start=True, stop=True)
                        last.then_inc(table_mm, 1)

                    last = nc.tensor.matmul(banks[0:2 * NF, 6, 0:C], out_w2[:, :, :].rearrange("m s c -> m (s c)"),
                                            last_wT[:, 0, :], start=True, stop=True)
                    last = nc.tensor.matmul(banks[:, 6, 100:101], last_wT[:, :, :].rearrange("m s c -> m (s c)"),
                                            out_b[:, :], start=True, stop=True)
                    last.then_inc(prep_pe, 1)

                    pe.wait_ge(prep_dve, 2)
                    nc.tensor.matmul(banks[:, 4, 0:B], K["pair_avg"][:, :], V["mean"][:, :],
                                     start=True, stop=True).then_inc(prep_pe, 1)
                    pe.wait_ge(prep_dve, 3)
                    nc.tensor.matmul(banks[:, 4, 8:8 + B], K["pair_avg"][:, :], V["e"][:, :], start=True, stop=True)
                    nc.tensor.matmul(banks[:, 4, 16:16 + B], K["quad_avg"][:, :], V["mc"][:, :],
                                     start=True, stop=True).then_inc(prep_pe, 1)
                    pe.wait_ge(prep_dve, 4)
                    nc.tensor.matmul(banks[:, 4, 24:24 + B], K["quad_avg"][:, :], V["e1"][:, :],
                                     start=True, stop=True)
                    nc.tensor.matmul(banks[:, 4, 32:32 + B], K["from_prev"][:, :], V["s"][:, :], start=True, stop=True)
                    nc.tensor.matmul(banks[:, 4, 40:40 + B], K["from_next"][:, :], V["s"][:, :],
                                     start=True, stop=True).then_inc(prep_pe, 1)
                    pe.wait_ge(prep_dve, 6)
                    nc.tensor.matmul(banks[:, 4, 48:48 + B], K["quad_avg"][:, :], V["m2"][:, :],
                                     start=True, stop=True).then_inc(prep_pe, 1)
                    pe.wait_ge(prep_dve, 7)
                    nc.tensor.matmul(banks[:, 4, 56:56 + B], K["quad_avg"][:, :], V["e2"][:, :],
                                     start=True, stop=True).then_inc(prep_pe, 1)
                    pe.wait_ge(prep_dve, 9)
                    bs = BS[:, :, :].rearrange("p q b -> p (q b)")
                    nc.tensor.matmul(banks[0:NL, 5, 0:8 * B], K["pick_half0"][:, :], bs[:, 0:8 * B], start=True, stop=True)
                    nc.tensor.matmul(banks[0:NL, 5, 64:64 + 8 * B], K["pick_half1"][:, :], bs[:, 0:8 * B],
                                     start=True, stop=True)
                    nc.tensor.matmul(banks[0:NF + 1, 5, 128:128 + 2 * B], K["pick_freq"][:, :], bs[:, 6 * B:8 * B],
                                     start=True, stop=True)
                    nc.tensor.matmul(banks[:, 5, 192:192 + 2 * B], K["pick_out"][:, :], bs[:, 8 * B:10 * B],
                                     start=True, stop=True).then_inc(prep_pe, 1)
                    pe.wait_ge(prep_dve, 10)
                    for b in range(B):
                        nc.tensor.matmul(banks[0:NF + 1, b % 4, 0:3 * NF], Bb[:, b, :], hid_wb[:, :], start=True, stop=True)
                    nc.tensor.matmul(banks[0:NL, 6, 0:B], w1T[0][:, :], H0[:, 5, :],
                                     start=True, stop=True).then_inc(prep_pe, 1)
                    pe.wait_ge(prep_act, 4)
                    for q in range(9):
                        last = nc.tensor.matmul(banks[0:NL, 6, 16 + q * B:16 + (q + 1) * B], w2T[0][:, q, :],
                                                hid[0][:, :], start=True, stop=True)
                    last.then_inc(prep_pe, 1)
                    pe.wait_ge(prep_dve, 11)
                    nc.tensor.matmul(banks[0:NL, 7, 0:B], w1T[1][:, :], pooled2s[:, :],
                                     start=True, stop=True).then_inc(prep_pe, 1)
                    pe.wait_ge(prep_act, 5)
                    for q in range(25):
                        last = nc.tensor.matmul(banks[0:NL, 7, 16 + q * B:16 + (q + 1) * B], w2T[1][:, q, :],
                                                hid[1][:, :], start=True, stop=True)
                    last.then_inc(prep_pe, 1)
                    pe.wait_ge(prep_dve, 12)
                    for c in range(NL):
                        last = nc.tensor.matmul(banks[:, c // 3 % 6, c % 3 * B * SETK:(c % 3 + 1) * B * SETK],
                                                K["spread"][:, c * 128:(c + 1) * 128],
                                                KB[:, :, :].rearrange("p b q -> p (b q)"), start=True, stop=True)
                    last.then_inc(prep_pe, 1)

                @block.scalar
                def _(act):
                    act.wait_ge(s_const, NCONST[0])
                    act.dma_start(ebuf[:, :], t["dft"][0]).then_inc(table_in, 16)
                    for n in range(NTAB):
                        act.wait_ge(table_mm, n + 1)
                        if n + 1 < NTAB:
                            act.dma_start(ebuf[:, :], t["dft"][n + 1]).then_inc(table_in, 16)
                        for j in range(4):
                            nc.scalar.copy(G[0][:, :, 32 * n + 8 * j:32 * n + 8 * (j + 1)].rearrange("p c f -> p f c"),
                                           banks[0:NWIN + 1, j, 0:8 * NF].rearrange("p (f c) -> p f c", c=NF)
                                           ).then_inc(table_hi, 1)
                    act.wait_ge(s_set, 4)
                    act.wait_ge(prep_dve, 5)
                    nc.scalar.activation(V["r"][:, :], V["i1"][:, :], ACT.Sqrt).then_inc(prep_act, 1)
                    nc.scalar.activation(V["g"][:, :], V["t2"][:, :], ACT.Sigmoid).then_inc(prep_act, 1)
                    act.wait_ge(prep_dve, 8)
                    nc.scalar.activation(V["r2"][:, :], V["i2"][:, :], ACT.Sqrt).then_inc(prep_act, 1)
                    act.wait_ge(prep_pe, 8)
                    nc.scalar.activation(hid[0][:, :], banks[0:NL, 6, 0:B], ACT.Relu, bias=b1[0][:, :]
                                         ).then_inc(prep_act, 1)
                    act.wait_ge(prep_pe, 10)
                    nc.scalar.activation(hid[1][:, :], banks[0:NL, 7, 0:B], ACT.Relu, bias=b1[1][:, :]
                                         ).then_inc(prep_act, 1)

                @block.vector
                def _(dve):
                    v = nc.vector
                    dve.sem_inc(stat_done, 2)
                    steps = [0]

                    def link(ins):
                        steps[0] += 1
                        ins.then_inc(prep_chain, 1)
                        dve.wait_ge(prep_chain, steps[0])

                    def done(ins, n):
                        ins.then_inc(prep_dve, 1)
                        dve.wait_ge(prep_dve, n)

                    all_stats = stats.rearrange("p b n s -> p (b n) s")
                    all_cols = cols.rearrange("p b n s -> p (b n) s")

                    def two_tiles(m):
                        for par in range(2):
                            dve.wait_ge(x_in[par], 16 * m + 16)
                            for r in range(SR):
                                v.bn_stats(all_stats[:, bass.ds((m * 2 + par) * SR + r, 1), :]
                                           .rearrange("p a s -> p (a s)"), xs[:, par, r * W:(r + 1) * W])
                            v.tensor_reduce(all_cols[:, bass.ds(m * 2 + par, 1), :].rearrange("p a s -> p (a s)"),
                                            xs[:, par, :].rearrange("p (r w) -> p w r", w=W)
                                            [:, 0:W:W - 1, :], AX, ALU.add).then_inc(stat_done, 1)

                    with dve.Fori(0, NTAB) as n:
                        for j in range(4):
                            for i in range(PER):
                                two_tiles((n * 4 + j) * PER + i)
                            dve.wait_ge(table_hi, 4 * n + j + 1)
                            v.tensor_tensor(G[1][:, :, bass.ds(n * 32 + 8 * j, 8)].rearrange("p c f -> p f c"),
                                            banks[0:NWIN + 1, j, 0:8 * NF].rearrange("p (f c) -> p f c", c=NF),
                                            G[0][:, :, bass.ds(n * 32 + 8 * j, 8)].rearrange("p c f -> p f c"),
                                            ALU.subtract).then_inc(table_out, 1)
                    with dve.Fori(4 * NTAB * PER, B * NST // 2) as m:
                        two_tiles(m)
                    dve.wait_ge(s_const, NCONST[0])
                    dve.wait_ge(prep_pe, 1)
                    v.tensor_scalar(final_w[0:2 * NF, 0, :], banks[0:2 * NF, 6, 0:C], K["side0"][:, :], None, ALU.mult)
                    v.tensor_scalar(final_w[0:2 * NF, 1, :], banks[0:2 * NF, 6, 0:C], K["side1"][:, :], None, ALU.mult)
                    done(v.tensor_tensor(bias_tot[:, :], banks[:, 6, 100:101], last_b[:, :], ALU.add), 1)
                    dve.wait_ge(stat_done, B * NST + 2)
                    for b in range(B):
                        last = v.bn_aggr(mv[:, b, :], stats[:, b, :, :].rearrange("p n s -> p (n s)"))
                    link(last)
                    v.tensor_copy(V["mean"][:, :], mv[:, :, 0])
                    done(v.tensor_copy(V["var"][:, :], mv[:, :, 1]), 2)

                    def tt(o, a, c, op):
                        return v.tensor_tensor(V[o][:, :], V[a][:, :], V[c][:, :], op)

                    dve.wait_ge(prep_pe, 2)
                    v.tensor_copy(V["mc"][:, :], banks[:, 4, 0:B])
                    link(v.tensor_tensor(V["d"][:, :], V["mean"][:, :], banks[:, 4, 0:B], ALU.subtract))
                    link(tt("d", "d", "d", ALU.mult))
                    done(tt("e", "d", "var", ALU.add), 3)
                    dve.wait_ge(prep_pe, 3)
                    v.tensor_copy(V["M"][:, :], banks[:, 4, 16:16 + B])
                    v.tensor_copy(V["vc"][:, :], banks[:, 4, 8:8 + B])
                    link(v.tensor_tensor(V["d1"][:, :], V["mc"][:, :], banks[:, 4, 16:16 + B], ALU.subtract))
                    link(v.tensor_scalar(V["s"][:, :], V["d1"][:, :], 0.0, None, ALU.is_ge))
                    link(v.tensor_scalar(V["s"][:, :], V["s"][:, :], 2.0, -1.0, ALU.mult, ALU.add))
                    link(tt("e1", "d1", "d1", ALU.mult))
                    done(tt("e1", "e1", "vc", ALU.add), 4)
                    dve.wait_ge(prep_pe, 4)
                    link(v.tensor_scalar(V["v1"][:, :], banks[:, 4, 24:24 + B], EPS_GN, None, ALU.add))
                    link(v.reciprocal(V["i1"][:, :], V["v1"][:, :]))
                    link(v.tensor_scalar(V["t1"][:, :], banks[:, 4, 32:32 + B], gate_w[:, 0:1], None, ALU.mult))
                    link(v.scalar_tensor_tensor(V["t1"][:, :], V["s"][:, :], gate_w[:, 1:2], V["t1"][:, :],
                                                ALU.mult, ALU.add))
                    link(v.scalar_tensor_tensor(V["t1"][:, :], banks[:, 4, 40:40 + B], gate_w[:, 2:3], V["t1"][:, :],
                                                ALU.mult, ALU.add))
                    done(v.tensor_scalar(V["t2"][:, :], V["t1"][:, :], 1.0 / HW, None, ALU.mult), 5)
                    dve.wait_ge(prep_act, 2)
                    link(tt("rg", "r", "g", ALU.mult))
                    link(v.tensor_scalar(V["a"][:, :], V["rg"][:, :], 1.0, None, ALU.add))
                    link(tt("m2", "d1", "rg", ALU.mult))
                    link(tt("m2", "m2", "mc", ALU.add))
                    link(tt("a2", "a", "a", ALU.mult))
                    link(tt("v2", "a2", "vc", ALU.mult))
                    link(tt("bb", "M", "rg", ALU.mult))
                    done(v.tensor_scalar(V["bb"][:, :], V["bb"][:, :], -1.0, None, ALU.mult), 6)
                    dve.wait_ge(prep_pe, 5)
                    link(v.tensor_tensor(V["d2"][:, :], V["m2"][:, :], banks[:, 4, 48:48 + B], ALU.subtract))
                    link(v.tensor_tensor(V["bm"][:, :], V["bb"][:, :], banks[:, 4, 48:48 + B], ALU.subtract))
                    link(tt("e2", "d2", "d2", ALU.mult))
                    done(tt("e2", "e2", "v2", ALU.add), 7)
                    dve.wait_ge(prep_pe, 6)
                    link(v.tensor_scalar(V["v3"][:, :], banks[:, 4, 56:56 + B], EPS_GN, None, ALU.add))
                    done(v.reciprocal(V["i2"][:, :], V["v3"][:, :]), 8)
                    dve.wait_ge(prep_act, 3)
                    link(tt("A", "a", "r2", ALU.mult))
                    link(tt("B", "bm", "r2", ALU.mult))
                    dve.wait_ge(edge_in, 32 * B)
                    v.tensor_reduce(BS[:, 0, :], edge[:, :, :], AX, ALU.add)
                    v.tensor_copy(BS[:, 1, :], edge[:, :, 0])
                    v.tensor_copy(BS[:, 2, :], edge[:, :, W - 1])
                    v.tensor_reduce(BS[:, 3, :], cols[:, :, :, 0], AX, ALU.add)
                    v.tensor_reduce(BS[:, 4, :], cols[:, :, :, 1], AX, ALU.add)
                    link(v.tensor_copy(BS[:, 5, :], V["mc"][:, :]))
                    for q, count in enumerate((W, 1, 1, HH, HH, 1)):
                        link(v.tensor_tensor(BS[:, q, :], BS[:, q, :], V["A"][:, :], ALU.mult))
                        link(v.scalar_tensor_tensor(BS[:, q, :], V["B"][:, :], float(count), BS[:, q, :],
                                                    ALU.mult, ALU.add))
                    v.tensor_copy(BS[:, 6, :], V["A"][:, :])
                    v.tensor_copy(BS[:, 7, :], V["B"][:, :])
                    v.tensor_copy(BS[:, 8, :], V["a"][:, :])
                    done(v.tensor_copy(BS[:, 9, :], V["bb"][:, :]), 9)

                    dve.wait_ge(prep_pe, 7)
                    v.tensor_copy(H0[:, :, :], banks[0:NL, 5, 0:8 * B].rearrange("p (q b) -> p q b", b=B))
                    v.tensor_copy(H1[:, :, :], banks[0:NL, 5, 64:64 + 8 * B].rearrange("p (q b) -> p q b", b=B))
                    v.tensor_copy(AB[:, :, :], banks[0:NF + 1, 5, 128:128 + 2 * B].rearrange("p (q b) -> p q b", b=B))
                    v.tensor_copy(res_a[:, :], banks[:, 5, 192:192 + B])
                    link(v.tensor_scalar(res_c[:, :], banks[:, 5, 192 + B:192 + 2 * B], bias_tot[:, :], None, ALU.add))
                    link(v.tensor_scalar(B49[:, :], AB[:, 1, :], K["ones_row"][:, :], None, ALU.add))
                    for b in range(B):
                        last = v.tensor_scalar(Bb[:, b, :], ones49[:, :], B49[:, b:b + 1], None, ALU.mult)
                    done(last, 10)

                    link(v.tensor_tensor(CS[:, :, :], H0[:, 3:5, :], H1[:, 3:5, :], ALU.add))
                    link(v.tensor_scalar(TOT[:, :], H0[:, 5, :], float(HW), None, ALU.mult))
                    for q in range(9):
                        dy, dx = q // 3 - 1, q % 3 - 1
                        dst = ST[:, :, q]
                        link(v.tensor_copy(dst, TOT[:, :]))
                        side = H0 if dy > 0 else H1
                        if dy:
                            link(v.tensor_tensor(dst, dst, side[:, 0, :], ALU.subtract))
                        if dx:
                            link(v.tensor_tensor(dst, dst, CS[:, 0 if dx > 0 else 1, :], ALU.subtract))
                        if dx and dy:
                            link(v.tensor_tensor(dst, dst, side[:, 1 if dx > 0 else 2, :], ALU.add))
                    dve.wait_ge(s_set, 7)
                    v.tensor_scalar(in_a[:, :], AB[:, 0, :], K["ones_row"][:, :], None, ALU.add)
                    dve.wait_ge(prep_pe, 8)
                    for b in range(B):
                        link(v.tensor_scalar(bias_row[:, b, :], banks[0:NF + 1, b % 4, 0:3 * NF],
                                             K["bias_scale"][:, :], None, ALU.mult))
                        link(v.scalar_tensor_tensor(bias_row[:, b, :], hid_wb[:, :], K["w_scale"][:, :],
                                                    bias_row[:, b, :], ALU.mult, ALU.add))
                        v.tensor_copy(hid_m[0][LO:LO + NF + 1, b, :], bias_row[:, b, :])
                        link(v.tensor_copy(hid_m[0][0:NF + 1, b, :], bias_row[:, b, :]))
                        link(v.tensor_tensor(hid_m[1][0:NF + 1, b, :], bias_row[:, b, :], hid_m[0][0:NF + 1, b, :],
                                             ALU.subtract))
                    dve.wait_ge(prep_pe, 9)
                    for b in range(B):
                        link(v.tensor_tensor(KB[:, b, 0:9], banks[0:NL, 6, 16 + b:16 + 9 * B:B], b2[0][:, :], ALU.add))
                    link(v.tensor_tensor(PR[:, :, :], KB[:, :, 0:9], ST[:, :, :], ALU.mult))
                    link(v.tensor_reduce(pooled2[:, :], PR[:, :, :], AX, ALU.add))
                    done(v.tensor_scalar(pooled2s[:, :], pooled2[:, :], 1.0 / HW, None, ALU.mult), 11)
                    dve.wait_ge(prep_pe, 11)
                    for b in range(B):
                        v.tensor_tensor(KB[:, b, 9:34], banks[0:NL, 7, 16 + b:16 + 25 * B:B], b2[1][:, :], ALU.add)
                        v.tensor_copy(KB[:, b, 34:35], H0[:, 6, b:b + 1])
                        last = v.tensor_copy(KB[:, b, 35:36], H0[:, 7, b:b + 1])
                    done(last, 12)
                    dve.wait_ge(prep_pe, 12)
                    for c in range(NL):
                        v.tensor_copy(local_k[:, c:B * NL:NL, :], banks[:, c // 3 % 6, c % 3 * B * SETK:(c % 3 + 1) * B * SETK]
                                      .rearrange("p (b q) -> p b q", q=SETK))

        with ExitStack() as st:
            def sb3(name, shape, dt=F32):
                return st.enter_context(nc.sbuf_tensor(name, shape, dt))

            def sem3(name):
                return st.enter_context(nc.semaphore(name))

            PARTS = ("hi", "lo")
            xl = sb3("xl", [128, 2, W])
            z = [sb3(f"z_{part}", [128, 2, W + 2], F16) for part in PARTS]
            y1 = [sb3(f"y1_{part}", [128, 2, W + 4], F16) for part in PARTS]
            y2 = sb3("y2", [128, 2, W])
            taps = sb3("taps", [128, 2, SETK])
            T_sum = sb3("T_sum", [128, 8, 132])
            T = [sb3(f"T_{part}", [128, 2, 8, 132], F16) for part in PARTS]
            l_set = sem3("local_pads_zero")
            l_in = [sem3(f"local_x{n}_in") for n in (0, 1)]
            l_zf = sem3("local_z")
            l_zh = sem3("local_z_high_part")
            l_z = sem3("local_z_low_part")
            l_p1 = sem3("local_3x3_products")
            l_y1h = sem3("local_y1_high_part")
            l_y1 = sem3("local_y1_low_part")
            l_p2 = sem3("local_5x5_products")
            l_y2 = sem3("local_y2")
            l_st = [sem3(f"local_y2_{n}_stored") for n in (0, 1)]
            l_taps = sem3("local_taps")
            l_T = sem3("local_matrices")
            l_chain = sem3("local_matrix_steps")
            NK = B * NL // 2
            NSTEP = 2 * NB
            LAG = min(4, NSTEP)

            def pairs(eng, body, tail):
                body(0, True)
                with eng.Fori(1, NK) as k:
                    body(k, False)
                tail(NK - 1)

            def lagging(step, k, n, lag, first):
                if not first or n >= lag:
                    step(k, n - lag)

            def split(to, weights, values, first, side):
                for dx in range(side):
                    for i, (g, h) in enumerate(((0, 1), (0, 0), (1, 0))):
                        last = nc.tensor.matmul(to, weights(g, first + dx), values(h, dx),
                                                start=dx == 0 and i == 0, stop=dx == side - 1 and i == 2)
                return last

            with nc.Block() as block:
                x_rows = x.rearrange("b c h w -> (b c) h w")
                y2_rows = scratch.rearrange("b c h w -> (b c) h w")

                @block.sync
                def _(sp):
                    sp.sem_inc(l_st[0], 1)
                    sp.sem_inc(l_st[1], 1)

                    def store_local(k, n):
                        r0, r1 = BANDS[n % NB][0]
                        sp.wait_ge(l_y2, k * NSTEP + n + 3)
                        sp.sem_inc(sp_passed, 1)
                        sp.dma_start(y2_rows[bass.ds(k * 2 + n // NB, 1), r0:r1, :].rearrange("a r w -> (a r) w"),
                                     y2[0:r1 - r0, n % 2, :]).then_inc(l_st[n % 2], 16)

                    def pair(b, c2, first):
                        k = b * (NL // 2) + c2
                        for n in range(NSTEP):
                            z0, z1 = BANDS[n % NB][2]
                            sp.wait_ge(l_z, k * NSTEP + n + 1)
                            sp.sem_inc(sp_passed, 1)
                            sp.dma_start(xl[0:z1 - z0, n % 2, :],
                                         x_rows[bass.ds(b * C + c2 * 2 + n // NB, 1), z0:z1, :]
                                         .rearrange("a r w -> (a r) w")).then_inc(l_in[n % 2], 16)
                            lagging(store_local, k, n, LAG, first)

                    pair(0, 0, True)
                    with sp.Fori(1, NL // 2) as c2:
                        pair(0, c2, False)
                    if B > 1:
                        with sp.Fori(1, B) as b:
                            with sp.Fori(0, NL // 2) as c2:
                                pair(b, c2, False)
                    for n in range(NSTEP - LAG, NSTEP):
                        store_local(NK - 1, n)
                    for n in (0, 1):
                        sp.wait_ge(l_st[n], 1 + 16 * NK * NB)

                @block.scalar
                def _(act):
                    act.sem_inc(l_y1h, 2)
                    act.wait_ge(l_set, 2)

                    def z_high(k, n):
                        z0, z1 = BANDS[n % NB][2]
                        act.wait_ge(l_in[n % 2], 16 * (k * NB + n // 2 + 1))
                        act.wait_ge(l_taps, 2 * k + n // NB + 1)
                        nc.scalar.activation(xl[0:z1 - z0, n % 2, :], xl[0:z1 - z0, n % 2, :],
                                             ACT.Identity, bias=taps[0:z1 - z0, n // NB, 35:36],
                                             scale=taps[0:z1 - z0, n // NB, 34:35]).then_inc(l_zf, 1)
                        act.wait_ge(l_zf, k * NSTEP + n + 1)
                        act.wait_ge(l_p1, k * NSTEP + n + 1)
                        nc.scalar.copy(z[0][0:z1 - z0, n % 2, 1:W + 1], xl[0:z1 - z0, n % 2, :]).then_inc(l_zh, 1)

                    def y1_high(k, n):
                        a0, a1 = BANDS[n % NB][1]
                        act.wait_ge(l_p1, k * NSTEP + n + 3)
                        act.wait_ge(l_p2, k * NSTEP + n + 1)
                        nc.scalar.activation(y1[0][0:a1 - a0, n % 2, 2:W + 2], banks[0:a1 - a0, n % 2, :],
                                             ACT.Copy, scale=1 / TAP_SCALE).then_inc(l_y1h, 1)

                    def pair(k, first):
                        for n in range(NSTEP):
                            z_high(k, n)
                            lagging(y1_high, k, n, 1, first)

                    pairs(act, pair, lambda k: y1_high(k, NSTEP - 1))

                @block.tensor
                def _(pe):
                    pe.sem_inc(l_p1, 2)
                    pe.sem_inc(l_p2, 2)
                    pe.wait_ge(l_set, 2)

                    def three(k, n):
                        ch = n // NB
                        _rows, (a0, a1), (z0, z1) = BANDS[n % NB]
                        if n % NB == 0:
                            pe.wait_ge(l_T, 2 * k + ch + 1)
                        pe.wait_ge(l_z, k * NSTEP + n + 3)
                        pe.wait_ge(l_y1, k * NSTEP + n + 1)
                        off = a0 - z0
                        split(banks[0:a1 - a0, n % 2, :], lambda g, dx: T[g][0:z1 - z0, ch, dx, off:off + a1 - a0],
                              lambda h, dx: z[h][0:z1 - z0, n % 2, dx:dx + W], 0, 3).then_inc(l_p1, 1)

                    def five(k, n):
                        ch = n // NB % 2
                        (r0, r1), (a0, a1), _rows = BANDS[n % NB]
                        pe.wait_ge(l_y1, k * NSTEP + n + 3)
                        pe.wait_ge(l_y2, k * NSTEP + n + 1)
                        off = r0 - a0
                        split(banks[0:r1 - r0, 2 + n % 2, :], lambda g, dx: T[g][0:a1 - a0, ch, dx, off:off + r1 - r0],
                              lambda h, dx: y1[h][0:a1 - a0, n % 2, dx:dx + W], 3, 5).then_inc(l_p2, 1)

                    def pair(k, first):
                        for n in range(NSTEP):
                            three(k, n)
                            lagging(five, k, n, 1, first)

                    pairs(pe, pair, lambda k: five(k, NSTEP - 1))

                @block.vector
                def _(dve):
                    v = nc.vector
                    for part in range(2):
                        for n in (0, 1):
                            v.memset(z[part][:, n, :], 0.0)
                            last = v.memset(y1[part][:, n, :], 0.0)
                    last.then_inc(l_set, 2)
                    dve.sem_inc(l_z, 2)
                    dve.sem_inc(l_y1, 2)
                    dve.sem_inc(l_y2, 2)
                    dve.sem_inc(l_chain, 1)

                    def matrices(cell, ch, first=False):
                        base = cell * 35 + 1
                        v.tensor_copy(taps[:, ch, :], local_k[:, bass.ds(cell, 1), :]
                                      .rearrange("p a q -> p (a q)")).then_inc(l_taps, 1)
                        dve.wait_ge(l_taps, cell + 1)
                        n = 0
                        for side, tap0, col in ((3, 0, 0), (5, 9, 3)):
                            for ky in range(side):
                                if ky:
                                    dve.wait_ge(l_chain, base + n)
                                for dx in range(side):
                                    s = 3 + ky - side // 2
                                    tap = taps[:, ch, tap0 + ky * side + dx:tap0 + ky * side + dx + 1]
                                    diagonal = K["diagonals"][:, s:s + 132]
                                    if ky == 0:
                                        i = v.tensor_scalar(T_sum[:, col + dx, :], diagonal, tap, None, ALU.mult)
                                    else:
                                        i = v.scalar_tensor_tensor(T_sum[:, col + dx, :], diagonal, tap,
                                                                   T_sum[:, col + dx, :], ALU.mult, ALU.add)
                                    n += 1
                                    i.then_inc(l_chain, 1)
                                if n in (9, 19, 29):
                                    yield
                        yield
                        dve.wait_ge(l_chain, base + 34)
                        if not first:
                            dve.wait_ge(l_p2, (cell - 1) * NB + 2)
                        v.tensor_copy(T[0][:, ch, :, :], T_sum[:, :, :]).then_inc(l_chain, 1)
                        dve.wait_ge(l_chain, base + 35)
                        v.tensor_tensor(T[1][:, ch, :, :], T_sum[:, :, :], T[0][:, ch, :, :], ALU.subtract
                                        ).then_inc(l_T, 1)

                    def z_low(k, n):
                        z0, z1 = BANDS[n % NB][2]
                        dve.wait_ge(l_zh, k * NSTEP + n + 1)
                        v.tensor_tensor(z[1][0:z1 - z0, n % 2, 1:W + 1], xl[0:z1 - z0, n % 2, :],
                                        z[0][0:z1 - z0, n % 2, 1:W + 1], ALU.subtract).then_inc(l_z, 1)

                    def y1_low(k, n):
                        a0, a1 = BANDS[n % NB][1]
                        dve.wait_ge(l_y1h, k * NSTEP + n + 3)
                        v.scalar_tensor_tensor(y1[1][0:a1 - a0, n % 2, 2:W + 2], banks[0:a1 - a0, n % 2, :],
                                               1 / TAP_SCALE, y1[0][0:a1 - a0, n % 2, 2:W + 2],
                                               ALU.mult, ALU.subtract).then_inc(l_y1, 1)

                    def y2_out(k, n):
                        r0, r1 = BANDS[n % NB][0]
                        dve.wait_ge(l_p2, k * NSTEP + n + 3)
                        dve.wait_ge(l_st[n % 2], 16 * (k * NB + n // 2) + 1)
                        v.tensor_scalar(y2[0:r1 - r0, n % 2, :], banks[0:r1 - r0, 2 + n % 2, :],
                                        1 / TAP_SCALE, None, ALU.mult).then_inc(l_y2, 1)

                    def pair(k, first):
                        for n in range(NSTEP):
                            z_low(k, n)
                            lagging(y1_low, k, n, 1, first)
                            if n % NB == 0:
                                cell = 2 * k + n // NB + 1
                                dve.wait_ge(l_T, cell)
                                parts = matrices(cell, 1 - n // NB)
                            next(parts, None)
                            if n % NB == NB - 1:
                                for _part in parts:
                                    pass
                            lagging(y2_out, k, n, 2, first)

                    for _part in matrices(0, 0, True):
                        pass
                    pairs(dve, pair, lambda k: (y1_low(k, NSTEP - 1), y2_out(k, NSTEP - 2), y2_out(k, NSTEP - 1)))

        early.close()

        band = sb("band", [NF + 1, WIN, W + 2])
        wins = sb("wins", [128, (W + 2) * WIN + 128 - NWIN], F16)
        hidden = [sb(f"hidden_{part}", [NWIN + 1, 3 * NF, PW], F16) for part in ("hi", "lo")]
        prod = sb("prod", [NSPEC, NPAIR, 2, NF])
        vpix = sb("vpix", [PX, NPAIR, 2, NF])
        kspec = sb("kspec", [NSPEC, 2, QKB * PW])
        minus_mean = sb("minus_mean", [NSPEC, NCH, 16])
        sq = sb("sq", [128, 2, 512])
        rstd = sb("rstd", [2 * NF, 2, 512])
        normed = sb("normed", [2 * NF, 512])
        mixed = sb("mixed", [128, PS, HWID])
        xa = sb("xa", [128, PS, HWID])
        ot = sb("ot", [128, PS, HWID])
        hid_cur = [sb(f"hid_cur_{part}", [128, 3 * NF], F16) for part in ("hi", "lo")]
        in_a_cur = sb("in_a_cur", [NF + 1, 1])
        a_cur = sb("a_cur", [128, 1])
        c_cur = sb("c_cur", [128, 1])

        m_set = sem("main_tiles_set")
        band_in = sem("band_in")
        pe_passed = sem("pe_passed_its_waits")
        pool_passed = sem("pool_passed_its_waits")
        edge_rows_in = sem("edge_rows_of_band_in")
        cur_set = sem("batch_coefficients_set")
        wins_hi = sem("windows_high_parts")
        wins_lo = sem("windows_low_parts")
        s1_mm = sem("s1_products")
        s1_act = sem("hidden_high_parts")
        s1_dve = sem("hidden_low_parts")
        qk_mm = sem("qk_products")
        qk_act = sem("k_spectra_copied")
        qk_dve = sem("spectral_products")
        v_mm = sem("v_products")
        v_act = sem("v_copied")
        o_mm = sem("inverse_dft")
        g_sum = sem("sums_over_channels")
        g_dve = sem("means_over_channels")
        g_pool = sem("spectra_centered")
        sq_act = sem("squared")
        var_mm = sem("variance")
        ln_act = sem("variance_log")
        r_act = sem("rstd_ready")
        vt_mm = sem("v_transposed")
        t_dve = sem("normed_ready")
        y_dve = sem("mixed_ready")
        fin_mm = sem("final_products")
        fin_dve = sem("final_sums")
        xr_in = sem("residual_x_in")
        y2_in = sem("local_branch_in")
        xa_done = sem("residual_scaled")
        stored = sem("output_stored")

        BVAR, BVT = 6, 7
        BCEN = (4, 5)
        BFIN = (BVAR, BVT)

        def after(eng, s, count):
            eng.wait_ge(s, count + 1)

        BLOCKS = [f"s{m}" for m in range(NS1)] + [f"q{q}" for q in range(NQK)] + [f"v{r}" for r in range(NV)]
        PLAN = {"s0": ["f0"], "s1": ["f1"], "s2": ["o0"], "s3": ["o1"], "s4": ["f2"], "s5": ["o2"],
                "s6": ["f3"], "s7": ["o3"], "s8": ["r0"], "s9": ["t0"], "s10": ["r1"], "s11": ["o4"],
                "s12": ["o5"], "s13": ["t1"], "s14": ["o6"], "s15": ["r2", "o7", "t2"], "q3": ["r3"],
                "q5": ["t3"]}
        PLAN_ACT = {"s1": ["w0"], "s4": ["c0"], "s5": ["w1"], "s6": ["w2"], "s7": ["c1"], "s8": ["r0"],
                    "s9": ["e0"], "s10": ["w3"], "s11": ["r1"], "s12": ["e1"], "s13": ["w4", "c2"],
                    "s15": ["w5", "w6", "r2"], "q0": ["w7"], "q1": ["e2"], "q2": ["c3"], "q3": ["r3", "e3"]}
        PLAN_DVE = {"s1": ["f0"], "s2": ["f1"], "s4": ["w0"], "s5": ["f2"], "s6": ["f3"], "s8": ["w1"],
                    "s9": ["n0"], "s11": ["y0"], "s12": ["n1"], "s13": ["y1"], "s15": ["w2", "w3", "w4"],
                    "q0": ["w5"], "q1": ["w6", "n2"], "q2": ["y2"], "q3": ["w7", "n3"], "v1": ["y3", "g0"],
                    "v2": ["g1", "g2", "g3"]}

        def rows_of_batch(eng, b, row):
            k0 = b * NPR
            row(k0, None, None, True)
            row(k0 + 1, k0, None, True)
            with eng.Fori(2, NPR - 1) as j:
                row(k0 + j, k0 + j - 1, k0 + j - 2, True)
            row(k0 + (NPR - 1), k0 + (NPR - 2), k0 + (NPR - 3), False)
            row(None, k0 + (NPR - 1), k0 + (NPR - 2), False)
            row(None, None, k0 + (NPR - 1), False)

        def run_row(plan, main, steps, k, kl, kf, following):
            for block in BLOCKS:
                if k is not None:
                    main[block[0]](k, int(block[1:]))
                for step in plan.get(block, ()):
                    kind, n = step[0], int(step[1:])
                    if kind == "g":
                        if k is not None:
                            steps[kind](k, n)
                    elif kind == "f":
                        if kf is not None:
                            steps[kind](kf, n)
                    elif kind == "w":
                        if following:
                            steps[kind](k + 1, n)
                    elif kl is not None:
                        steps[kind](kl, n)

        def window_part(i):
            return i * (W // NWP), (i + 1) * (W // NWP) + (2 if i == NWP - 1 else 0)

        def s1_slot(m):
            return (m + 1) % 2 * 2

        with nc.Block() as block:
            @block.gpsimd
            def _(pool):
                nc.gpsimd.memset(band[:, :, :], 1.0).then_inc(m_set, 1)
                nc.gpsimd.memset(hidden[0][:, :, :], 1.0).then_inc(m_set, 1)
                nc.gpsimd.memset(hidden[1][:, :, :], 0.0).then_inc(m_set, 1)
                nc.gpsimd.memset(wins[:, :], 0.0).then_inc(m_set, 1)
                nc.gpsimd.memset(sq[:, :, :], 0.0).then_inc(m_set, 1)
                pool.wait_ge(m_set, 5)
                nc.gpsimd.memset(band[:, :, 0:1], 0.0).then_inc(m_set, 1)
                nc.gpsimd.memset(band[:, :, W + 1:W + 2], 0.0).then_inc(m_set, 1)
                pool.sem_inc(xa_done, 1)
                pool.sem_inc(g_pool, 1)
                with pool.Fori(0, B) as b:
                    pool.wait_ge(cur_set, b + 1)
                    pool.sem_inc(pool_passed, 1)
                    with pool.Fori(0, NPR) as j:
                        k = b * NPR + j
                        for c in range(NCH):
                            after(pool, g_dve, 4 * k + c + 1)
                            pool.sem_inc(pool_passed, 1)
                            chunk = prod[:, 8 * c:8 * (c + 1), :, :].rearrange("p i s c -> p (i s) c")
                            nc.gpsimd.tensor_tensor(chunk, chunk, minus_mean[:, c, :].unsqueeze(2)
                                                    .to_broadcast([NSPEC, 16, NF]), ALU.add).then_inc(g_pool, 1)
                        after(pool, xr_in, 32 * (k + 1))
                        pool.sem_inc(pool_passed, 1)
                        nc.gpsimd.tensor_scalar(xa[:, :, :], xa[:, :, :], a_cur[:, :], c_cur[:, :],
                                                ALU.mult, ALU.add).then_inc(xa_done, 1)

            @block.sync
            def _(sp):
                for s in (xr_in, y2_in, stored):
                    sp.sem_inc(s, 1)
                sp.sem_inc(band_in, 1)
                sp.wait_ge(m_set, 7)

                def load_band(b, k, j, y0, n, at):
                    sp.dma_start(band[0:NF, at:at + n, 1:W + 1], x[b, NL:C, bass.ds(y0, n), :]
                                 ).then_inc(band_in, 16)

                def set_row(r, source):
                    if source == "zeros":
                        sp.dma_start(band[:, r, 1:W + 1], t["zeros"][:, :]).then_inc(edge_rows_in, 16)
                    else:
                        sp.dma_start(band[NF:NF + 1, r, 1:W + 1], t["ones"][:, :]).then_inc(edge_rows_in, 16)

                def load_rest(b, k, j):
                    after(sp, fin_dve, 4 * k)
                    sp.sem_inc(sp_passed, 1)
                    after(sp, fin_mm, 4 * k)
                    sp.sem_inc(sp_passed, 1)
                    for s in range(2):
                        sp.dma_start(xa[C * s:C * (s + 1), :, :],
                                     x[b, :, bass.ds(j * PS, PS), HWID * s:HWID * (s + 1)]).then_inc(xr_in, 16)
                        p = 2 * NF + NL * s
                        sp.dma_start(mixed[p:p + NL, :, :],
                                     scratch[b, :, bass.ds(j * PS, PS), HWID * s:HWID * (s + 1)]).then_inc(y2_in, 16)

                def store(b, k, j):
                    after(sp, fin_dve, 4 * (k + 1))
                    sp.sem_inc(sp_passed, 1)
                    for s in range(2):
                        sp.dma_start(out[b, :, bass.ds(j * PS, PS), HWID * s:HWID * (s + 1)],
                                     ot[C * s:C * (s + 1), :, :]).then_inc(stored, 16)

                def band_free(k):
                    after(sp, wins_lo, NWP * k)
                    sp.sem_inc(sp_passed, 1)

                with sp.Fori(0, B) as b:
                    k0 = b * NPR
                    band_free(k0)
                    set_row(0, "zeros")
                    set_row(WIN - 1, "ones")
                    sp.wait_ge(edge_rows_in, 64 * b + 32)
                    load_band(b, k0, 0, 0, PS + 1, 1)
                    band_free(k0 + 1)
                    set_row(0, "ones")
                    sp.wait_ge(edge_rows_in, 64 * b + 48)
                    load_band(b, k0 + 1, 1, PS - 1, WIN, 0)
                    load_rest(b, k0, 0)
                    band_free(k0 + 2)
                    load_band(b, k0 + 2, 2, 2 * PS - 1, WIN, 0)
                    band_free(k0 + 3)
                    load_band(b, k0 + 3, 3, 3 * PS - 1, WIN, 0)
                    with sp.Fori(4, NPR - 1) as j:
                        store(b, k0 + j - 4, j - 4)
                        load_rest(b, k0 + j - 3, j - 3)
                        band_free(k0 + j)
                        load_band(b, k0 + j, j, j * PS - 1, WIN, 0)
                    j = NPR - 1
                    store(b, k0 + j - 4, j - 4)
                    load_rest(b, k0 + j - 3, j - 3)
                    band_free(k0 + j)
                    set_row(WIN - 1, "zeros")
                    sp.wait_ge(edge_rows_in, 64 * b + 64)
                    load_band(b, k0 + j, j, j * PS - 1, WIN - 1, 0)
                    for j in range(NPR - 3, NPR):
                        store(b, k0 + j - 1, j - 1)
                        load_rest(b, k0 + j, j)
                    store(b, k0 + NPR - 1, NPR - 1)
                sp.wait_ge(stored, 32 * B * NPR + 1)

            @block.tensor
            def _(pe):
                for s in (s1_mm, qk_mm, v_mm, o_mm, var_mm, vt_mm, fin_mm):
                    pe.sem_inc(s, 1)
                pe.wait_ge(m_set, 7)

                def s1(k, m):
                    if m == 1:
                        pe.wait_ge(v_act, 3 * k + 2)
                    elif m >= 2:
                        after(pe, s1_dve, 16 * k + m - 1)
                    after(pe, wins_lo, NWP * k + min(m // GPW + 1 + (m % GPW == GPW - 1), NWP))
                    if m == 0:
                        pe.wait_ge(v_act, 3 * k - 1 + 2)
                    for i in range(4):
                        x0 = (4 * m + i) * PS
                        for part in range(2):
                            last = nc.tensor.matmul(banks[:, s1_slot(m) + i // 2, i % 2 * 3 * NF:(i % 2 + 1) * 3 * NF],
                                                    wins[:, x0 * WIN:x0 * WIN + 128], hid_cur[part][:, :],
                                                    start=part == 0, stop=part == 1)
                    last.then_inc(s1_mm, 1)

                def split_product(to, ch, columns, o):
                    for n, (g, h) in enumerate(((0, 1), (0, 0), (1, 0))):
                        last = nc.tensor.matmul(to, G[g][:, ch, columns], hidden[h][:, o, :], start=n == 0, stop=n == 2)
                    return last

                def s2_qk(k, q):
                    if q == 0:
                        after(pe, s1_dve, 16 * k + 16)
                    elif q >= 2:
                        after(pe, qk_dve, 6 * k + q - 1)
                    for part in range(2):
                        for c in range(QKB):
                            ch = q * QKB + c
                            last = split_product(banks[:, q % 2 * 2 + part, c * PW:(c + 1) * PW], ch,
                                                 slice(part * NSPEC, (part + 1) * NSPEC), part * NF + ch)
                    last.then_inc(qk_mm, 1)

                def s2_v(k, r):
                    if r < 2:
                        after(pe, qk_dve, 6 * k + 5 + r)
                    else:
                        pe.wait_ge(v_act, 3 * k + 1 + 2)
                    for c in range(VB):
                        ch = r * VB + c
                        last = split_product(banks[0:PX, r % 2 * 2 + c // 8, c % 8 * PW:(c % 8 + 1) * PW], ch,
                                             slice(2 * NSPEC, NG), 2 * NF + ch)
                    last.then_inc(v_mm, 1)

                def chunk_out(bank, i):
                    return banks[0:2 * NF, bank, :].rearrange("p (y i x) -> p y i x", y=PS, i=8)[:, :, i, :]

                def inverse_dft(k, half):
                    c = half // 2
                    if half % 2 == 0:
                        after(pe, t_dve, 4 * k + max(c - 1, 0))
                        after(pe, g_pool, 4 * k + c + 1)
                    for i in range(half % 2 * 4, half % 2 * 4 + 4):
                        last = nc.tensor.matmul(chunk_out(BCEN[c % 2], i),
                                                prod[:, 8 * c + i, :, :].rearrange("p s c -> p (s c)"),
                                                K["inverse"][:, :].rearrange("p (y x) -> p y x", y=PS),
                                                start=True, stop=True)
                    if half % 2:
                        last.then_inc(o_mm, 1)

                def variance(k, c):
                    if c == 0:
                        after(pe, fin_dve, 4 * k)
                    after(pe, ln_act, 4 * k + c)
                    after(pe, sq_act, 4 * k + c + 1)
                    nc.tensor.matmul(banks[:, BVAR, :], K["chan_avg"][:, :], sq[:, c % 2, :],
                                     start=True, stop=True).then_inc(var_mm, 1)

                def transpose_v(k, c):
                    after(pe, y_dve, 4 * k + c)
                    pe.sem_inc(pe_passed, 1)
                    for i in range(8):
                        last = nc.tensor.transpose(chunk_out(BVT, i),
                                                   vpix[:, 8 * c + i, :, :].rearrange("p s c -> p (s c)"),
                                                   K["identity"][:, :].rearrange("p (y x) -> p y x", y=PS))
                    last.then_inc(vt_mm, 1)

                def final(k, f):
                    if f == 0:
                        after(pe, y_dve, 4 * k + 4)
                        after(pe, y2_in, 32 * (k + 1))
                        after(pe, ln_act, 4 * k + 4)
                    elif f >= 2:
                        after(pe, fin_dve, 4 * k + f - 1)
                    nc.tensor.matmul(banks[:, BFIN[f % 2], :], final_w[:, :, :].rearrange("p s c -> p (s c)"),
                                     mixed[:, f * RPG:(f + 1) * RPG, :].rearrange("p r x -> p (r x)"),
                                     start=True, stop=True).then_inc(fin_mm, 1)

                def row(*which):
                    run_row(PLAN, {"s": s1, "q": s2_qk, "v": s2_v},
                            {"o": inverse_dft, "r": variance, "t": transpose_v, "f": final}, *which)

                with pe.Fori(0, B) as b:
                    pe.wait_ge(cur_set, b + 1)
                    rows_of_batch(pe, b, row)

            def hidden_at(part, m):
                return hidden[part][0:NWIN, :, 4 * m:4 * m + 4].rearrange("p o (b t) -> p b t o", b=2)

            def hidden_from(m):
                return banks[0:NWIN, s1_slot(m):s1_slot(m) + 2, 0:6 * NF].rearrange("p b (t o) -> p b t o", t=2)

            def window_at(p, lo, hi):
                return wins[p:p + NF + 1, lo * WIN:hi * WIN].rearrange("p (x y) -> p x y", y=WIN)

            @block.scalar
            def _(act):
                nc.scalar.preload_act_table_set("natural_log_exp_and_others")
                for s in (wins_hi, s1_act, qk_act, sq_act, ln_act, r_act):
                    act.sem_inc(s, 1)
                act.sem_inc(v_act, 2)

                def window_hi(k, i):
                    if i == 0:
                        after(act, band_in, 16 * (k + 1))
                    lo, hi = window_part(i)
                    nc.scalar.activation(window_at(0, lo, hi), band[:, :, lo:hi].rearrange("p y x -> p x y"),
                                         ACT.Copy, scale=in_a_cur[:, :]).then_inc(wins_hi, 1)

                def hidden_hi(k, m):
                    after(act, s1_mm, 16 * k + m + 1)
                    nc.scalar.activation(hidden_at(0, m), hidden_from(m), ACT.Copy, scale=1 / HID_SCALE
                                         ).then_inc(s1_act, 1)

                def copy_k(k, q):
                    after(act, qk_mm, 6 * k + q + 1)
                    after(act, qk_dve, 6 * k + max(q - 1, 0))
                    nc.scalar.copy(kspec[:, q % 2, :], banks[:, q % 2 * 2 + 1, :]).then_inc(qk_act, 1)

                def copy_v(k, r):
                    after(act, v_mm, 3 * k + r + 1)
                    nc.scalar.activation(vpix[:, :, :, r * VB:(r + 1) * VB].rearrange("p i s c -> p c s i"),
                                         banks[0:PX, r % 2 * 2:r % 2 * 2 + 2, :]
                                         .rearrange("p b (c s i) -> p (b c) s i", s=2, i=NPAIR),
                                         ACT.Copy, scale=1 / SPEC_SCALE).then_inc(v_act, 1)

                def square(k, c):
                    after(act, o_mm, 4 * k + c + 1)
                    nc.scalar.activation(sq[0:2 * NF, c % 2, :], banks[0:2 * NF, BCEN[c % 2], :], ACT.Square
                                         ).then_inc(sq_act, 1)

                def log_variance(k, c):
                    after(act, var_mm, 4 * k + c + 1)
                    after(act, t_dve, 4 * k + max(c - 1, 0))
                    nc.scalar.activation(rstd[:, c % 2, :], banks[0:2 * NF, BVAR, :], ACT.Ln,
                                         bias=eps_ln[0:2 * NF, :]).then_inc(ln_act, 1)

                def inverse_deviation(k, c):
                    after(act, ln_act, 4 * k + c + 1)
                    nc.scalar.activation(rstd[:, c % 2, :], rstd[:, c % 2, :], ACT.Exp, scale=-0.5).then_inc(r_act, 1)

                def row(*which):
                    run_row(PLAN_ACT, {"s": hidden_hi, "q": copy_k, "v": copy_v},
                            {"c": square, "r": log_variance, "e": inverse_deviation, "w": window_hi}, *which)

                act.wait_ge(m_set, 7)
                with act.Fori(0, B) as b:
                    act.wait_ge(cur_set, b + 1)
                    for i in range(NWP):
                        window_hi(b * NPR, i)
                    rows_of_batch(act, b, row)

            @block.vector
            def _(dve):
                v = nc.vector
                for s in (wins_lo, s1_dve, qk_dve, g_sum, g_dve, t_dve, y_dve, fin_dve):
                    dve.sem_inc(s, 1)

                def window_lo(k, i):
                    after(dve, wins_hi, NWP * k + i + 1)
                    lo, hi = window_part(i)
                    v.scalar_tensor_tensor(window_at(LO, lo, hi), band[:, :, lo:hi].rearrange("p y x -> p x y"),
                                           in_a_cur[:, :], window_at(0, lo, hi), ALU.mult, ALU.subtract
                                           ).then_inc(wins_lo, 1)

                def norm(k, c):
                    after(dve, r_act, 4 * k + c + 1)
                    after(dve, y_dve, 4 * k + c)
                    v.scalar_tensor_tensor(normed[:, :], banks[0:2 * NF, BCEN[c % 2], :], ln_w[:, :], rstd[:, c % 2, :],
                                           ALU.mult, ALU.mult).then_inc(t_dve, 1)

                def mix(k, c):
                    after(dve, t_dve, 4 * k + c + 1)
                    after(dve, vt_mm, 4 * k + c + 1)
                    v.scalar_tensor_tensor(mixed[0:2 * NF, :, 64 * c:64 * (c + 1)],
                                           normed[:, :].rearrange("p (y x) -> p y x", y=PS), ln_b[:, :],
                                           banks[0:2 * NF, BVT, :].rearrange("p (y x) -> p y x", y=PS),
                                           ALU.add, ALU.mult).then_inc(y_dve, 1)

                def final(k, f):
                    if f == 0:
                        after(dve, xa_done, k + 1)
                        after(dve, stored, 32 * k)
                    after(dve, fin_mm, 4 * k + f + 1)
                    rows = slice(f * RPG, (f + 1) * RPG)
                    v.tensor_tensor(ot[:, rows, :], banks[:, BFIN[f % 2], :]
                                    .rearrange("p (r x) -> p r x", r=RPG), xa[:, rows, :], ALU.add).then_inc(fin_dve, 1)

                def hidden_lo(k, m):
                    after(dve, s1_act, 16 * k + m + 1)
                    v.scalar_tensor_tensor(hidden_at(1, m), hidden_from(m), 1 / HID_SCALE, hidden_at(0, m),
                                           ALU.mult, ALU.subtract).then_inc(s1_dve, 1)

                def spectral_product(k, q):
                    after(dve, qk_mm, 6 * k + q + 1)
                    after(dve, qk_act, 6 * k + q + 1)
                    v.tensor_tensor(prod[:, :, :, q * QKB:(q + 1) * QKB].rearrange("p i s c -> p c s i"),
                                    banks[:, q % 2 * 2, :].rearrange("p (c s i) -> p c s i", s=2, i=NPAIR),
                                    kspec[:, q % 2, :].rearrange("p (c s i) -> p c s i", s=2, i=NPAIR),
                                    ALU.mult).then_inc(qk_dve, 1)

                def mean(k, c):
                    after(dve, qk_dve, 6 * k + 6)
                    v.tensor_reduce(minus_mean[:, c, :], prod[:, 8 * c:8 * (c + 1), :, :]
                                    .rearrange("p i s c -> p (i s) c"), AX, ALU.add).then_inc(g_sum, 1)
                    after(dve, g_sum, 4 * k + c + 1)
                    v.tensor_scalar(minus_mean[:, c, :], minus_mean[:, c, :], -1.0 / NF, None, ALU.mult
                                    ).then_inc(g_dve, 1)

                def row(*which):
                    run_row(PLAN_DVE, {"s": hidden_lo, "q": spectral_product, "v": lambda k, r: None},
                            {"g": mean, "n": norm, "y": mix, "f": final, "w": window_lo}, *which)

                dve.wait_ge(m_set, 7)
                with dve.Fori(0, B) as b:
                    for part in range(2):
                        v.tensor_copy(hid_cur[part][:, :], hid_m[part][:, bass.ds(b, 1), :].rearrange("p b o -> p (b o)"))
                    v.tensor_copy(in_a_cur[:, :], in_a[:, bass.ds(b, 1)])
                    v.tensor_copy(a_cur[:, :], res_a[:, bass.ds(b, 1)])
                    v.tensor_copy(c_cur[:, :], res_c[:, bass.ds(b, 1)]).then_inc(cur_set, 1)
                    for i in range(NWP):
                        window_lo(b * NPR, i)
                    rows_of_batch(dve, b, row)


def kernel(**inputs):
    import numpy as _np
    import concourse.bacc as _bacc
    from concourse import mybir as _mybir
    from concourse.bass_utils import run_bass_kernel_spmd as _run

    def a(name):
        return _np.asarray(inputs[name])

    def twice(v):
        return _np.concatenate([v, v]).reshape(-1, 1)

    table, inverse = dft_tables()
    arrays = dict(shape_constants())
    arrays["inverse"] = inverse
    arrays["dft"] = table.reshape(NG // 32, 10, 32 * (NWIN + 1))
    B, _, H, W = a("x").shape
    arrays["zeros"] = _np.zeros((NF + 1, W), _np.float32)
    arrays["ones"] = _np.ones((1, W), _np.float32)
    arrays["x"] = a("x")
    arrays["gate_w"] = _np.broadcast_to(a("L0_conv_w").reshape(1, 3), (128, 3))
    for n, side in ((1, 3), (2, 5)):
        pre = f"L1_conv_dl{n}_"
        arrays[f"mlp{n}_w1T"] = a(pre + "w1").T
        arrays[f"mlp{n}_b1"] = a(pre + "b1").reshape(NL, 1)
        arrays[f"mlp{n}_w2T"] = a(pre + "w2").reshape(NL, side * side, NL).transpose(2, 1, 0)
        arrays[f"mlp{n}_b2"] = a(pre + "b2").reshape(NL, side * side)
    arrays["hid_wb"] = _np.concatenate([a("L1_conv_fs_hid_w").T, a("L1_conv_fs_hid_b")[None]])
    arrays["dw_wb"] = _np.concatenate([a("L1_conv_fs_dw_w").reshape(3 * NF, 9).T, a("L1_conv_fs_dw_b")[None]])
    arrays["ln_w"] = twice(a("L1_conv_fs_ln_w"))
    arrays["ln_b"] = twice(a("L1_conv_fs_ln_b"))
    arrays["out_w"] = a("L1_conv_fs_out_w")
    arrays["out_b"] = a("L1_conv_fs_out_b").reshape(NF, 1)
    arrays["last_wT"] = a("L1_conv_last_w").T
    arrays["last_b"] = twice(a("L1_conv_last_b"))
    arrays = {n: _np.ascontiguousarray(v) for n, v in arrays.items()}

    nc = _bacc.Bacc("TRN2", target_bir_lowering=False, num_devices=1)
    f32 = _mybir.dt.float32
    t = {n: nc.dram_tensor(f"in_{n}_dram", v.shape, f32, kind="ExternalInput").ap() for n, v in arrays.items()}
    t["out"] = nc.dram_tensor("out_0_dram", (B, C, H, W), f32, kind="ExternalOutput").ap()
    t["local_scratch"] = nc.dram_tensor("local_scratch", (B, NL, H, W), f32, kind="Internal").ap()
    program(nc, t)
    r = _run(nc, [{f"in_{n}_dram": v for n, v in arrays.items()}], core_ids=[0])
    return r.results[0]["out_0_dram"]
```
